# Optimizing a Trainium2 kernel written in Bass

```python
import numpy as np
import jax
import jax.numpy as jnp

def _softmax(x, axis=-1):
    return jax.nn.softmax(x, axis=axis)

def _gelu(x):
    return jax.nn.gelu(x, approximate=True)

def _silu(x):
    return jax.nn.silu(x)

def _sigmoid(x):
    return jax.nn.sigmoid(x)

def _layernorm(x, axis=-1, eps=1e-05):
    m = jnp.mean(x, axis=axis, keepdims=True)
    v = jnp.var(x, axis=axis, keepdims=True)
    return (x - m) / jnp.sqrt(v + eps)

def _scatter_add(tgt, idx, src, axis=0):
    return tgt.at[idx].add(src)

def _segment_sum(src, seg, n):
    return jax.ops.segment_sum(src, seg, n)
kernel_name = 'mk_flamingo_gated_d2_seqx_r4_de9880'

def setup_inputs(seed: int=0):
    np.random.seed(seed)
    _w = jnp.asarray

    def _rec_inputs():
        import jax
        import jax.numpy as jnp
        _rk = jax.random.key(seed)
        x = 7.22e-05 + 1 * jax.random.normal(jax.random.fold_in(_rk, 1), (16, 128, 1024), jnp.float32)
        _lenS = 128 - jax.random.randint(jax.random.fold_in(_rk, 7), (16,), 0, max(1, 128 // 4) + 1, jnp.int32)
        _lenS2 = 128 - jax.random.randint(jax.random.fold_in(_rk, 8), (16,), 0, max(1, 128 // 4) + 1, jnp.int32)
        _ctx_4096P = jax.random.normal(jax.random.fold_in(_rk, 11), (16, 16, 1024), jnp.float32)
        _ctx_4096c = jax.random.dirichlet(jax.random.fold_in(_rk, 511), 0.3 * jnp.ones((16,), jnp.float32), (16, 128))
        _ctx_4096t = jnp.einsum('bsk,bkd->bsd', _ctx_4096c, _ctx_4096P)
        _ctx_4096t = _ctx_4096t * jax.lax.rsqrt(jnp.mean(jnp.square(_ctx_4096t)) + 1e-12) * 0.953939
        ctx_4096 = 4.13588e-05 + 0.999923 * (_ctx_4096t + 0.3 * jax.random.normal(jax.random.fold_in(_rk, 611), (16, 128, 1024), jnp.float32))
        _g = jax.random.normal(jax.random.fold_in(_rk, 9001), (2, 2), jnp.float32)
        _g = jnp.sign(_g) * jnp.maximum(jnp.abs(_g), 1.0) + (_g == 0) * 1.0
        g_xattn = _g[0]
        g_ffn = _g[1]
        return (x, ctx_4096, g_xattn, g_ffn)
    x, ctx_4096, g_xattn, g_ffn = _rec_inputs()

    def _L0_xattn_setup():
        import jax, jax.numpy as jnp
        import numpy as np
        import math
        D_MODEL = 256
        NHEAD = 16
        MAX_SUP = 4
        DK = D_MODEL // NHEAD
        DM = D_MODEL * MAX_SUP
        B, S = (2, 256)
        key = jax.random.key(seed)
        ks = jax.random.split(key, 12)
        std = 0.02
        inp = {'q': jax.random.normal(ks[0], (B, S, DM), jnp.float32), 'k': jax.random.normal(ks[1], (B, S, DM), jnp.float32), 'v': jax.random.normal(ks[2], (B, S, DM), jnp.float32), 'Wq': jax.random.normal(ks[3], (DM, DM), jnp.float32) * std, 'bq': jnp.zeros((DM,), jnp.float32), 'Wk': jax.random.normal(ks[4], (DM, DM), jnp.float32) * std, 'bk': jnp.zeros((DM,), jnp.float32), 'Wv': jax.random.normal(ks[5], (DM, DM), jnp.float32) * std, 'bv': jnp.zeros((DM,), jnp.float32), 'interference': jax.random.normal(ks[6], (NHEAD, MAX_SUP, MAX_SUP), jnp.float32), 'amp': jnp.ones((1,), jnp.float32), 'Wo': jax.random.normal(ks[7], (DM, DM), jnp.float32) * std, 'bo': jnp.zeros((DM,), jnp.float32)}
        return inp
    _L0_xattn_all = _L0_xattn_setup()
    _L0_xattn_in = {k: v for k, v in _L0_xattn_all.items() if k in ('Wq', 'bq', 'Wk', 'bk', 'Wv', 'bv', 'interference', 'amp', 'Wo', 'bo')}
    del _L0_xattn_all

    def _L0_ffn_setup():
        import jax, jax.numpy as jnp
        import numpy as np
        key = jax.random.key(seed)
        k = jax.random.split(key, 6)
        x = jax.random.normal(k[0], (4, 512, 1024), jnp.float32)
        W = jax.random.normal(k[1], (1024, 1024), jnp.float32) * 0.02
        bias = jax.random.normal(k[2], (1024,), jnp.float32) * 0.02
        A = jax.random.normal(k[3], (16, 16, 1024), jnp.float32) * 0.02
        Bf = jax.random.normal(k[4], (16, 1024, 16), jnp.float32) * 0.02
        coeffs = jax.random.uniform(k[5], (16,), jnp.float32)
        scales = jnp.full((16,), 0.5, jnp.float32)
        return {'x': x, 'W': W, 'bias': bias, 'A': A, 'Bf': Bf, 'coeffs': coeffs, 'scales': scales}
    _L0_ffn_all = _L0_ffn_setup()
    _L0_ffn_in = {k: v for k, v in _L0_ffn_all.items() if k in ('W', 'bias', 'A', 'Bf', 'coeffs', 'scales')}
    del _L0_ffn_all

    def _L1_xattn_setup():
        import jax, jax.numpy as jnp
        import numpy as np
        HEADS = 8
        WINDOW = 16

        def _pointwise(W, b, t):
            return jnp.einsum('oc,bct->bot', W, t) + b[None, :, None]
        key = jax.random.key(seed)
        ks = jax.random.split(key, 10)
        B, C, T = (4, 128, 1024)
        s = 0.02
        return {'x': jax.random.normal(ks[0], (B, C, T), jnp.float32), 'cond': jax.random.normal(ks[1], (B, C, T), jnp.float32), 'Wq': jax.random.normal(ks[2], (C, C), jnp.float32) * s, 'bq': jnp.zeros((C,), jnp.float32), 'Wk': jax.random.normal(ks[3], (C, C), jnp.float32) * s, 'bk': jnp.zeros((C,), jnp.float32), 'Wv': jax.random.normal(ks[4], (C, C), jnp.float32) * s, 'bv': jnp.zeros((C,), jnp.float32), 'Wo': jax.random.normal(ks[5], (C, C), jnp.float32) * s, 'bo': jnp.zeros((C,), jnp.float32)}
    _L1_xattn_all = _L1_xattn_setup()
    _L1_xattn_in = {k: v for k, v in _L1_xattn_all.items() if k in ('Wq', 'bq', 'Wk', 'bk', 'Wv', 'bv', 'Wo', 'bo')}
    del _L1_xattn_all

    def _L1_ffn_setup():
        import jax, jax.numpy as jnp
        import numpy as np
        IN_F = 1024
        OUT_F = 1024
        N_CLUSTERS = 64
        THRESHOLD = 0.01
        TEMPERATURE = 0.1
        BATCH, SEQ = (4, 512)
        key = jax.random.key(seed)
        k1, k2, k3, k4, k5 = jax.random.split(key, 5)
        s = 1.0 / np.sqrt(IN_F)
        return {'input': jax.random.normal(k1, (BATCH, SEQ, IN_F), dtype=jnp.float32), 'weight': jax.random.normal(k2, (OUT_F, IN_F), dtype=jnp.float32) * s, 'bias': jax.random.uniform(k3, (OUT_F,), dtype=jnp.float32, minval=-s, maxval=s), 'centroids': jax.random.normal(k4, (N_CLUSTERS, IN_F), dtype=jnp.float32) * s, 'assignments': jax.random.randint(k5, (OUT_F,), 0, N_CLUSTERS, dtype=jnp.int32)}
    _L1_ffn_all = _L1_ffn_setup()
    _L1_ffn_in = {k: v for k, v in _L1_ffn_all.items() if k in ('weight', 'bias', 'centroids', 'assignments')}
    del _L1_ffn_all
    return {'x': x, 'ctx_4096': ctx_4096, 'g_xattn': g_xattn, 'g_ffn': g_ffn, 'L0_xattn_Wq': _L0_xattn_in['Wq'], 'L0_xattn_bq': _L0_xattn_in['bq'], 'L0_xattn_Wk': _L0_xattn_in['Wk'], 'L0_xattn_bk': _L0_xattn_in['bk'], 'L0_xattn_Wv': _L0_xattn_in['Wv'], 'L0_xattn_bv': _L0_xattn_in['bv'], 'L0_xattn_interference': _L0_xattn_in['interference'], 'L0_xattn_amp': _L0_xattn_in['amp'], 'L0_xattn_Wo': _L0_xattn_in['Wo'], 'L0_xattn_bo': _L0_xattn_in['bo'], 'L0_ffn_W': _L0_ffn_in['W'], 'L0_ffn_bias': _L0_ffn_in['bias'], 'L0_ffn_A': _L0_ffn_in['A'], 'L0_ffn_Bf': _L0_ffn_in['Bf'], 'L0_ffn_coeffs': _L0_ffn_in['coeffs'], 'L0_ffn_scales': _L0_ffn_in['scales'], 'L1_xattn_Wq': _L1_xattn_in['Wq'], 'L1_xattn_bq': _L1_xattn_in['bq'], 'L1_xattn_Wk': _L1_xattn_in['Wk'], 'L1_xattn_bk': _L1_xattn_in['bk'], 'L1_xattn_Wv': _L1_xattn_in['Wv'], 'L1_xattn_bv': _L1_xattn_in['bv'], 'L1_xattn_Wo': _L1_xattn_in['Wo'], 'L1_xattn_bo': _L1_xattn_in['bo'], 'L1_ffn_weight': _L1_ffn_in['weight'], 'L1_ffn_bias': _L1_ffn_in['bias'], 'L1_ffn_centroids': _L1_ffn_in['centroids'], 'L1_ffn_assignments': _L1_ffn_in['assignments']}

def reference(x, ctx_4096, g_xattn, g_ffn, L0_xattn_Wq, L0_xattn_bq, L0_xattn_Wk, L0_xattn_bk, L0_xattn_Wv, L0_xattn_bv, L0_xattn_interference, L0_xattn_amp, L0_xattn_Wo, L0_xattn_bo, L0_ffn_W, L0_ffn_bias, L0_ffn_A, L0_ffn_Bf, L0_ffn_coeffs, L0_ffn_scales, L1_xattn_Wq, L1_xattn_bq, L1_xattn_Wk, L1_xattn_bk, L1_xattn_Wv, L1_xattn_bv, L1_xattn_Wo, L1_xattn_bo, L1_ffn_weight, L1_ffn_bias, L1_ffn_centroids, L1_ffn_assignments):
    import jax
    import jax.numpy as jnp

    def _L0_xattn_ref(q, k, v, Wq, bq, Wk, bk, Wv, bv, interference, amp, Wo, bo):
        import jax, jax.numpy as jnp
        import numpy as np
        import math
        D_MODEL = 256
        NHEAD = 16
        MAX_SUP = 4
        DK = D_MODEL // NHEAD
        DM = D_MODEL * MAX_SUP
        B, S = (2, 256)
        b, s, dm = q.shape
        H, M = (interference.shape[0], interference.shape[1])
        dk = dm // (H * M)

        def proj(x, W, bias):
            y = x @ W.T + bias
            y = y.reshape(b, s, H, dk, M)
            return jnp.transpose(y, (0, 2, 1, 3, 4))
        qh = proj(q, Wq, bq)
        kh = proj(k, Wk, bk)
        vh = proj(v, Wv, bv)

        def interfere(x):
            return x + 0.1 * amp[0] * jnp.einsum('bhsdi,hij->bhsdj', x, interference)
        qh, kh, vh = (interfere(qh), interfere(kh), interfere(vh))
        scores = jnp.einsum('bhqdm,bhkdm->bhqkm', qh, kh) / math.sqrt(dk)
        weights = jax.nn.softmax(scores, axis=3)
        out = jnp.einsum('bhqkm,bhkdm->bhqdm', weights, vh)
        out = jnp.transpose(out, (0, 2, 1, 3, 4)).reshape(b, s, dm)
        return out @ Wo.T + bo

    def _L0_ffn_ref(x, W, bias, A, Bf, coeffs, scales):
        import jax, jax.numpy as jnp
        import numpy as np
        out = jnp.einsum('bsd,od->bso', x, W) + bias
        xa = jnp.einsum('bsd,erd->ebsr', x, A)
        w = coeffs * scales
        upd = jnp.einsum('ebsr,eor,e->bso', xa, Bf, w)
        return out + upd

    def _L1_xattn_ref(x, cond, Wq, bq, Wk, bk, Wv, bv, Wo, bo):
        import jax, jax.numpy as jnp
        import numpy as np
        HEADS = 8
        WINDOW = 16

        def _pointwise(W, b, t):
            return jnp.einsum('oc,bct->bot', W, t) + b[None, :, None]
        B, C, T = x.shape
        H, W = (HEADS, WINDOW)
        hd = C // H
        scale = hd ** (-0.5)
        pad_left = W // 2
        pad_right = W - pad_left - 1
        q = _pointwise(Wq, bq, x)
        k = _pointwise(Wk, bk, cond)
        v = _pointwise(Wv, bv, cond)
        k = jnp.pad(k, ((0, 0), (0, 0), (pad_left, pad_right)))
        v = jnp.pad(v, ((0, 0), (0, 0), (pad_left, pad_right)))
        idx = jnp.arange(T)[:, None] + jnp.arange(W)[None, :]
        k_win = k[:, :, idx].reshape(B, H, hd, T, W)
        v_win = v[:, :, idx].reshape(B, H, hd, T, W)
        qh = q.reshape(B, H, hd, T)
        dots = jnp.einsum('bhdt,bhdtw->bhtw', qh, k_win) * scale
        attn = jax.nn.softmax(dots, axis=-1)
        out = jnp.einsum('bhtw,bhdtw->bhdt', attn, v_win)
        out = out.reshape(B, C, T)
        return _pointwise(Wo, bo, out)

    def _L1_ffn_ref(input, weight, bias, centroids, assignments):
        import jax, jax.numpy as jnp
        import numpy as np
        IN_F = 1024
        OUT_F = 1024
        N_CLUSTERS = 64
        THRESHOLD = 0.01
        TEMPERATURE = 0.1
        BATCH, SEQ = (4, 512)
        shape = input.shape
        x = input.reshape(-1, shape[-1])
        dots = jax.nn.softmax(x @ centroids.T / TEMPERATURE, axis=-1)
        hits = dots > THRESHOLD
        query_sel = jnp.any(hits, axis=1)
        cluster_sel = jnp.any(hits, axis=0)
        row_sel = cluster_sel[assignments]
        dense = x @ weight.T + bias
        out = jnp.where(query_sel[:, None] & row_sel[None, :], dense, jnp.zeros((), dense.dtype))
        return out.reshape(*shape[:-1], -1)
    x = x + jnp.tanh(g_xattn[0]) * _L0_xattn_ref(_layernorm(x, axis=-1), ctx_4096, ctx_4096, L0_xattn_Wq, L0_xattn_bq, L0_xattn_Wk, L0_xattn_bk, L0_xattn_Wv, L0_xattn_bv, L0_xattn_interference, L0_xattn_amp, L0_xattn_Wo, L0_xattn_bo)
    x = x + jnp.tanh(g_ffn[0]) * _L0_ffn_ref(_layernorm(x, axis=-1), L0_ffn_W, L0_ffn_bias, L0_ffn_A, L0_ffn_Bf, L0_ffn_coeffs, L0_ffn_scales)
    x = x + jnp.tanh(g_xattn[1]) * _L1_xattn_ref(_layernorm(x, axis=-1), ctx_4096, L1_xattn_Wq, L1_xattn_bq, L1_xattn_Wk, L1_xattn_bk, L1_xattn_Wv, L1_xattn_bv, L1_xattn_Wo, L1_xattn_bo)
    x = x + jnp.tanh(g_ffn[1]) * _L1_ffn_ref(_layernorm(x, axis=-1), L1_ffn_weight, L1_ffn_bias, L1_ffn_centroids, L1_ffn_assignments)
    return x

_drawn_inputs = setup_inputs


def setup_inputs(seed=0):
    import zlib

    import numpy as np

    out = dict(_drawn_inputs(seed))
    spreads = {'g_ffn': (-1.0, 0.2),
     'L0_xattn_bq': (0.0, 0.8),
     'L0_xattn_bk': (0.0, 0.8),
     'L0_xattn_bv': (0.0, 0.1),
     'L0_xattn_bo': (0.0, 0.1),
     'L0_ffn_scales': (0.5, 0.6),
     'L1_xattn_bq': (0.0, 0.8),
     'L1_xattn_bk': (0.0, 0.8),
     'L1_xattn_bv': (0.0, 0.693),
     'L1_xattn_bo': (0.0, 0.1)}
    factors = {'L0_ffn_bias': 5.532,
     'L0_ffn_coeffs': 4.405,
     'L1_xattn_Wq': 8.0,
     'L1_xattn_Wk': 8.0,
     'L1_xattn_Wv': 7.042,
     'L1_xattn_Wo': 4.257,
     'L1_ffn_bias': 6.805}
    for name, (base, spread) in spreads.items():
        noise = np.random.default_rng([zlib.crc32(name.encode()), seed]).standard_normal(out[name].shape)
        drawn = base * np.exp(spread * noise) if base else spread * noise
        out[name] = jnp.asarray(drawn.astype(out[name].dtype))
    for name, factor in factors.items():
        out[name] = (out[name] * factor).astype(out[name].dtype)
    return out
```

```python
from contextlib import ExitStack

import numpy as np

import concourse.bass as bass
from concourse import mybir

F32 = mybir.dt.float32
F32R = mybir.dt.float32r
BF16 = mybir.dt.bfloat16
I32 = mybir.dt.int32
ALU = mybir.AluOpType
ACT = mybir.ActivationFunctionType
X = mybir.AxisListType.X

P = 128
B = 16
D = 1024
NC = D // P
TOK = B * P
M = 4
HD = 16
HP = 32
UH = 8
NU = D // (UH * HD)
WIN, PADL = 16, 8
TSTEP = P - WIN + 1
NT1 = 9
NCL = 64
QS = 0.25
START = 16


def done(t):
    return t + START + 1


def free(t, depth=2):
    return t + START + 1 - depth


def t_range(i):
    if i == 0:
        return 0, PADL + TSTEP, 0
    t0 = PADL + TSTEP * i
    return t0, min(TSTEP, D - t0), min(t0 - PADL, D - P)


class Env:
    pass


class Stage(ExitStack):

    def __init__(self, nc):
        super().__init__()
        self.nc, self.sems = nc, []
        self.callback(self.clear)

    def clear(self):
        self.nc.clear_and_free_semaphores(self.sems)
        self.nc.all_engine_barrier()


def scope(nc, ctx):
    def sb(name, shape, dt=F32):
        return ctx.enter_context(nc.sbuf_tensor(name, shape, dt))

    def ps(name, shape, dt=F32):
        return ctx.enter_context(nc.psum_tensor(name, shape, dt))

    def sem(name):
        ctx.sems.append(nc.alloc_semaphore(name=name))
        return ctx.sems[-1]

    return sb, ps, sem


def begin(eng, *sems):
    for s in sems:
        eng.sem_inc(s, START)


def one_ahead(eng, turns, first, second):
    first(0, 0)
    with eng.Fori(0, turns // 2 - 1) as i:
        for s in range(2):
            first(2 * i + s + 1, 1 - s)
            second(2 * i + s, s)
    first(turns - 1, 1)
    second(turns - 2, 0)
    second(turns - 1, 1)



def setup(nc, e):
    with Stage(nc) as ctx:
        sb, ps, sem = scope(nc, ctx)
        rep_mask = sb("rep_mask", [P, P])
        perm = sb("perm", [P, P])
        coef = sb("coef", [P, NC, M])
        amp = sb("amp", [P, 1])
        coefs = sb("coefs", [P, NC, M])
        tmp = sb("tmp", [P, P])
        bq = sb("bq", [P, NC]); bk = sb("bk", [P, NC]); bv = sb("bv", [P, NC])
        bvr = sb("bvr", [P, NC, P])
        graw = sb("graw", [P, 4])
        pb = ps("pb", [P, 2, 512])
        pv = ps("pv", [P, 2, 512])
        ld = sem("su_ld"); vec = sem("su_vec"); pe_done = sem("su_pe"); gate = sem("su_gate")
        block = ctx.enter_context(nc.Block())
        rep = lambda a: a.partition_broadcast(P)

        @block.sync
        def _(sp):
            for dst, src in ((e.ident[:], e.i["ident"]), (rep_mask[:], e.i["rep_mask"]), (perm[:], e.i["perm"]),
                             (coef[:], e.i["coef"]), (amp[:], rep(e.i["amp"])),
                             (bq[:], e.i["bq0"]), (bk[:], e.i["bk0"]), (bv[:], e.i["bv0"]),
                             (graw[:, 0:2], rep(e.i["g_xattn"])), (graw[:, 2:4], rep(e.i["g_ffn"]))):
                sp.dma_start(dst, src).then_inc(ld, 16)

        @block.scalar
        def _(act):
            act.wait_ge(ld, 160)
            act.activation(e.gate[:], graw[:], ACT.Tanh).then_inc(gate, 1)

        @block.vector
        def _(dve):
            n = 0

            def chain(ins):
                nonlocal n
                n += 1
                ins.then_inc(vec, 1)
                dve.wait_ge(vec, n)

            dve.wait_ge(ld, 160)
            chain(dve.tensor_scalar(coefs[:], coef[:], amp[:, 0:1], 0.1, ALU.mult, ALU.mult))
            chain(dve.tensor_copy(bvr[:], bv[:].unsqueeze(2).to_broadcast([P, NC, P])))
            for c in range(NC):
                g4 = lambda a: a.rearrange("p (h j d) -> p h j d", h=2, j=M)
                co = coefs[:, c, :].unsqueeze(1).unsqueeze(3).to_broadcast([P, 2, M, HD])
                chain(dve.tensor_tensor(g4(tmp[:]), g4(rep_mask[:]), co, ALU.mult))
                chain(dve.tensor_tensor(e.fold[:, c, :], tmp[:], perm[:], ALU.add))
            dve.wait_ge(pe_done, 1)
            dve.tensor_scalar(e.bqf[:], pb[:, 0, 0:NC], QS, None, ALU.mult)
            dve.tensor_copy(e.bkf[:], pb[:, 0, NC:2 * NC])
            dve.tensor_copy(e.bvf[:].rearrange("p (a b) -> p a b", a=2), pv[:]).then_inc(vec, 1)
            dve.wait_ge(vec, n + 1)
            dve.wait_ge(gate, 1)

        @block.tensor
        def _(pe):
            pe.wait_ge(vec, 2 + 2 * NC)
            for c in range(NC):
                pe.matmul(pb[:, 0, c:c + 1], e.fold[:, c, :], bq[:, c:c + 1], start=True, stop=True,
                          skip_group_check=True)
                pe.matmul(pb[:, 0, NC + c:NC + c + 1], e.fold[:, c, :], bk[:, c:c + 1], start=True, stop=True,
                          skip_group_check=True)
                m = pe.matmul(pv[:, c // 4, c % 4 * P:(c % 4 + 1) * P], bvr[:, c, :], e.fold[:, c, :],
                              start=True, stop=True, skip_group_check=True)
            m.then_inc(pe_done, 1)



class FoldedWeight:

    def __init__(self, nc, ctx, e, name, src, scale=1.0, share=None):
        sb, ps, sem = scope(nc, ctx)
        self.e, self.src, self.scale = e, src, scale
        self.hi = sb(f"{name}_hi", [P, NC, D], F32R)
        self.lo = sb(f"{name}_lo", [P, NC, D], F32R)
        if share:
            self.raw, self.loaded, self.folded = share.raw, share.loaded, share.folded
            self.hi_done, self.lo_done, self.base = share.hi_done, share.lo_done, NC
            return
        self.base = 0
        self.raw = sb(f"{name}_raw", [P, 2, D])
        self.loaded = [sem(f"{name}_loaded{k}") for k in range(2)]
        self.folded = sem(f"{name}_folded")
        self.hi_done = sem(f"{name}_hi_done")
        self.lo_done = sem(f"{name}_lo_done")

    def load(self, sp):
        w = self.src.rearrange("(o p) c -> o p c", p=P)
        with sp.Fori(0, NC // 2) as i:
            for k in range(2):
                sp.wait_ge(self.folded, free(self.base + 2 * i + k))
                sp.dma_start(self.raw[:, k, :], w[2 * i + k]).then_inc(self.loaded[k], 16)

    def fold(self, pe, banks):
        if not self.base:
            begin(pe, self.folded)
        with pe.Fori(0, NC // 2) as i:
            for k in range(2):
                pe.wait_ge(self.loaded[k], 8 * self.base + 16 * i + 16)
                pe.wait_ge(self.lo_done, free(self.base + 2 * i + k))
                for c in range(NC):
                    m = pe.matmul(banks[:, 2 * k + c // 4, c % 4 * P:(c % 4 + 1) * P],
                                  self.raw[:, k, c * P:(c + 1) * P],
                                  self.e.fold[:, 2 * i + k, :], start=True, stop=True, skip_group_check=True)
                m.then_inc(self.folded, 1)

    def _views(self, i, k, h, banks):
        v = banks[:, 2 * k + h, :].rearrange("p (c o) -> p c o", c=4)
        at = (slice(None), slice(4 * h, 4 * h + 4), bass.ts(2 * i + k, P))
        return v, self.hi[at], self.lo[at]

    def split_hi(self, act, banks):
        if not self.base:
            begin(act, self.hi_done)
        with act.Fori(0, NC // 2) as i:
            for k in range(2):
                act.wait_ge(self.folded, done(self.base + 2 * i + k))
                for h in range(2):
                    v, hi, _ = self._views(i, k, h, banks)
                    a = act.activation(hi, v, ACT.Copy, scale=self.scale)
                a.then_inc(self.hi_done, 1)

    def split_lo(self, dve, banks):
        if not self.base:
            begin(dve, self.lo_done)
        with dve.Fori(0, NC // 2) as i:
            for k in range(2):
                dve.wait_ge(self.hi_done, done(self.base + 2 * i + k))
                for h in range(2):
                    v, hi, lo = self._views(i, k, h, banks)
                    a = dve.scalar_tensor_tensor(lo, v, self.scale, hi.bitcast(F32), ALU.mult, ALU.subtract)
                a.then_inc(self.lo_done, 1)

    def ready(self, pe):
        pe.wait_ge(self.lo_done, done(self.base + NC - 1))


class PlainWeight:

    def __init__(self, nc, ctx, name, src, lowrank=None, mask=None):
        sb, ps, sem = scope(nc, ctx)
        self.src, self.lowrank, self.mask = src, lowrank, mask
        self.hi = sb(f"{name}_hi", [P, NC, D], F32R)
        self.lo = sb(f"{name}_lo", [P, NC, D], F32R)
        self.raw = sb(f"{name}_raw", [P, 2, D])
        self.loaded = [sem(f"{name}_loaded{k}") for k in range(2)]
        self.hi_done = sem(f"{name}_hi_done")
        self.lo_done = sem(f"{name}_lo_done")
        if lowrank:
            self.a = sb(f"{name}_a", [P, 2, D])
            self.bt = sb(f"{name}_bt", [P, 2, D])
            self.ce = sb(f"{name}_ce", [P, 3, 2])
            self.lr_loaded = sem(f"{name}_lr_loaded")
            self.lr = sem(f"{name}_lr")
        if lowrank or mask is not None:
            self.summed = sem(f"{name}_summed")

    def load(self, sp):
        if self.lowrank:
            a, bt, co, sc = self.lowrank
            for dst, src in ((self.a[:], a.rearrange("(k p) n -> p k n", p=P)),
                             (self.bt[:], bt.rearrange("(k p) n -> p k n", p=P)),
                             (self.ce[:, 0, :], co), (self.ce[:, 1, :], sc)):
                sp.dma_start(dst, src).then_inc(self.lr_loaded, 16)
        w = self.src.rearrange("(o p) c -> o p c", p=P)
        with sp.Fori(0, NC // 2) as i:
            for k in range(2):
                sp.wait_ge(self.lo_done, free(2 * i + k))
                sp.dma_start(self.raw[:, k, :], w[2 * i + k]).then_inc(self.loaded[k], 16)

    def lowrank_product(self, pe, banks):
        begin(pe, self.lr)
        pe.wait_ge(self.summed, 3)
        for c in range(NC):
            if c:
                pe.wait_ge(self.summed, 3 + c)
            for h in range(2):
                for r in range(2):
                    m = pe.matmul(banks[:, h, :], self.a[:, r, c * P:(c + 1) * P],
                                  self.bt[:, r, h * 512:(h + 1) * 512], start=(r == 0), stop=(r == 1))
            m.then_inc(self.lr, 1)

    def split_hi(self, act, banks=None):
        begin(act, self.hi_done)
        with act.Fori(0, NC // 2) as i:
            for k in range(2):
                if self.lowrank:
                    act.wait_ge(self.summed, 3 + 2 * i + k + 1)
                elif self.mask is not None:
                    act.wait_ge(self.summed, 2 * i + k + 1)
                else:
                    act.wait_ge(self.loaded[k], 16 * i + 16)
                act.activation(self.hi[:, 2 * i + k, :], self.raw[:, k, :], ACT.Copy).then_inc(self.hi_done, 1)

    def split_lo(self, dve, banks=None):
        begin(dve, self.lo_done)
        if self.lowrank:
            dve.wait_ge(self.lr_loaded, 64)
            dve.tensor_tensor(self.ce[:, 2, :], self.ce[:, 0, :], self.ce[:, 1, :],
                              ALU.mult).then_inc(self.summed, 1)
            dve.wait_ge(self.summed, 1)
            for r in range(2):
                dve.tensor_scalar(self.bt[:, r, :], self.bt[:, r, :], self.ce[:, 2, r:r + 1], None,
                                  ALU.mult).then_inc(self.summed, 1)
        with dve.Fori(0, NC // 2) as i:
            for k in range(2):
                raw = self.raw[:, k, :]
                if self.lowrank:
                    dve.wait_ge(self.loaded[k], 16 * i + 16)
                    dve.wait_ge(self.lr, done(2 * i + k))
                    dve.tensor_tensor(raw.rearrange("p (a b) -> p a b", a=2), banks[:, 0:2, :],
                                      raw.rearrange("p (a b) -> p a b", a=2), ALU.add).then_inc(self.summed, 1)
                if self.mask is not None:
                    dve.wait_ge(self.loaded[k], 16 * i + 16)
                    dve.tensor_tensor(raw, raw, self.mask, ALU.mult).then_inc(self.summed, 1)
                dve.wait_ge(self.hi_done, done(2 * i + k))
                dve.tensor_tensor(self.lo[:, 2 * i + k, :], raw, self.hi[:, 2 * i + k, :].bitcast(F32),
                                  ALU.subtract).then_inc(self.lo_done, 1)

    def ready(self, pe):
        pe.wait_ge(self.lo_done, done(NC - 1))


def three_passes(pe, out, a, b, chunks):
    terms = [(0, 0), (0, 1), (1, 0)]
    n = len(chunks) * len(terms)
    for j, c in enumerate(chunks):
        for i, (x, y) in enumerate(terms):
            m = pe.matmul(out, a(x, c), b(y, c), start=(i + j == 0), stop=(len(terms) * j + i == n - 1))
    return m



class Norm:

    def __init__(self, nc, ctx, name):
        sb, ps, sem = scope(nc, ctx)
        self.stats = sb(f"{name}_stats", [P, 2, 2, 6])
        self.mv = sb(f"{name}_mv", [P, 2, 2])
        self.veps = sb(f"{name}_veps", [P, 2])
        self.rstd = sb(f"{name}_rstd", [P, 2])
        self.power = sb(f"{name}_power", [P, 1])
        self.mark = sb(f"{name}_mark", [P, 1])
        self.step = sem(f"{name}_step")
        self.root = sem(f"{name}_root")

    def pool(self, pool, turns, of=2):
        pool.memset(self.power[:], -0.5).then_inc(self.root, 1)
        pool.wait_ge(self.root, 1)
        with pool.Fori(0, turns) as i:
            for k in range(of):
                self.pool_tile(pool, of * i + k, k % 2)

    def pool_tile(self, pool, t, k):
        pool.wait_ge(self.step, 3 * t + 3)
        pool.tensor_tensor(self.rstd[:, k:k + 1], self.veps[:, k:k + 1], self.power[:],
                           ALU.pow).then_inc(self.root, 1)

    def run(self, dve, t, k, src, dst):
        for h in range(2):
            a = dve.bn_stats(self.stats[:, k, h, :], src[:, h * 512:(h + 1) * 512])
        a.then_inc(self.step, 1)
        dve.wait_ge(self.step, 3 * t + 1)
        dve.memset(self.mark[:], 0.0)
        dve.bn_aggr(self.mv[:, k, :], self.stats[:, k, :, :]).then_inc(self.step, 1)
        dve.wait_ge(self.step, 3 * t + 2)
        dve.tensor_scalar(self.veps[:, k:k + 1], self.mv[:, k, 1:2], 1e-5, None, ALU.add).then_inc(self.step, 1)
        dve.wait_ge(self.root, t + 2)
        return dve.tensor_scalar(dst, src, self.mv[:, k, 0:1], self.rstd[:, k:k + 1], ALU.subtract, ALU.mult)



def project_q(nc, e):
    G = B // 2
    with Stage(nc) as ctx:
        sb, ps, sem = scope(nc, ctx)
        w = FoldedWeight(nc, ctx, e, "wq", e.i["Wq0"], QS)
        ln = Norm(nc, ctx, "qln")
        xin = sb("q_xin", [P, 2, D]); xn = sb("q_xn", [P, 2, D])
        xt = [sb("q_xt_hi", [P, 2, NC, 2 * P], F32R), sb("q_xt_lo", [P, 2, NC, 2 * P], F32R)]
        out = [sb("q_out_hi", [P, 2, 2 * P], F32R), sb("q_out_lo", [P, 2, 2 * P], F32R)]
        tb = ps("q_tb", [P, 4, 512]); qb = ps("q_qb", [P, 4, 512])
        x_in = [sem(f"q_x_in{k}") for k in range(2)]
        normed = sem("q_normed"); turned = sem("q_turned"); xhi = sem("q_xhi"); xlo = sem("q_xlo")
        mm = sem("q_mm"); qhi = sem("q_qhi"); qlo = sem("q_qlo")
        q_out = [sem(f"q_q_out{s}") for s in range(2)]
        block = ctx.enter_context(nc.Block())

        @block.sync
        def _(sp):
            begin(sp, *q_out)
            w.load(sp)

            def load(g, s):
                for k in range(2):
                    sp.wait_ge(normed, free(2 * g + k))
                    sp.dma_start(xin[:, k, :], e.i["x"][2 * g + k]).then_inc(x_in[k], 16)

            def store(g, s):
                for o in range(NC):
                    sp.wait_ge(qlo, done(NC * g + o))
                    for part, dram in zip(out, e.q0):
                        sp.dma_start(dram[o * P:(o + 1) * P, bass.ts(g, 2 * P)],
                                     part[:, o % 2, :].bitcast(F32)).then_inc(q_out[o % 2], 16)

            one_ahead(sp, G, load, store)
            for k in range(2):
                sp.wait_ge(q_out[k], 32 * (NC // 2) * G + START)

        @block.gpsimd
        def _(pool):
            ln.pool(pool, G)

        @block.vector
        def _(dve):
            w.split_lo(dve, qb)
            begin(dve, normed, xlo, qlo)

            def inputs(g, s):
                for k in range(2):
                    dve.wait_ge(x_in[k], 16 * g + 16)
                    dve.wait_ge(turned, free(2 * g + k))
                    ln.run(dve, 2 * g + k, k, xin[:, k, :], xn[:, k, :]).then_inc(normed, 1)
                for k in range(2):
                    dve.wait_ge(xhi, done(2 * g + k))
                    for h in range(2):
                        at = (slice(None), s, slice(4 * h, 4 * h + 4), slice(k * P, (k + 1) * P))
                        a = dve.tensor_tensor(xt[1][at], tb[:, 2 * k + h, :].rearrange("p (c t) -> p c t", c=4),
                                              xt[0][at].bitcast(F32), ALU.subtract)
                    a.then_inc(xlo, 1)

            def outputs(g, s):
                for o in range(NC):
                    dve.wait_ge(qhi, done(NC * g + o))
                    dve.scalar_tensor_tensor(out[1][:, o % 2, :], qb[:, o % 4, 0:2 * P], e.bqf[:, o:o + 1],
                                             out[0][:, o % 2, :].bitcast(F32), ALU.add, ALU.subtract).then_inc(qlo, 1)

            one_ahead(dve, G, inputs, outputs)

        @block.scalar
        def _(act):
            w.split_hi(act, qb)
            begin(act, xhi, qhi)

            def inputs(g, s):
                for k in range(2):
                    act.wait_ge(turned, done(2 * g + k))
                    for h in range(2):
                        a = act.activation(xt[0][:, s, 4 * h:4 * h + 4, k * P:(k + 1) * P],
                                           tb[:, 2 * k + h, :].rearrange("p (c t) -> p c t", c=4), ACT.Copy)
                    a.then_inc(xhi, 1)

            def outputs(g, s):
                for o in range(NC):
                    act.wait_ge(mm, done(NC * g + o))
                    act.wait_ge(q_out[o % 2], 32 * ((NC // 2) * g + o // 2) + START)
                    act.activation(out[0][:, o % 2, :], qb[:, o % 4, 0:2 * P], ACT.Identity,
                                   bias=e.bqf[:, o:o + 1]).then_inc(qhi, 1)

            one_ahead(act, G, inputs, outputs)

        @block.tensor
        def _(pe):
            w.fold(pe, qb)
            begin(pe, turned, mm)
            w.ready(pe)

            def turn(g, s):
                for k in range(2):
                    pe.wait_ge(normed, done(2 * g + k))
                    pe.wait_ge(xlo, free(2 * g + k))
                    for c in range(NC):
                        m = pe.transpose(tb[:, 2 * k + c // 4, c % 4 * P:(c % 4 + 1) * P],
                                         xn[:, k, c * P:(c + 1) * P], e.ident[:])
                    m.then_inc(turned, 1)

            def product(g, s):
                pe.wait_ge(xlo, done(2 * g + 1))
                for o in range(NC):
                    pe.wait_ge(qlo, free(NC * g + o, 4))
                    three_passes(pe, qb[:, o % 4, 0:2 * P],
                                 lambda x, c: (w.hi, w.lo)[x][:, c, o * P:(o + 1) * P],
                                 lambda y, c: xt[y][:, s, c, :], range(NC)).then_inc(mm, 1)

            one_ahead(pe, G, turn, product)


def project_kv(nc, e):
    G = B // 2
    with Stage(nc) as ctx:
        sb, ps, sem = scope(nc, ctx)
        wk = FoldedWeight(nc, ctx, e, "wk", e.i["Wk0"])
        wv = FoldedWeight(nc, ctx, e, "wv", e.i["Wv0"], share=wk)
        cin = sb("kv_cin", [P, NC, 2 * P])
        ct = [sb("kv_ct_hi", [P, 2, NC, 2 * P], F32R), sb("kv_ct_lo", [P, 2, NC, 2 * P], F32R)]
        out = [sb("kv_k_hi", [P, 2, 2 * P], F32R), sb("kv_k_lo", [P, 2, 2 * P], F32R)]
        vout = sb("kv_v", [P, 2, D])
        kb = ps("kv_kb", [P, 4, 512]); vb = ps("kv_vb", [P, 4, 512])
        c_in = sem("kv_c_in"); chi = sem("kv_chi"); clo = sem("kv_clo"); mm = sem("kv_mm")
        khi = sem("kv_khi"); klo = sem("kv_klo"); vmm = sem("kv_vmm"); vdone = sem("kv_vdone")
        k_out = [sem(f"kv_k_out{s}") for s in range(2)]; v_out = [sem(f"kv_v_out{s}") for s in range(2)]
        block = ctx.enter_context(nc.Block())
        ctx_t = e.i["ctxT"].rearrange("(c p) t -> p c t", p=P)

        @block.sync
        def _(sp):
            begin(sp, *k_out, *v_out)
            wk.load(sp)
            wv.load(sp)

            def load(g, s):
                sp.wait_ge(clo, free(g, 1))
                sp.dma_start(cin[:], ctx_t[:, :, bass.ts(g, 2 * P)]).then_inc(c_in, 16)

            def store(g, s):
                for o in range(NC):
                    sp.wait_ge(klo, done(NC * g + o))
                    for part, dram in zip(out, e.k0):
                        sp.dma_start(dram[o * P:(o + 1) * P, bass.ts(g, 2 * P)],
                                     part[:, o % 2, :].bitcast(F32)).then_inc(k_out[o % 2], 16)
                for k in range(2):
                    sp.wait_ge(vdone, 2 * (2 * g + k) + 2 + START)
                    sp.dma_start(e.v0[2 * g + k], vout[:, k, :]).then_inc(v_out[k], 16)

            one_ahead(sp, G, load, store)
            for k in range(2):
                sp.wait_ge(k_out[k], 32 * (NC // 2) * G + START)
                sp.wait_ge(v_out[k], 16 * G + START)

        @block.vector
        def _(dve):
            wk.split_lo(dve, kb)
            wv.split_lo(dve, kb)
            begin(dve, clo, klo, vdone)

            def inputs(g, s):
                dve.wait_ge(chi, done(g))
                dve.tensor_tensor(ct[1][:, s], cin[:], ct[0][:, s].bitcast(F32), ALU.subtract).then_inc(clo, 1)

            def outputs(g, s):
                for o in range(NC):
                    dve.wait_ge(khi, done(NC * g + o))
                    dve.scalar_tensor_tensor(out[1][:, o % 2, :], kb[:, o % 4, 0:2 * P], e.bkf[:, o:o + 1],
                                             out[0][:, o % 2, :].bitcast(F32), ALU.add, ALU.subtract).then_inc(klo, 1)
                for k in range(2):
                    dve.wait_ge(v_out[k], 16 * g + START)
                    for h in range(2):
                        dve.wait_ge(vmm, done(4 * g + 2 * k + h))
                        dve.tensor_tensor(vout[:, k, h * 512:(h + 1) * 512], vb[:, 2 * k + h, :],
                                          e.bvf[:, h * 512:(h + 1) * 512], ALU.add).then_inc(vdone, 1)

            one_ahead(dve, G, inputs, outputs)

        @block.scalar
        def _(act):
            wk.split_hi(act, kb)
            wv.split_hi(act, kb)
            begin(act, chi, khi)

            def inputs(g, s):
                act.wait_ge(c_in, 16 * g + 16)
                act.wait_ge(vmm, 4 * g - 4 + START)
                act.activation(ct[0][:, s], cin[:], ACT.Copy).then_inc(chi, 1)

            def outputs(g, s):
                for o in range(NC):
                    act.wait_ge(mm, done(NC * g + o))
                    act.wait_ge(k_out[o % 2], 32 * ((NC // 2) * g + o // 2) + START)
                    act.activation(out[0][:, o % 2, :], kb[:, o % 4, 0:2 * P], ACT.Identity,
                                   bias=e.bkf[:, o:o + 1]).then_inc(khi, 1)

            one_ahead(act, G, inputs, outputs)

        @block.tensor
        def _(pe):
            wk.fold(pe, kb)
            wv.fold(pe, kb)
            begin(pe, mm, vmm)
            wv.ready(pe)

            def product(g, s):
                pe.wait_ge(clo, done(g))
                for o in range(NC):
                    pe.wait_ge(klo, free(NC * g + o, 4))
                    three_passes(pe, kb[:, o % 4, 0:2 * P],
                                 lambda x, c: (wk.hi, wk.lo)[x][:, c, o * P:(o + 1) * P],
                                 lambda y, c: ct[y][:, s, c, :], range(NC)).then_inc(mm, 1)
                for k in range(2):
                    for h in range(2):
                        pe.wait_ge(vdone, free(4 * g + 2 * k + h, 4))
                        three_passes(pe, vb[:, 2 * k + h, :],
                                     lambda x, c: ct[x][:, s, c, k * P:(k + 1) * P],
                                     lambda y, c: (wv.hi, wv.lo)[y][:, c, h * 512:(h + 1) * 512],
                                     range(NC)).then_inc(vmm, 1)

            with pe.Fori(0, G // 2) as i:
                for s in range(2):
                    product(2 * i + s, s)



def staggered(eng, units, per_loop, stages):
    top = max(lead for lead, _ in stages)
    assert top <= per_loop

    def step(i, s, last):
        for lead, f in stages:
            at = s + lead
            if at < 0 or (last and at >= per_loop):
                continue
            turn = i + 1 if at >= per_loop else i
            f(per_loop * turn + at % per_loop, at % per_loop, turn)

    for s in range(-top, 0):
        step(0, s, False)
    turns = units // per_loop
    with eng.Fori(0, turns - 1) as i:
        for s in range(per_loop):
            step(i, s, False)
    for s in range(per_loop):
        step(turns - 1, s, True)


class Units:

    def __init__(self, layer):
        self.layer = layer
        self.per_batch = NU if layer == 0 else NT1
        self.per_loop = 2 * self.per_batch

    def rows(self, s):
        return P if self.layer == 0 else t_range(s % NT1)[1]

    def first(self, s):
        return s % self.per_batch == 0

    def edge(self, s):
        return {0: 0, NT1 - 1: 1}.get(s % NT1) if self.layer == 1 else None


def attend(nc, e, layer):
    un = Units(layer)
    n = f"a{layer}_"
    with Stage(nc) as ctx:
        sb, ps, sem = scope(nc, ctx)
        if layer == 0:
            pairs, length = 16, P
        else:
            pairs, length = 4, D
        qs = sb(n + "qs", [P, 2, pairs, length], F32R)
        ks = sb(n + "ks", [P, 2, pairs, 2, length], F32R)
        heads = 64 if layer == 0 else UH * NT1
        vraw = sb(n + "vraw", [P, 2, heads, HD])
        vpad = sb(n + "vpad", [P, 2, heads, HP])
        nmax = sb(n + "nmax", [P, 2, UH])
        probs = sb(n + "probs", [P, 2, UH, P])
        pt = sb(n + "pt", [P, 2, UH * P])
        osb = sb(n + "osb", [P, 2, 2 * P])
        rinv = sb(n + "rinv", [P, 2, UH])
        att = sb(n + "att", [P, 2, D])
        mark = sb(n + "mark", [P, 1])
        if layer == 1:
            bandf = sb(n + "bandf", [P, 3, P])
            band = sb(n + "band", [P, 3, 2, P], BF16)
            identb = sb(n + "identb", [P, P], BF16)
            edges = sb(n + "edges", [P, 2, 2])
            raw = sb(n + "raw", [P, UH])
            low = sb(n + "low", [P, 2, UH])
            epad = sb(n + "epad", [P, 2, UH])
            den = sb(n + "den", [P, UH])
        s_bank = ps(n + "s_bank", [P, 4, 512]); t_bank = ps(n + "t_bank", [P, 2, 512])
        o_bank = ps(n + "o_bank", [P, 1, 512]); b_bank = ps(n + "b_bank", [P, 1, 512])
        zeroed = sem(n + "zeroed"); const = sem(n + "const")
        qk_in = [sem(n + f"qk_in{k}") for k in range(2)]
        v_in = [sem(n + f"v_in{k}") for k in range(2)]
        v_ready = sem(n + "v_ready")
        scored = sem(n + "scored"); maxed = sem(n + "maxed"); expd = sem(n + "expd")
        turned = sem(n + "turned"); ev_dve = sem(n + "ev_dve"); ev_act = sem(n + "ev_act")
        valued = sem(n + "valued"); ev_o = sem(n + "ev_o"); back = sem(n + "back")
        inv = sem(n + "inv"); padmax = sem(n + "padmax"); normed = sem(n + "normed")
        out_sem = [sem(n + f"out{k}") for k in range(2)]
        block = ctx.enter_context(nc.Block())
        upb = un.per_batch

        def scores(s):
            return s_bank[:, 2 * (s % 2):2 * (s % 2) + 2, :].rearrange("p b (h x) -> p (b h) x", h=4)

        @block.sync
        def _(sp):
            begin(sp, *out_sem)
            if layer == 1:
                sp.dma_start(bandf[:], e.i["band"]).then_inc(const, 16)
                sp.dma_start(edges[:], e.i["edges"]).then_inc(const, 16)
            sp.wait_ge(zeroed, 2)

            def halves(b, s):
                for h in range(2):
                    sp.wait_ge(scored, done(8 * b + 4 * h - 5))
                    for j in range(4):
                        q = e.q0[j // 2].rearrange("(h p r) t -> h r p t", h=2, r=32)
                        sp.dma_start(qs[32 * j:32 * j + 32, h, :, :].bitcast(F32),
                                     q[h, :, :, bass.ts(b, P)]).then_inc(qk_in[h], 16)
                        k = e.k0[j % 2].rearrange("(h p r) t -> h r p t", h=2, r=32)
                        for a in range(2):
                            r = 32 * j + 16 * a
                            sp.dma_start(ks[r:r + 16, h, :, a, :].bitcast(F32),
                                         k[h, 16 * a:16 * a + 16, :, bass.ts(b, P)]).then_inc(qk_in[h], 16)

            def batch(b, s):
                sp.wait_ge(scored, upb * (b - 1) + START)
                for j in range(4):
                    q = e.q1[j // 2].rearrange("b (p r) t -> b r p t", r=32)
                    sp.dma_start(qs[32 * j:32 * j + 32, s, :, :].bitcast(F32), q[b]).then_inc(qk_in[s], 16)
                    k = e.k1[j % 2].rearrange("b (p r) t -> b r p t", r=32)
                    for a in range(2):
                        r = 32 * j + 16 * a
                        sp.dma_start(ks[r:r + 16, s, :, a, :].bitcast(F32),
                                     k[b][16 * a:16 * a + 16]).then_inc(qk_in[s], 16)

            def load(b, s):
                (halves if layer == 0 else batch)(b, s)
                sp.wait_ge(v_ready, free(b))
                if layer == 0:
                    src = e.v0[b].rearrange("t (h d) -> t h d", d=HD)
                    sp.dma_start(vraw[:, s], src).then_inc(v_in[s], 16)
                else:
                    for i in range(NT1):
                        w0 = t_range(i)[2]
                        src = e.v1[b][w0:w0 + P, :].rearrange("t (h d) -> t h d", d=HD)
                        sp.dma_start(vraw[:, s, UH * i:UH * i + UH, :], src).then_inc(v_in[s], 16)

            def store(b, s):
                if layer == 0:
                    sp.wait_ge(normed, done(upb * b + upb - 1))
                    sp.dma_start(e.att0[b], att[:, s, :]).then_inc(out_sem[s], 16)
                else:
                    for i in range(NT1):
                        t0, m, _ = t_range(i)
                        sp.wait_ge(normed, done(upb * b + i))
                        o = (s * NT1 + i) % 2
                        sp.dma_start(e.att1[b][t0:t0 + m, :], att[0:m, o, 0:P]).then_inc(out_sem[o], 16)

            one_ahead(sp, B, load, store)
            for k in range(2):
                sp.wait_ge(out_sem[k], 16 * (B // 2) * (1 if layer == 0 else NT1) + START)

        @block.gpsimd
        def _(pool):
            pool.memset(ks[:].bitcast(F32), 0.0).then_inc(zeroed, 1)
            pool.memset(mark[:], 0.0)
            pool.memset(vpad[:], 0.0).then_inc(zeroed, 1)
            pool.wait_ge(zeroed, 2)
            pool.memset(vpad[:, :, :, HD:HD + 1], 1.0).then_inc(zeroed, 1)
            pool.wait_ge(zeroed, 3)
            begin(pool, v_ready)
            with pool.Fori(0, B // 2) as i:
                for s in range(2):
                    b = 2 * i + s
                    pool.wait_ge(v_in[s], 16 * (i + 1) * (1 if layer == 0 else NT1))
                    pool.wait_ge(valued, upb * (b - 1) + START)
                    pool.wait_ge(v_ready, free(b, 1))
                    pool.tensor_tensor(mark[:], mark[:], mark[:], ALU.mult)
                    pool.tensor_copy(vpad[:, s, :, 0:HD], vraw[:, s]).then_inc(v_ready, 1)

        @block.vector
        def _(dve):
            begin(dve, maxed, ev_dve, ev_o, normed)
            if layer == 1:
                dve.wait_ge(const, 32)
                dve.tensor_copy(band[:], bandf[:].unsqueeze(2).to_broadcast([P, 3, 2, P]))
                dve.tensor_copy(identb[:], e.ident[:]).then_inc(const, 1)

            def maximum(u, s, i):
                m, k = un.rows(s), s % 2
                dve.wait_ge(scored, done(u))
                dve.wait_ge(expd, free(u))
                if un.edge(s) is None:
                    dve.tensor_reduce(nmax[0:m, k, :], scores(s)[0:m], X, ALU.max, negate=True).then_inc(maxed, 1)
                    return
                nth = 4 * i + 2 * (s // NT1) + un.edge(s)
                dve.tensor_reduce(raw[0:m, :], scores(s)[0:m], X, ALU.max, negate=True).then_inc(padmax, 1)
                dve.wait_ge(padmax, nth + 1)
                dve.tensor_scalar(low[0:m, un.edge(s), :], raw[0:m, :], 0.0, None, ALU.min)
                dve.tensor_scalar(nmax[0:m, k, :], raw[0:m, :], edges[0:m, un.edge(s), 1:2], None,
                                  ALU.min).then_inc(maxed, 1)

            def turn_out(u, s, i):
                m, k = un.rows(s), s % 2
                dve.wait_ge(turned, done(u))
                dve.wait_ge(valued, free(u))
                dve.tensor_copy(pt[:, k, 0:512].rearrange("p (h t) -> p h t", h=4)[:, :, 0:m],
                                t_bank[:, 0, :].rearrange("p (h t) -> p h t", h=4)[:, :, 0:m]).then_inc(ev_dve, 1)

            def value_out(u, s, i):
                m, k = un.rows(s), s % 2
                dve.wait_ge(valued, done(u))
                dve.wait_ge(back, free(u))
                dve.tensor_copy(osb[:, k, :].rearrange("p (g t) -> p g t", g=2)[:, :, 0:m],
                                o_bank[:, 0, 0:2 * P].rearrange("p (g t) -> p g t", g=2)[:, :, 0:m]).then_inc(ev_o, 1)

            def divide(u, s, i):
                m, k = un.rows(s), s % 2
                dve.wait_ge(back, done(u))
                o = b_bank[0:m, 0, 0:2 * P].rearrange("p (h d) -> p h d", d=HP)
                if un.edge(s) is None:
                    steps = u + 1 if layer == 0 else u + 4 * i + 2 * (s // NT1) + 2
                    dve.reciprocal(rinv[0:m, k, :], o[:, :, HD]).then_inc(inv, 1)
                else:
                    ed = un.edge(s)
                    steps = u + 4 * i + 2 * (s // NT1) + 2 + ed
                    dve.scalar_tensor_tensor(den[0:m, :], epad[0:m, ed, :], edges[0:m, ed, 0:1], o[:, :, HD],
                                             ALU.mult, ALU.add).then_inc(inv, 1)
                    dve.wait_ge(inv, steps - 1)
                    dve.reciprocal(rinv[0:m, k, :], den[0:m, :]).then_inc(inv, 1)
                dve.wait_ge(inv, steps)
                if layer == 0:
                    slot, unit = s // NU, s % NU
                    if unit == 0:
                        dve.wait_ge(out_sem[slot], 16 * i + START)
                    dst = att[:, slot, unit * P:(unit + 1) * P].rearrange("p (h d m) -> p h m d", h=2, m=M)
                    g = lambda a: a.rearrange("p (h m) d -> p h m d", h=2)
                    dve.tensor_tensor(dst, g(o[:, :, 0:HD]),
                                      g(rinv[:, k, :].unsqueeze(2).to_broadcast([P, UH, HD])),
                                      ALU.mult).then_inc(normed, 1)
                else:
                    dve.wait_ge(out_sem[k], 16 * (NT1 * i + s // 2) + START)
                    dve.tensor_tensor(att[0:m, k, 0:P].rearrange("p (h d) -> p h d", d=HD), o[:, :, 0:HD],
                                      rinv[0:m, k, :].unsqueeze(2).to_broadcast([m, UH, HD]),
                                      ALU.mult).then_inc(normed, 1)

            staggered(dve, B * upb, un.per_loop, [(4, maximum), (2, turn_out), (1, value_out), (0, divide)])

        @block.scalar
        def _(act):
            begin(act, expd, ev_act)

            def exponential(u, s, i):
                m, k = un.rows(s), s % 2
                act.wait_ge(maxed, done(u))
                act.wait_ge(turned, free(u))
                if un.edge(s) is not None:
                    act.activation(epad[0:m, un.edge(s), :], low[0:m, un.edge(s), :], ACT.Exp)
                for h in range(UH):
                    a = act.activation(probs[0:m, k, h, :], scores(s)[0:m, h, :], ACT.Exp,
                                       bias=nmax[0:m, k, h:h + 1])
                a.then_inc(expd, 1)

            def turn_out(u, s, i):
                m, k = un.rows(s), s % 2
                act.wait_ge(turned, done(u))
                act.wait_ge(valued, free(u))
                act.activation(pt[:, k, 512:1024].rearrange("p (h t) -> p h t", h=4)[:, :, 0:m],
                               t_bank[:, 1, :].rearrange("p (h t) -> p h t", h=4)[:, :, 0:m],
                               ACT.Copy).then_inc(ev_act, 1)

            staggered(act, B * upb, un.per_loop, [(3, exponential), (2, turn_out)])

        @block.tensor
        def _(pe):
            begin(pe, scored, turned, valued, back)
            if layer == 1:
                pe.wait_ge(const, 33)

            def score(u, s, i):
                m, k = un.rows(s), s % 2
                if layer == 0:
                    slot = s // 4 % 2
                    if s % 4 == 0:
                        pe.wait_ge(qk_in[slot], 192 * (2 * i + s // 8 + 1))
                else:
                    slot = s // NT1
                    if un.first(s):
                        pe.wait_ge(qk_in[slot], 192 * (i + 1))
                pe.wait_ge(expd, free(u))
                for j in range(4):
                    out = s_bank[0:m, 2 * k + j // 2, (j % 2) * 256:(j % 2) * 256 + 256]
                    out = out.rearrange("p (a x) -> p a x", a=2)
                    if layer == 0:
                        a = pe.matmul(out, qs[:, slot, 4 * (s % 4) + j, :], ks[:, slot, 4 * (s % 4) + j, :, :],
                                      start=True, stop=True, skip_group_check=True)
                    else:
                        t0, _, w0 = t_range(s % NT1)
                        kind = {None: 1, 0: 0, 1: 2}[un.edge(s)]
                        pe.matmul(out, qs[:, slot, j, t0:t0 + m], ks[:, slot, j, :, w0:w0 + P],
                                  start=True, stop=False, skip_group_check=True)
                        a = pe.matmul(out, identb[:, 0:m], band[:, kind, :, :],
                                      start=False, stop=True, skip_group_check=True)
                a.then_inc(scored, 1)

            def turn(u, s, i):
                m, k = un.rows(s), s % 2
                pe.wait_ge(expd, done(u))
                pe.wait_ge(ev_dve, free(u, 1))
                pe.wait_ge(ev_act, free(u, 1))
                for h in range(UH):
                    a = pe.transpose(t_bank[:, h // 4, h % 4 * P:h % 4 * P + m], probs[0:m, k, h, :],
                                     e.ident[0:m, 0:m])
                a.then_inc(turned, 1)

            def value(u, s, i):
                m, k = un.rows(s), s % 2
                slot = s // upb
                if un.first(s):
                    pe.wait_ge(v_ready, done(2 * i + slot))
                pe.wait_ge(ev_dve, done(u))
                pe.wait_ge(ev_act, done(u))
                pe.wait_ge(ev_o, free(u, 1))
                for g in range(2):
                    for j in range(4):
                        h = 4 * g + j
                        a = pe.matmul(o_bank[32 * j:32 * j + 32, 0, g * P:g * P + m],
                                      vpad[:, slot, UH * (s % upb) + h, :], pt[:, k, h * P:h * P + m],
                                      start=True, stop=True, skip_group_check=True)
                a.then_inc(valued, 1)

            def turn_back(u, s, i):
                m, k = un.rows(s), s % 2
                pe.wait_ge(ev_o, done(u))
                pe.wait_ge(normed, free(u, 1))
                for g in range(2):
                    a = pe.transpose(b_bank[0:m, 0, g * P:(g + 1) * P], osb[:, k, g * P:g * P + m], e.ident[:])
                a.then_inc(back, 1)

            staggered(pe, B * upb, un.per_loop, [(4, score), (2, turn), (1, value), (0, turn_back)])


def attend0(nc, e):
    attend(nc, e, 0)



def gemm(nc, e, name, weight, src, resid, gate, bias, dst, mask=None):
    n = name + "_"
    ln_on = src is None
    with Stage(nc) as ctx:
        sb, ps, sem = scope(nc, ctx)
        w = weight(ctx)
        if ln_on:
            ln = Norm(nc, ctx, n + "ln")
        xin = sb(n + "xin", [P, 2, D])
        rows = sb(n + "rows", [P, 2, D])
        xt = [sb(n + "xt_hi", [P, 2, NC, P], F32R), sb(n + "xt_lo", [P, 2, NC, P], F32R)]
        biasb = sb(n + "biasb", [P, D])
        out = sb(n + "out", [P, 2, D])
        tb = ps(n + "tb", [P, 4, 512]); gb = ps(n + "gb", [P, 4, 512])
        bias_in = sem(n + "bias_in"); masked = sem(n + "masked")
        x_in = [sem(n + f"x_in{k}") for k in range(2)]
        ready = sem(n + "ready") if ln_on else None
        turned = sem(n + "turned"); xhi = sem(n + "xhi"); xlo = sem(n + "xlo"); mm = sem(n + "mm")
        based = sem(n + "based"); summed = sem(n + "res_added")
        out_sem = [sem(n + f"out{k}") for k in range(2)]
        block = ctx.enter_context(nc.Block())
        loads = 1 if ln_on else 2
        halves = lambda a: a.rearrange("p (a b) -> p a b", a=2)

        @block.sync
        def _(sp):
            begin(sp, *out_sem)
            sp.dma_start(biasb[:], bias.partition_broadcast(P)).then_inc(bias_in, 16)
            w.load(sp)

            def load(t, s):
                sp.wait_ge(summed, free(t))
                sp.dma_start(xin[:, s, :], resid[t]).then_inc(x_in[s], 16)
                if not ln_on:
                    sp.dma_start(rows[:, s, :], src[t]).then_inc(x_in[s], 16)

            def store(t, s):
                sp.wait_ge(summed, done(t))
                sp.dma_start(dst[t], out[:, s, :]).then_inc(out_sem[s], 16)

            one_ahead(sp, B, load, store)
            for k in range(2):
                sp.wait_ge(out_sem[k], 16 * (B // 2) + START)

        if ln_on:
            @block.gpsimd
            def _(pool):
                ln.pool(pool, B // 2)

        @block.vector
        def _(dve):
            dve.wait_ge(bias_in, 16)
            if mask is not None:
                dve.tensor_tensor(biasb[:], biasb[:], mask, ALU.mult).then_inc(masked, 1)
            w.split_lo(dve, gb)
            begin(dve, xlo, summed)
            if ln_on:
                begin(dve, ready)
            if mask is not None:
                dve.wait_ge(masked, 1)

            def inputs(t, s):
                dve.wait_ge(x_in[s], 16 * loads * (t - s) // 2 + 16 * loads)
                if ln_on:
                    dve.wait_ge(turned, free(t))
                    ln.run(dve, t, s, xin[:, s, :], rows[:, s, :]).then_inc(ready, 1)
                    dve.wait_ge(ready, done(t))
                dve.scalar_tensor_tensor(xin[:, s, :], biasb[:], gate(t), xin[:, s, :],
                                         ALU.mult, ALU.add).then_inc(based, 1)
                dve.wait_ge(xhi, done(t))
                a = dve.tensor_tensor(xt[1][:, s].rearrange("p (a c) t -> p a (c t)", a=2),
                                      tb[:, 2 * s:2 * s + 2, :],
                                      xt[0][:, s].rearrange("p (a c) t -> p a (c t)", a=2).bitcast(F32),
                                      ALU.subtract)
                a.then_inc(xlo, 1)

            def outputs(t, s):
                dve.wait_ge(mm, done(t))
                dve.wait_ge(based, t + 1)
                dve.wait_ge(out_sem[s], 8 * (t - s) + START)
                dve.scalar_tensor_tensor(halves(out[:, s, :]), gb[:, 2 * s:2 * s + 2, :], gate(t),
                                         halves(xin[:, s, :]), ALU.mult, ALU.add).then_inc(summed, 1)

            one_ahead(dve, B, inputs, outputs)

        @block.scalar
        def _(act):
            w.split_hi(act, gb)
            begin(act, xhi)

            def turned_hi(t, s):
                act.wait_ge(turned, done(t))
                act.wait_ge(mm, free(t))
                act.activation(xt[0][:, s].rearrange("p (a c) t -> p a (c t)", a=2),
                               tb[:, 2 * s:2 * s + 2, :], ACT.Copy).then_inc(xhi, 1)

            with act.Fori(0, B // 2) as i:
                for s in range(2):
                    turned_hi(2 * i + s, s)

        @block.tensor
        def _(pe):
            if w.lowrank:
                w.lowrank_product(pe, gb)
            begin(pe, turned, mm)

            def turn(t, s):
                if ln_on:
                    pe.wait_ge(ready, done(t))
                else:
                    pe.wait_ge(x_in[s], 16 * loads * (t - s) // 2 + 16 * loads)
                pe.wait_ge(xlo, free(t))
                for c in range(NC):
                    m = pe.transpose(tb[:, 2 * s + c // 4, c % 4 * P:(c % 4 + 1) * P],
                                     rows[:, s, c * P:(c + 1) * P], e.ident[:])
                m.then_inc(turned, 1)

            def product(t, s):
                pe.wait_ge(xlo, done(t))
                pe.wait_ge(summed, free(t))
                for h in range(2):
                    m = three_passes(pe, gb[:, 2 * s + h, :], lambda x, c: xt[x][:, s, c, :],
                                     lambda y, c: (w.hi, w.lo)[y][:, c, h * 512:(h + 1) * 512], range(NC))
                m.then_inc(mm, 1)

            w.ready(pe)
            one_ahead(pe, B, turn, product)


def project_o0(nc, e):
    gemm(nc, e, "wo", lambda ctx: PlainWeight(nc, ctx, "wo", e.i["WoT0"]), e.att0, e.i["x"],
         lambda t: e.gate[:, 0:1], e.i["bo0"], e.x1)


def ffn0(nc, e):
    low = (e.i["A0"], e.i["BfT0"], e.i["coeffs"], e.i["scales"])
    gemm(nc, e, "f0", lambda ctx: PlainWeight(nc, ctx, "f0", e.i["WfT0"], low), None, e.x1,
         lambda t: e.gate[:, 2:3], e.i["bf0"], e.x2)


def ffn1(nc, e):
    gemm(nc, e, "f1", lambda ctx: PlainWeight(nc, ctx, "f1", e.i["WfT1"], mask=e.row_mask[:]), None, e.x3,
         lambda t: e.token_gate[:, bass.ds(t, 1)], e.i["bf1"], e.out, mask=e.row_mask[:])



def project1(nc, e):
    with Stage(nc) as ctx:
        sb, ps, sem = scope(nc, ctx)
        ln = Norm(nc, ctx, "p1ln")
        wt = sb("p1_wt", [P, 4, P]); b = sb("p1_b", [P, 4]); bvb = sb("p1_bvb", [P, P])
        xin = sb("p1_xin", [P, 2, D]); xn = sb("p1_xn", [P, 2, D]); cin = sb("p1_cin", [P, 2, D])
        qk = [[sb(f"p1_{x}_{p}", [P, 2, D], F32R) for p in ("hi", "lo")] for x in "qk"]
        vout = sb("p1_v", [P, 2, NC, P])
        banks = [ps("p1_qb", [P, 2, 512]), ps("p1_kb", [P, 2, 512])]
        vb = ps("p1_vb", [P, 2, 512])
        w_in = sem("p1_w_in"); scaled = sem("p1_scaled")
        x_in = [sem(f"p1_x_in{k}") for k in range(2)]; c_in = [sem(f"p1_c_in{k}") for k in range(2)]
        normed = sem("p1_normed")
        mm = [sem("p1_qmm"), sem("p1_kmm")]; hi = [sem("p1_qhi"), sem("p1_khi")]
        lo = [sem("p1_qlo"), sem("p1_klo")]
        vmm = sem("p1_vmm"); vdone = sem("p1_vdone")
        out_sem = [sem(f"p1_out{k}") for k in range(2)]
        block = ctx.enter_context(nc.Block())
        halves = lambda a: a.rearrange("p (a b) -> p a b", a=2)

        @block.sync
        def _(sp):
            begin(sp, *out_sem)
            for dst, src in ((wt[:], e.i["WT1"]), (b[:], e.i["b1"]), (bvb[:], e.i["bv1"].partition_broadcast(P))):
                sp.dma_start(dst, src).then_inc(w_in, 16)

            def load(t, s):
                sp.wait_ge(mm[0], free(t))
                sp.dma_start(xin[:, s, :], e.x2[t]).then_inc(x_in[s], 16)
                sp.wait_ge(vmm, free(t))
                sp.dma_start(cin[:, s, :], e.i["ctx"][t]).then_inc(c_in[s], 16)

            def store(t, s):
                for j, dram in enumerate((e.q1, e.k1)):
                    sp.wait_ge(lo[j], done(t))
                    for p in range(2):
                        sp.dma_start(dram[p][t], qk[j][p][:, s, :].bitcast(F32)).then_inc(out_sem[s], 16)
                sp.wait_ge(vdone, done(t))
                sp.dma_start(e.v1[t].rearrange("(c p) o -> p c o", p=P), vout[:, s]).then_inc(out_sem[s], 16)

            one_ahead(sp, B, load, store)
            for k in range(2):
                sp.wait_ge(out_sem[k], 80 * (B // 2) + START)

        @block.gpsimd
        def _(pool):
            ln.pool(pool, B // 2)

        @block.vector
        def _(dve):
            begin(dve, normed, lo[0], lo[1], vdone)
            dve.wait_ge(w_in, 48)
            dve.tensor_scalar(wt[:, 0, :], wt[:, 0, :], QS, None, ALU.mult)
            dve.tensor_scalar(b[:, 0:1], b[:, 0:1], QS, None, ALU.mult).then_inc(scaled, 1)
            dve.wait_ge(scaled, 1)

            def inputs(t, s):
                dve.wait_ge(x_in[s], 8 * (t - s) + 16)
                dve.wait_ge(mm[0], free(t))
                ln.run(dve, t, s, xin[:, s, :], xn[:, s, :]).then_inc(normed, 1)

            def outputs(t, s):
                for j in (1, 0):
                    dve.wait_ge(hi[j], done(t))
                    dve.scalar_tensor_tensor(halves(qk[j][1][:, s, :]), banks[j][:], b[:, j:j + 1],
                                             halves(qk[j][0][:, s, :]).bitcast(F32),
                                             ALU.add, ALU.subtract).then_inc(lo[j], 1)
                    if j == 1:
                        dve.wait_ge(vmm, done(t))
                        dve.wait_ge(out_sem[s], 40 * (t - s) + START)
                        dve.tensor_tensor(vout[:, s], vb[:].rearrange("p a (c o) -> p (a c) o", o=P),
                                          bvb[:].unsqueeze(1).to_broadcast([P, NC, P]), ALU.add).then_inc(vdone, 1)

            one_ahead(dve, B, inputs, outputs)

        @block.scalar
        def _(act):
            begin(act, hi[0], hi[1])
            act.wait_ge(scaled, 1)
            with act.Fori(0, B // 2) as i:
                for s in range(2):
                    t = 2 * i + s
                    act.wait_ge(out_sem[s], 80 * i + START)
                    for j in (1, 0):
                        act.wait_ge(mm[j], done(t))
                        act.activation(halves(qk[j][0][:, s, :]), banks[j][:], ACT.Identity,
                                       bias=b[:, j:j + 1]).then_inc(hi[j], 1)

        @block.tensor
        def _(pe):
            begin(pe, mm[0], mm[1], vmm)
            pe.wait_ge(scaled, 1)
            with pe.Fori(0, B // 2) as i:
                for s in range(2):
                    t = 2 * i + s
                    pe.wait_ge(c_in[s], 16 * i + 16)
                    pe.wait_ge(lo[1], free(t, 1))
                    for h in range(2):
                        m = pe.matmul(banks[1][:, h, :], wt[:, 1, :], cin[:, s, h * 512:(h + 1) * 512],
                                      start=True, stop=True)
                    m.then_inc(mm[1], 1)
                    pe.wait_ge(vdone, free(t, 1))
                    for c in range(NC):
                        m = pe.matmul(vb[:, c // 4, c % 4 * P:(c % 4 + 1) * P], cin[:, s, c * P:(c + 1) * P],
                                      wt[:, 2, :], start=True, stop=True, skip_group_check=True)
                    m.then_inc(vmm, 1)
                    pe.wait_ge(normed, done(t))
                    pe.wait_ge(lo[0], free(t, 1))
                    for h in range(2):
                        m = pe.matmul(banks[0][:, h, :], wt[:, 0, :], xn[:, s, h * 512:(h + 1) * 512],
                                      start=True, stop=True)
                    m.then_inc(mm[0], 1)


def attend1(nc, e):
    attend(nc, e, 1)



def select(nc, e):
    with Stage(nc) as ctx:
        sb, ps, sem = scope(nc, ctx)
        ln = Norm(nc, ctx, "seln")
        wt = sb("se_wt", [P, P]); b = sb("se_b", [P, 4]); gbo = sb("se_gbo", [P, 1])
        cent = sb("se_cent", [P, NC, NCL]); iota = sb("se_iota", [NCL, 1])
        assign = sb("se_assign", [NCL, D], I32); onehot = sb("se_onehot", [NCL, D])
        a_in = sb("se_a", [P, 2, NC, P]); x2 = sb("se_x2", [P, 2, D])
        att_t = sb("se_att_t", [P, 2, D]); delta = sb("se_delta", [P, 2, D])
        x3 = sb("se_x3", [P, 2, D]); xn = sb("se_xn", [P, 2, D]); xt = sb("se_xt", [P, 2, NC, P])
        low = sb("se_low", [P, 2, 2]); ex = sb("se_ex", [P, 2, NCL]); total = sb("se_total", [P, 1]); share = sb("se_share", [P, 1])
        hits = sb("se_hits", [P, NCL]); seen = sb("se_seen", [P, NCL]); any_ = sb("se_any", [P, 1])
        ones = sb("se_ones", [P, 1]); sel = sb("se_sel", [NCL, P])
        ab = ps("se_ab", [P, 2, 512]); ob = ps("se_ob", [P, 2, 512]); xb = ps("se_xb", [P, 2, 512])
        lb = ps("se_lb", [P, 1, 512]); cb = ps("se_cb", [P, 1, 512])
        w_in = sem("se_w_in"); prep = sem("se_prep")
        ld = [sem(f"se_ld{k}") for k in range(2)]
        a_turned = sem("se_a_turned"); a_out = sem("se_a_out"); o_mm = sem("se_o_mm"); o_out = sem("se_o_out")
        summed = sem("se_summed"); normed = sem("se_normed"); x_turned = sem("se_x_turned")
        x_out = sem("se_x_out"); logit = sem("se_logit"); lowed = sem("se_lowed"); expd = sem("se_expd")
        small = sem("se_small"); chosen = sem("se_chosen"); fin = sem("se_fin"); fin_pe = sem("se_fin_pe")
        out_sem = [sem(f"se_out{k}") for k in range(2)]
        block = ctx.enter_context(nc.Block())
        halves = lambda a: a.rearrange("p (a b) -> p a b", a=2)

        def batches(eng, stages):
            pairs = [(lead, lambda t, s, i, f=f: f(t, s % 2, 2 * i + s // 2)) for lead, f in stages]
            staggered(eng, B, 4, pairs)

        @block.sync
        def _(sp):
            begin(sp, *out_sem)
            for dst, src in ((wt[:], e.i["WT1"][:, 3, :]), (b[:], e.i["b1"]),
                             (cent[:], e.i["centT"].rearrange("(c p) n -> p c n", p=P)),
                             (iota[:], e.i["iota"]), (assign[:], e.i["assign"].partition_broadcast(NCL))):
                sp.dma_start(dst, src).then_inc(w_in, 16)

            def load(t, s):
                sp.wait_ge(a_turned, free(t))
                sp.dma_start(a_in[:, s], e.att1[t].rearrange("(c p) o -> p c o", p=P)).then_inc(ld[s], 16)
                sp.wait_ge(summed, free(t))
                sp.dma_start(x2[:, s, :], e.x2[t]).then_inc(ld[s], 16)

            def store(t, s):
                sp.wait_ge(summed, done(t))
                sp.dma_start(e.x3[t], x3[:, s, :]).then_inc(out_sem[s], 16)

            one_ahead(sp, B, load, store)
            for k in range(2):
                sp.wait_ge(out_sem[k], 16 * (B // 2) + START)

        @block.gpsimd
        def _(pool):
            ln.pool(pool, B // 2)

        @block.vector
        def _(dve):
            begin(dve, summed, normed, lowed, chosen)
            dve.memset(seen[:], 0.0)
            dve.memset(ones[:], 1.0)
            dve.wait_ge(w_in, 80)
            dve.tensor_copy(onehot[:], assign[:]).then_inc(prep, 1)
            dve.wait_ge(prep, 1)
            dve.tensor_scalar(onehot[:], onehot[:], iota[:, 0:1], None, ALU.is_equal)
            dve.tensor_tensor(gbo[:], b[:, 3:4], e.gate[:, 1:2], ALU.mult).then_inc(prep, 1)
            dve.wait_ge(prep, 2)

            def residual(t, s, i):
                dve.wait_ge(ld[s], 32 * i + 32)
                dve.wait_ge(o_out, done(t))
                dve.wait_ge(out_sem[s], 16 * i + START)
                dve.tensor_tensor(x3[:, s, :], delta[:, s, :], x2[:, s, :], ALU.add).then_inc(summed, 1)
                dve.wait_ge(summed, done(t))
                dve.wait_ge(x_turned, free(t))
                ln.run(dve, t, s, x3[:, s, :], xn[:, s, :]).then_inc(normed, 1)

            def lowest(t, s, i):
                dve.wait_ge(logit, done(t))
                dve.tensor_reduce(low[:, s, 0:1], lb[:, 0, 0:NCL], X, ALU.max, negate=True).then_inc(small, 1)
                dve.wait_ge(small, 5 * t + 1)
                dve.tensor_scalar(low[:, s, 1:2], low[:, s, 0:1], 10.0, None, ALU.mult).then_inc(lowed, 1)

            def choose(t, s, i):
                dve.wait_ge(expd, done(t))
                dve.tensor_reduce(total[:], ex[:, s, :], X, ALU.add).then_inc(small, 1)
                dve.wait_ge(small, 5 * t + 2)
                dve.reciprocal(share[:], total[:]).then_inc(small, 1)
                dve.wait_ge(small, 5 * t + 3)
                dve.tensor_scalar(hits[:], ex[:, s, :], share[:, 0:1], 0.01, ALU.mult, ALU.is_gt).then_inc(small, 1)
                dve.wait_ge(small, 5 * t + 4)
                dve.tensor_tensor(seen[:], seen[:], hits[:], ALU.max)
                dve.tensor_reduce(any_[:], hits[:], X, ALU.max).then_inc(small, 1)
                dve.wait_ge(small, 5 * t + 5)
                dve.tensor_scalar(e.token_gate[:, bass.ds(t, 1)], any_[:], e.gate[:, 3:4], None,
                                  ALU.mult).then_inc(chosen, 1)

            batches(dve, [(2, residual), (0, lowest), (0, choose)])
            dve.wait_ge(fin_pe, 1)
            dve.tensor_scalar(sel[:], cb[0:NCL, 0, 0:1].to_broadcast([NCL, P]), 1.0, None, ALU.min).then_inc(fin, 1)
            dve.wait_ge(fin_pe, 2)
            dve.tensor_copy(halves(e.row_mask[:]), ob[:]).then_inc(fin, 1)
            dve.wait_ge(fin, 2)

        @block.scalar
        def _(act):
            begin(act, a_out, o_out, x_out, expd)
            act.wait_ge(prep, 2)

            def attention_out(t, s, i):
                act.wait_ge(a_turned, done(t))
                act.wait_ge(o_mm, free(t))
                act.activation(halves(att_t[:, s, :]), ab[:], ACT.Copy).then_inc(a_out, 1)

            def projected(t, s, i):
                act.wait_ge(o_mm, done(t))
                act.wait_ge(summed, free(t))
                act.activation(halves(delta[:, s, :]), ob[:], ACT.Identity, bias=gbo[:],
                               scale=e.gate[:, 1:2]).then_inc(o_out, 1)

            def rows_out(t, s, i):
                act.wait_ge(x_turned, done(t))
                act.wait_ge(logit, free(t))
                act.activation(xt[:, s].rearrange("p (a c) t -> p a (c t)", a=2), xb[:], ACT.Copy).then_inc(x_out, 1)

            def exponential(t, s, i):
                act.wait_ge(lowed, done(t))
                act.activation(ex[:, s, :], lb[:, 0, 0:NCL], ACT.Exp, bias=low[:, s, 1:2],
                               scale=10.0).then_inc(expd, 1)

            batches(act, [(3, attention_out), (2, projected), (1, rows_out), (0, exponential)])

        @block.tensor
        def _(pe):
            begin(pe, a_turned, o_mm, x_turned, logit)
            pe.wait_ge(prep, 2)

            def turn_attention(t, s, i):
                pe.wait_ge(ld[s], 32 * i + 32)
                pe.wait_ge(a_out, free(t, 1))
                for c in range(NC):
                    m = pe.transpose(ab[:, c // 4, c % 4 * P:(c % 4 + 1) * P], a_in[:, s, c, :], e.ident[:])
                m.then_inc(a_turned, 1)

            def project(t, s, i):
                pe.wait_ge(a_out, done(t))
                pe.wait_ge(o_out, free(t, 1))
                for h in range(2):
                    m = pe.matmul(ob[:, h, :], wt[:], att_t[:, s, h * 512:(h + 1) * 512], start=True, stop=True)
                m.then_inc(o_mm, 1)

            def turn_rows(t, s, i):
                pe.wait_ge(normed, done(t))
                pe.wait_ge(x_out, free(t, 1))
                for c in range(NC):
                    m = pe.transpose(xb[:, c // 4, c % 4 * P:(c % 4 + 1) * P], xn[:, s, c * P:(c + 1) * P],
                                     e.ident[:])
                m.then_inc(x_turned, 1)

            def logits(t, s, i):
                pe.wait_ge(x_out, done(t))
                pe.wait_ge(expd, free(t, 1))
                for c in range(NC):
                    m = pe.matmul(lb[:, 0, 0:NCL], xt[:, s, c, :], cent[:, c, :], start=(c == 0), stop=(c == NC - 1))
                m.then_inc(logit, 1)

            batches(pe, [(3, turn_attention), (2, project), (1, turn_rows), (0, logits)])
            pe.wait_ge(chosen, done(B - 1))
            pe.matmul(cb[0:NCL, 0, 0:1], seen[:], ones[:], start=True, stop=True).then_inc(fin_pe, 1)
            pe.wait_ge(fin, 1)
            for h in range(2):
                m = pe.matmul(ob[:, h, :], sel[:], onehot[:, h * 512:(h + 1) * 512], start=True, stop=True)
            m.then_inc(fin_pe, 1)



def program(nc, ins, out, stages=99):
    e = Env()
    e.i = ins
    dram = lambda name, shape, dt=F32: nc.dram_tensor(name, shape, dt).ap()
    e.q0 = [dram(f"q0_{n}", [D, TOK]) for n in ("hi", "lo")]
    e.k0 = [dram(f"k0_{n}", [D, TOK]) for n in ("hi", "lo")]
    e.v0 = dram("v0", [B, P, D])
    e.att0 = dram("att0", [B, P, D])
    e.x1 = dram("x1", [B, P, D]); e.x2 = dram("x2", [B, P, D]); e.x3 = dram("x3", [B, P, D])
    e.q1 = [dram(f"q1_{n}", [B, P, D]) for n in ("hi", "lo")]
    e.k1 = [dram(f"k1_{n}", [B, P, D]) for n in ("hi", "lo")]
    e.v1 = dram("v1", [B, D, P]); e.att1 = dram("att1", [B, D, P])
    with ExitStack() as ctx:
        sb, ps, sem = scope(nc, ctx)
        e.ident = sb("ident_sb", [P, P]); e.fold = sb("fold", [P, NC, P])
        e.gate = sb("gate", [P, 4])
        e.token_gate = sb("token_gate", [P, B]); e.row_mask = sb("row_mask", [P, D])
        e.out = out
        e.bqf = sb("bqf", [P, NC]); e.bkf = sb("bkf", [P, NC]); e.bvf = sb("bvf", [P, D])
        for stage in STAGES[:stages]:
            stage(nc, e)


STAGES = [setup, project_q, project_kv, attend0, project_o0, ffn0, project1, attend1, select, ffn1]


def layout(x, ctx_4096, g_xattn, g_ffn, L0_xattn_Wq, L0_xattn_bq, L0_xattn_Wk, L0_xattn_bk, L0_xattn_Wv, L0_xattn_bv,
           L0_xattn_interference, L0_xattn_amp, L0_xattn_Wo, L0_xattn_bo, L0_ffn_W, L0_ffn_bias, L0_ffn_A, L0_ffn_Bf,
           L0_ffn_coeffs, L0_ffn_scales, L1_xattn_Wq, L1_xattn_bq, L1_xattn_Wk, L1_xattn_bk, L1_xattn_Wv,
           L1_xattn_bv, L1_xattn_Wo, L1_xattn_bo, L1_ffn_weight, L1_ffn_bias, L1_ffn_centroids,
           L1_ffn_assignments):
    part, free_ = np.arange(P)[:, None], np.arange(P)[None, :]
    h, d, i = part // 64, part // 4 % 16, part % 4
    h2, j, d2 = free_ // 64, free_ // 16 % 4, free_ % 16
    same = (h == h2) & (d == d2)
    band, edges = np.full((P, 3, P), 0.0, np.float32), np.zeros((P, 2, 2), np.float32)
    for n, tile in enumerate((0, 1, NT1 - 1)):
        t0, m, w0 = t_range(tile)
        off = w0 + free_ - (t0 + part)
        band[:, n, :] = np.where((off >= -PADL) & (off < WIN - PADL), 0.0, -1e30)
    for n, tile in enumerate((0, NT1 - 1)):
        t = t_range(tile)[0] + np.arange(P)
        edges[:, n, 0] = np.maximum(0, PADL - t) + np.maximum(0, t + WIN - PADL - D)
        edges[:, n, 1] = np.where(edges[:, n, 0] > 0, 0.0, 3e38)
    col = lambda b: np.ascontiguousarray(b.reshape(-1, P).T)
    coef = np.broadcast_to(L0_xattn_interference.reshape(NC, 2, 1, M, M), (NC, 2, HD, M, M))
    er = lambda w: np.ascontiguousarray(np.broadcast_to(w[:, None], (16, 16)).reshape(2, P).T)
    c = np.ascontiguousarray
    f = np.float32
    return {
        "ident": np.eye(P, dtype=f),
        "rep_mask": same.astype(f),
        "perm": (same & (i == j)).astype(f),
        "band": band, "edges": edges,
        "iota": np.arange(NCL, dtype=f)[:, None],
        "coef": c(coef.reshape(NC, P, M).transpose(1, 0, 2)),
        "amp": L0_xattn_amp, "g_xattn": g_xattn, "g_ffn": g_ffn,
        "x": x, "ctx": ctx_4096, "ctxT": c(ctx_4096.reshape(TOK, D).T),
        "Wq0": L0_xattn_Wq, "Wk0": L0_xattn_Wk, "Wv0": L0_xattn_Wv,
        "bq0": col(L0_xattn_bq), "bk0": col(L0_xattn_bk), "bv0": col(L0_xattn_bv),
        "WoT0": c(L0_xattn_Wo.T), "bo0": L0_xattn_bo,
        "WfT0": c(L0_ffn_W.T), "bf0": L0_ffn_bias,
        "A0": c(L0_ffn_A.reshape(256, D)), "BfT0": c(L0_ffn_Bf.transpose(0, 2, 1).reshape(256, D)),
        "coeffs": er(L0_ffn_coeffs), "scales": er(L0_ffn_scales),
        "WT1": c(np.stack([w.T for w in (L1_xattn_Wq, L1_xattn_Wk, L1_xattn_Wv, L1_xattn_Wo)], 1)),
        "b1": c(np.stack([L1_xattn_bq, L1_xattn_bk, L1_xattn_bv, L1_xattn_bo], 1)), "bv1": L1_xattn_bv,
        "WfT1": c(L1_ffn_weight.T), "bf1": L1_ffn_bias,
        "centT": c(L1_ffn_centroids.T), "assign": L1_ffn_assignments,
    }


def kernel(**inputs):
    import concourse.bacc as bacc
    from concourse.bass_utils import run_bass_kernel_spmd

    nc = bacc.Bacc("TRN2", target_bir_lowering=False, num_devices=1)
    arrays = {f"in_{name}": np.ascontiguousarray(a) for name, a in layout(**inputs).items()}
    ins = {name[3:]: nc.dram_tensor(name, a.shape, mybir.dt.from_np(a.dtype), kind="ExternalInput").ap()
           for name, a in arrays.items()}
    out = nc.dram_tensor("out", (B, P, D), F32, kind="ExternalOutput").ap()
    program(nc, ins, out)
    r = run_bass_kernel_spmd(nc, [arrays], core_ids=[0])
    return r.results[0]["out"]
```

```python
from contextlib import ExitStack

import numpy as np

import concourse.bass as bass
from concourse import mybir

F32 = mybir.dt.float32
F32R = mybir.dt.float32r
BF16 = mybir.dt.bfloat16
I32 = mybir.dt.int32
ALU = mybir.AluOpType
ACT = mybir.ActivationFunctionType
X = mybir.AxisListType.X

P = 128
B = 16
D = 1024
NC = D // P
TOK = B * P
M = 4
HD = 16
HP = 32
UH = 8
NU = D // (UH * HD)
WIN, PADL = 16, 8
TSTEP = P - WIN + 1
NT1 = 9
NCL = 64
QS = 0.25
RAW = 4
START = 16


def done(t):
    return t + START + 1


def free(t, depth=2):
    return t + START + 1 - depth


def t_range(i):
    if i == 0:
        return 0, PADL + TSTEP, 0
    t0 = PADL + TSTEP * i
    return t0, min(TSTEP, D - t0), min(t0 - PADL, D - P)


class Env:
    pass


class Stage(ExitStack):

    def __init__(self, nc):
        super().__init__()
        self.nc, self.sems = nc, []
        self.callback(self.clear)

    def clear(self):
        self.nc.clear_and_free_semaphores(self.sems)
        self.nc.all_engine_barrier()


def scope(nc, ctx):
    def sb(name, shape, dt=F32):
        return ctx.enter_context(nc.sbuf_tensor(name, shape, dt))

    def ps(name, shape, dt=F32):
        return ctx.enter_context(nc.psum_tensor(name, shape, dt))

    def sem(name):
        ctx.sems.append(nc.alloc_semaphore(name=name))
        return ctx.sems[-1]

    return sb, ps, sem


def begin(eng, *sems):
    for s in sems:
        eng.sem_inc(s, START)


def one_ahead(eng, turns, first, second):
    first(0, 0)
    with eng.Fori(0, turns // 2 - 1) as i:
        for s in range(2):
            first(2 * i + s + 1, 1 - s)
            second(2 * i + s, s)
    first(turns - 1, 1)
    second(turns - 2, 0)
    second(turns - 1, 1)



def setup(nc, e):
    with Stage(nc) as ctx:
        sb, ps, sem = scope(nc, ctx)
        rep_mask = sb("rep_mask", [P, P])
        perm = sb("perm", [P, P])
        coef = sb("coef", [P, NC, M])
        amp = sb("amp", [P, 1])
        coefs = sb("coefs", [P, NC, M])
        tmp = sb("tmp", [P, P])
        bq = sb("bq", [P, NC]); bk = sb("bk", [P, NC]); bv = sb("bv", [P, NC])
        bvr = sb("bvr", [P, NC, P])
        graw = sb("graw", [P, 4])
        pb = ps("pb", [P, 2, 512])
        pv = ps("pv", [P, 2, 512])
        ld = sem("su_ld"); vec = sem("su_vec"); pe_done = sem("su_pe"); gate = sem("su_gate")
        block = ctx.enter_context(nc.Block())
        rep = lambda a: a.partition_broadcast(P)

        @block.sync
        def _(sp):
            for dst, src in ((e.ident[:], e.i["ident"]), (rep_mask[:], e.i["rep_mask"]), (perm[:], e.i["perm"]),
                             (coef[:], e.i["coef"]), (amp[:], rep(e.i["amp"])),
                             (bq[:], e.i["bq0"]), (bk[:], e.i["bk0"]), (bv[:], e.i["bv0"]),
                             (graw[:, 0:2], rep(e.i["g_xattn"])), (graw[:, 2:4], rep(e.i["g_ffn"]))):
                sp.dma_start(dst, src).then_inc(ld, 16)

        @block.scalar
        def _(act):
            act.wait_ge(ld, 160)
            act.activation(e.gate[:], graw[:], ACT.Tanh).then_inc(gate, 1)

        @block.vector
        def _(dve):
            n = 0

            def chain(ins):
                nonlocal n
                n += 1
                ins.then_inc(vec, 1)
                dve.wait_ge(vec, n)

            dve.wait_ge(ld, 160)
            chain(dve.tensor_scalar(coefs[:], coef[:], amp[:, 0:1], 0.1, ALU.mult, ALU.mult))
            chain(dve.tensor_copy(bvr[:], bv[:].unsqueeze(2).to_broadcast([P, NC, P])))
            for c in range(NC):
                g4 = lambda a: a.rearrange("p (h j d) -> p h j d", h=2, j=M)
                co = coefs[:, c, :].unsqueeze(1).unsqueeze(3).to_broadcast([P, 2, M, HD])
                chain(dve.tensor_tensor(g4(tmp[:]), g4(rep_mask[:]), co, ALU.mult))
                chain(dve.tensor_tensor(e.fold[:, c, :], tmp[:], perm[:], ALU.add))
            dve.wait_ge(pe_done, 1)
            dve.tensor_scalar(e.bqf[:], pb[:, 0, 0:NC], QS, None, ALU.mult)
            dve.tensor_copy(e.bkf[:], pb[:, 0, NC:2 * NC])
            dve.tensor_copy(e.bvf[:].rearrange("p (a b) -> p a b", a=2), pv[:]).then_inc(vec, 1)
            dve.wait_ge(vec, n + 1)
            dve.wait_ge(gate, 1)

        @block.tensor
        def _(pe):
            pe.wait_ge(vec, 2 + 2 * NC)
            for c in range(NC):
                pe.matmul(pb[:, 0, c:c + 1], e.fold[:, c, :], bq[:, c:c + 1], start=True, stop=True,
                          skip_group_check=True)
                pe.matmul(pb[:, 0, NC + c:NC + c + 1], e.fold[:, c, :], bk[:, c:c + 1], start=True, stop=True,
                          skip_group_check=True)
                m = pe.matmul(pv[:, c // 4, c % 4 * P:(c % 4 + 1) * P], bvr[:, c, :], e.fold[:, c, :],
                              start=True, stop=True, skip_group_check=True)
            m.then_inc(pe_done, 1)



class FoldedWeight:

    def __init__(self, nc, ctx, e, name, src, scale=1.0, share=None, raw=None):
        sb, ps, sem = scope(nc, ctx)
        self.e, self.src, self.scale = e, src, scale
        self.hi = sb(f"{name}_hi", [P, NC, D], F32R)
        self.lo = sb(f"{name}_lo", [P, NC, D], F32R)
        if share:
            self.raw, self.loaded, self.folded = share.raw, share.loaded, share.folded
            self.hi_done, self.lo_done, self.base = share.hi_done, share.lo_done, NC
            return
        self.base = 0
        self.raw = sb(f"{name}_raw", [P, RAW, D]) if raw is None else raw
        self.loaded = [sem(f"{name}_loaded{k}") for k in range(RAW)]
        self.folded = sem(f"{name}_folded")
        self.hi_done = sem(f"{name}_hi_done")
        self.lo_done = sem(f"{name}_lo_done")

    def load(self, sp):
        w = self.src.rearrange("(o p) c -> o p c", p=P)
        with sp.Fori(0, NC // RAW) as i:
            for k in range(RAW):
                sp.wait_ge(self.folded, free(self.base + RAW * i + k, RAW))
                sp.dma_start(self.raw[:, k, :], w[RAW * i + k]).then_inc(self.loaded[k], 16)

    def fold(self, pe, banks):
        if not self.base:
            begin(pe, self.folded)
        with pe.Fori(0, NC // RAW) as i:
            for k in range(RAW):
                pe.wait_ge(self.loaded[k], 16 * (self.base // RAW + i + 1))
                pe.wait_ge(self.lo_done, free(self.base + RAW * i + k))
                for c in range(NC):
                    m = pe.matmul(banks[:, 2 * (k % 2) + c // 4, c % 4 * P:(c % 4 + 1) * P],
                                  self.raw[:, k, c * P:(c + 1) * P],
                                  self.e.fold[:, RAW * i + k, :], start=True, stop=True, skip_group_check=True)
                m.then_inc(self.folded, 1)

    def _views(self, i, k, h, banks):
        v = banks[:, 2 * (k % 2) + h, :].rearrange("p (c o) -> p c o", c=4)
        at = (slice(None), slice(4 * h, 4 * h + 4), bass.ts(RAW * i + k, P))
        return v, self.hi[at], self.lo[at]

    def split_hi(self, act, banks):
        if not self.base:
            begin(act, self.hi_done)
        with act.Fori(0, NC // RAW) as i:
            for k in range(RAW):
                act.wait_ge(self.folded, done(self.base + RAW * i + k))
                for h in range(2):
                    v, hi, _ = self._views(i, k, h, banks)
                    a = act.activation(hi, v, ACT.Copy, scale=self.scale)
                a.then_inc(self.hi_done, 1)

    def split_lo(self, dve, banks):
        if not self.base:
            begin(dve, self.lo_done)
        with dve.Fori(0, NC // RAW) as i:
            for k in range(RAW):
                dve.wait_ge(self.hi_done, done(self.base + RAW * i + k))
                for h in range(2):
                    v, hi, lo = self._views(i, k, h, banks)
                    a = dve.scalar_tensor_tensor(lo, v, self.scale, hi.bitcast(F32), ALU.mult, ALU.subtract)
                a.then_inc(self.lo_done, 1)

    def ready(self, pe):
        pe.wait_ge(self.lo_done, done(self.base + NC - 1))


class PlainWeight:

    def __init__(self, nc, ctx, name, src, lowrank=None, mask=None):
        sb, ps, sem = scope(nc, ctx)
        self.src, self.lowrank, self.mask = src, lowrank, mask
        self.hi = sb(f"{name}_hi", [P, NC, D], F32R)
        self.lo = sb(f"{name}_lo", [P, NC, D], F32R)
        self.raw = sb(f"{name}_raw", [P, RAW, D])
        self.loaded = [sem(f"{name}_loaded{k}") for k in range(RAW)]
        self.hi_done = sem(f"{name}_hi_done")
        self.lo_done = sem(f"{name}_lo_done")
        if lowrank:
            self.a = sb(f"{name}_a", [P, 2, D])
            self.bt = sb(f"{name}_bt", [P, 2, D])
            self.ce = sb(f"{name}_ce", [P, 3, 2])
            self.lr_loaded = sem(f"{name}_lr_loaded")
            self.lr = sem(f"{name}_lr")
        if lowrank or mask is not None:
            self.summed = sem(f"{name}_summed")

    def load(self, sp):
        if self.lowrank:
            a, bt, co, sc = self.lowrank
            for dst, src in ((self.a[:], a.rearrange("(k p) n -> p k n", p=P)),
                             (self.bt[:], bt.rearrange("(k p) n -> p k n", p=P)),
                             (self.ce[:, 0, :], co), (self.ce[:, 1, :], sc)):
                sp.dma_start(dst, src).then_inc(self.lr_loaded, 16)
        w = self.src.rearrange("(o p) c -> o p c", p=P)
        with sp.Fori(0, NC // RAW) as i:
            for k in range(RAW):
                sp.wait_ge(self.lo_done, free(RAW * i + k, RAW))
                sp.dma_start(self.raw[:, k, :], w[RAW * i + k]).then_inc(self.loaded[k], 16)

    def lowrank_product(self, pe, banks):
        begin(pe, self.lr)
        pe.wait_ge(self.summed, 3)
        for c in range(NC):
            if c:
                pe.wait_ge(self.summed, 3 + c)
            for h in range(2):
                for r in range(2):
                    m = pe.matmul(banks[:, h, :], self.a[:, r, c * P:(c + 1) * P],
                                  self.bt[:, r, h * 512:(h + 1) * 512], start=(r == 0), stop=(r == 1))
            m.then_inc(self.lr, 1)

    def split_hi(self, act, banks=None):
        begin(act, self.hi_done)
        with act.Fori(0, NC // RAW) as i:
            for k in range(RAW):
                if self.lowrank:
                    act.wait_ge(self.summed, 3 + RAW * i + k + 1)
                elif self.mask is not None:
                    act.wait_ge(self.summed, RAW * i + k + 1)
                else:
                    act.wait_ge(self.loaded[k], 16 * i + 16)
                act.activation(self.hi[:, RAW * i + k, :], self.raw[:, k, :], ACT.Copy).then_inc(self.hi_done, 1)

    def split_lo(self, dve, banks=None):
        begin(dve, self.lo_done)
        if self.lowrank:
            dve.wait_ge(self.lr_loaded, 64)
            dve.tensor_tensor(self.ce[:, 2, :], self.ce[:, 0, :], self.ce[:, 1, :],
                              ALU.mult).then_inc(self.summed, 1)
            dve.wait_ge(self.summed, 1)
            for r in range(2):
                dve.tensor_scalar(self.bt[:, r, :], self.bt[:, r, :], self.ce[:, 2, r:r + 1], None,
                                  ALU.mult).then_inc(self.summed, 1)
        with dve.Fori(0, NC // RAW) as i:
            for k in range(RAW):
                raw = self.raw[:, k, :]
                if self.lowrank:
                    dve.wait_ge(self.loaded[k], 16 * i + 16)
                    dve.wait_ge(self.lr, done(RAW * i + k))
                    dve.tensor_tensor(raw.rearrange("p (a b) -> p a b", a=2), banks[:, 0:2, :],
                                      raw.rearrange("p (a b) -> p a b", a=2), ALU.add).then_inc(self.summed, 1)
                if self.mask is not None:
                    dve.wait_ge(self.loaded[k], 16 * i + 16)
                    dve.tensor_tensor(raw, raw, self.mask, ALU.mult).then_inc(self.summed, 1)
                dve.wait_ge(self.hi_done, done(RAW * i + k))
                dve.tensor_tensor(self.lo[:, RAW * i + k, :], raw, self.hi[:, RAW * i + k, :].bitcast(F32),
                                  ALU.subtract).then_inc(self.lo_done, 1)

    def ready(self, pe):
        pe.wait_ge(self.lo_done, done(NC - 1))


def three_passes(pe, out, a, b, chunks):
    terms = [(0, 0), (0, 1), (1, 0)]
    n = len(chunks) * len(terms)
    for j, c in enumerate(chunks):
        for i, (x, y) in enumerate(terms):
            m = pe.matmul(out, a(x, c), b(y, c), start=(i + j == 0), stop=(len(terms) * j + i == n - 1))
    return m



class Norm:

    def __init__(self, nc, ctx, name):
        sb, ps, sem = scope(nc, ctx)
        self.stats = sb(f"{name}_stats", [P, 2, 2, 6])
        self.mv = sb(f"{name}_mv", [P, 2, 2])
        self.veps = sb(f"{name}_veps", [P, 2])
        self.rstd = sb(f"{name}_rstd", [P, 2])
        self.power = sb(f"{name}_power", [P, 1])
        self.mark = sb(f"{name}_mark", [P, 1])
        self.step = sem(f"{name}_step")
        self.root = sem(f"{name}_root")

    def pool(self, pool, turns, of=2):
        pool.memset(self.power[:], -0.5).then_inc(self.root, 1)
        pool.wait_ge(self.root, 1)
        with pool.Fori(0, turns) as i:
            for k in range(of):
                self.pool_tile(pool, of * i + k, k % 2)

    def pool_tile(self, pool, t, k):
        pool.wait_ge(self.step, 3 * t + 3)
        pool.tensor_tensor(self.rstd[:, k:k + 1], self.veps[:, k:k + 1], self.power[:],
                           ALU.pow).then_inc(self.root, 1)

    def run(self, dve, t, k, src, dst):
        for h in range(2):
            a = dve.bn_stats(self.stats[:, k, h, :], src[:, h * 512:(h + 1) * 512])
        a.then_inc(self.step, 1)
        dve.wait_ge(self.step, 3 * t + 1)
        dve.memset(self.mark[:], 0.0)
        dve.bn_aggr(self.mv[:, k, :], self.stats[:, k, :, :]).then_inc(self.step, 1)
        dve.wait_ge(self.step, 3 * t + 2)
        dve.tensor_scalar(self.veps[:, k:k + 1], self.mv[:, k, 1:2], 1e-5, None, ALU.add).then_inc(self.step, 1)
        dve.wait_ge(self.root, t + 2)
        return dve.tensor_scalar(dst, src, self.mv[:, k, 0:1], self.rstd[:, k:k + 1], ALU.subtract, ALU.mult)



def project_q(nc, e):
    G = B // 2
    with Stage(nc) as ctx:
        sb, ps, sem = scope(nc, ctx)
        w = FoldedWeight(nc, ctx, e, "wq", e.i["Wq0"], QS)
        ln = Norm(nc, ctx, "qln")
        xin = sb("q_xin", [P, 4, D]); xn = sb("q_xn", [P, 2, D])
        xt = [sb("q_xt_hi", [P, 2, NC, 2 * P], F32R), sb("q_xt_lo", [P, 2, NC, 2 * P], F32R)]
        out = [sb("q_out_hi", [P, 4, 2 * P], F32R), sb("q_out_lo", [P, 4, 2 * P], F32R)]
        tb = ps("q_tb", [P, 4, 512]); qb = ps("q_qb", [P, 4, 512])
        x_in = [sem(f"q_x_in{k}") for k in range(4)]
        normed = sem("q_normed"); turned = sem("q_turned"); xhi = sem("q_xhi"); xlo = sem("q_xlo")
        mm = sem("q_mm"); qhi = sem("q_qhi"); qlo = sem("q_qlo")
        q_out = [sem(f"q_q_out{s}") for s in range(4)]
        block = ctx.enter_context(nc.Block())

        @block.sync
        def _(sp):
            begin(sp, *q_out)
            w.load(sp)

            def load(g, s, i):
                for k in range(2):
                    sp.wait_ge(normed, free(2 * g + k, 4))
                    sp.dma_start(xin[:, 2 * s + k, :], e.i["x"][2 * g + k]).then_inc(x_in[2 * s + k], 16)

            def store(g, s, i):
                for o in range(NC):
                    sp.wait_ge(qlo, done(NC * g + o))
                    for part, dram in zip(out, e.q0):
                        sp.dma_start(dram[o * P:(o + 1) * P, bass.ts(g, 2 * P)],
                                     part[:, o % 4, :].bitcast(F32)).then_inc(q_out[o % 4], 16)

            staggered(sp, G, 2, [(2, load), (0, store)])
            for k in range(4):
                sp.wait_ge(q_out[k], 32 * (NC // 4) * G + START)

        @block.gpsimd
        def _(pool):
            ln.pool(pool, G)

        @block.vector
        def _(dve):
            w.split_lo(dve, qb)
            begin(dve, normed, xlo, qlo)

            def normalise(g, s, i):
                for k in range(2):
                    dve.wait_ge(x_in[2 * s + k], 16 * i + 16)
                    dve.wait_ge(turned, free(2 * g + k))
                    ln.run(dve, 2 * g + k, k, xin[:, 2 * s + k, :], xn[:, k, :]).then_inc(normed, 1)

            def turned_lo(g, s, i):
                for k in range(2):
                    dve.wait_ge(xhi, done(2 * g + k))
                    for h in range(2):
                        at = (slice(None), s, slice(4 * h, 4 * h + 4), slice(k * P, (k + 1) * P))
                        a = dve.tensor_tensor(xt[1][at], tb[:, 2 * k + h, :].rearrange("p (c t) -> p c t", c=4),
                                              xt[0][at].bitcast(F32), ALU.subtract)
                    a.then_inc(xlo, 1)

            def outputs(g, first):
                for o in range(first, first + NC // 2):
                    dve.wait_ge(qhi, done(NC * g + o))
                    dve.scalar_tensor_tensor(out[1][:, o % 4, :], qb[:, o % 4, 0:2 * P], e.bqf[:, o:o + 1],
                                             out[0][:, o % 4, :].bitcast(F32), ALU.add, ALU.subtract).then_inc(qlo, 1)

            staggered(dve, G, 2, [(1, normalise), (0, lambda g, s, i: outputs(g, 0)), (1, turned_lo),
                                  (0, lambda g, s, i: outputs(g, NC // 2))])

        @block.scalar
        def _(act):
            w.split_hi(act, qb)
            begin(act, xhi, qhi)

            def turned_hi(g, s, i):
                for k in range(2):
                    act.wait_ge(turned, done(2 * g + k))
                    for h in range(2):
                        a = act.activation(xt[0][:, s, 4 * h:4 * h + 4, k * P:(k + 1) * P],
                                           tb[:, 2 * k + h, :].rearrange("p (c t) -> p c t", c=4), ACT.Copy)
                    a.then_inc(xhi, 1)

            def outputs(g, first):
                for o in range(first, first + NC // 2):
                    act.wait_ge(mm, done(NC * g + o))
                    act.wait_ge(q_out[o % 4], 32 * ((NC // 4) * g + o // 4) + START)
                    act.activation(out[0][:, o % 4, :], qb[:, o % 4, 0:2 * P], ACT.Identity,
                                   bias=e.bqf[:, o:o + 1]).then_inc(qhi, 1)

            staggered(act, G, 2, [(0, lambda g, s, i: outputs(g, 0)), (1, turned_hi),
                                  (0, lambda g, s, i: outputs(g, NC // 2))])

        @block.tensor
        def _(pe):
            w.fold(pe, qb)
            begin(pe, turned, mm)
            w.ready(pe)

            def turn(g, s, i):
                for k in range(2):
                    pe.wait_ge(normed, done(2 * g + k))
                    pe.wait_ge(xlo, free(2 * g + k))
                    for c in range(NC):
                        m = pe.transpose(tb[:, 2 * k + c // 4, c % 4 * P:(c % 4 + 1) * P],
                                         xn[:, k, c * P:(c + 1) * P], e.ident[:])
                    m.then_inc(turned, 1)

            def product(g, s, first):
                pe.wait_ge(xlo, done(2 * g + 1))
                for o in range(first, first + NC // 2):
                    pe.wait_ge(qlo, free(NC * g + o, 4))
                    three_passes(pe, qb[:, o % 4, 0:2 * P],
                                 lambda x, c: (w.hi, w.lo)[x][:, c, o * P:(o + 1) * P],
                                 lambda y, c: xt[y][:, s, c, :], range(NC)).then_inc(mm, 1)

            staggered(pe, G, 2, [(0, lambda g, s, i: product(g, s, 0)), (1, turn),
                                 (0, lambda g, s, i: product(g, s, NC // 2))])


def project_kv(nc, e):
    G = B // 2
    with Stage(nc) as ctx:
        sb, ps, sem = scope(nc, ctx)
        raw = sb("kv_raw", [P, RAW, D])
        cin = raw[:, 0:2, :].rearrange("p k (c t) -> p (k c) t", t=2 * P)
        vout = raw[:, 2:4, :]
        ct = [sb("kv_ct_hi", [P, 2, NC, 2 * P], F32R), sb("kv_ct_lo", [P, 2, NC, 2 * P], F32R)]
        wk = FoldedWeight(nc, ctx, e, "wk", e.i["Wk0"], raw=raw)
        wv = FoldedWeight(nc, ctx, e, "wv", e.i["Wv0"], share=wk)
        out = [sb("kv_k_hi", [P, 2, 2 * P], F32R), sb("kv_k_lo", [P, 2, 2 * P], F32R)]
        kb = ps("kv_kb", [P, 4, 512]); vb = ps("kv_vb", [P, 4, 512])
        c_in = sem("kv_c_in"); chi = sem("kv_chi"); clo = sem("kv_clo"); mm = sem("kv_mm")
        khi = sem("kv_khi"); klo = sem("kv_klo"); vmm = sem("kv_vmm"); vdone = sem("kv_vdone")
        k_out = [sem(f"kv_k_out{s}") for s in range(2)]; v_out = [sem(f"kv_v_out{s}") for s in range(2)]
        block = ctx.enter_context(nc.Block())
        ctx_t = e.i["ctxT"].rearrange("(c p) t -> p c t", p=P)

        @block.sync
        def _(sp):
            begin(sp, *k_out, *v_out)
            wk.load(sp)
            wv.load(sp)
            sp.wait_ge(wk.folded, done(2 * NC - 1))

            def load(g, s):
                sp.wait_ge(clo, free(g, 1))
                sp.dma_start(cin, ctx_t[:, :, bass.ts(g, 2 * P)]).then_inc(c_in, 16)

            def store(g, s):
                for o in range(NC):
                    sp.wait_ge(klo, done(NC * g + o))
                    for part, dram in zip(out, e.k0):
                        sp.dma_start(dram[o * P:(o + 1) * P, bass.ts(g, 2 * P)],
                                     part[:, o % 2, :].bitcast(F32)).then_inc(k_out[o % 2], 16)
                for k in range(2):
                    sp.wait_ge(vdone, 2 * (2 * g + k) + 2 + START)
                    sp.dma_start(e.v0[2 * g + k], vout[:, k, :]).then_inc(v_out[k], 16)

            one_ahead(sp, G, load, store)
            for k in range(2):
                sp.wait_ge(k_out[k], 32 * (NC // 2) * G + START)
                sp.wait_ge(v_out[k], 16 * G + START)

        @block.vector
        def _(dve):
            wk.split_lo(dve, kb)
            wv.split_lo(dve, kb)
            begin(dve, clo, klo, vdone)

            def inputs(g, s):
                dve.wait_ge(chi, done(g))
                dve.tensor_tensor(ct[1][:, s], cin, ct[0][:, s].bitcast(F32), ALU.subtract).then_inc(clo, 1)

            def outputs(g, s):
                for o in range(NC):
                    dve.wait_ge(khi, done(NC * g + o))
                    dve.scalar_tensor_tensor(out[1][:, o % 2, :], kb[:, o % 4, 0:2 * P], e.bkf[:, o:o + 1],
                                             out[0][:, o % 2, :].bitcast(F32), ALU.add, ALU.subtract).then_inc(klo, 1)
                for k in range(2):
                    dve.wait_ge(v_out[k], 16 * g + START)
                    for h in range(2):
                        dve.wait_ge(vmm, done(4 * g + 2 * k + h))
                        dve.tensor_tensor(vout[:, k, h * 512:(h + 1) * 512], vb[:, 2 * k + h, :],
                                          e.bvf[:, h * 512:(h + 1) * 512], ALU.add).then_inc(vdone, 1)

            one_ahead(dve, G, inputs, outputs)

        @block.scalar
        def _(act):
            wk.split_hi(act, kb)
            wv.split_hi(act, kb)
            begin(act, chi, khi)

            def inputs(g, s):
                act.wait_ge(c_in, 16 * g + 16)
                act.wait_ge(vmm, 4 * g - 4 + START)
                act.activation(ct[0][:, s], cin, ACT.Copy).then_inc(chi, 1)

            def outputs(g, s):
                for o in range(NC):
                    act.wait_ge(mm, done(NC * g + o))
                    act.wait_ge(k_out[o % 2], 32 * ((NC // 2) * g + o // 2) + START)
                    act.activation(out[0][:, o % 2, :], kb[:, o % 4, 0:2 * P], ACT.Identity,
                                   bias=e.bkf[:, o:o + 1]).then_inc(khi, 1)

            one_ahead(act, G, inputs, outputs)

        @block.tensor
        def _(pe):
            wk.fold(pe, kb)
            wv.fold(pe, kb)
            begin(pe, mm, vmm)
            wv.ready(pe)

            def product(g, s):
                pe.wait_ge(clo, done(g))
                for o in range(NC):
                    pe.wait_ge(klo, free(NC * g + o, 4))
                    three_passes(pe, kb[:, o % 4, 0:2 * P],
                                 lambda x, c: (wk.hi, wk.lo)[x][:, c, o * P:(o + 1) * P],
                                 lambda y, c: ct[y][:, s, c, :], range(NC)).then_inc(mm, 1)
                for k in range(2):
                    for h in range(2):
                        pe.wait_ge(vdone, free(4 * g + 2 * k + h, 4))
                        three_passes(pe, vb[:, 2 * k + h, :],
                                     lambda x, c: ct[x][:, s, c, k * P:(k + 1) * P],
                                     lambda y, c: (wv.hi, wv.lo)[y][:, c, h * 512:(h + 1) * 512],
                                     range(NC)).then_inc(vmm, 1)

            with pe.Fori(0, G // 2) as i:
                for s in range(2):
                    product(2 * i + s, s)



def staggered(eng, units, per_loop, stages):
    top = max(lead for lead, _ in stages)
    assert top <= per_loop

    def step(i, s, last):
        for lead, f in stages:
            at = s + lead
            if at < 0 or (last and at >= per_loop):
                continue
            turn = i + 1 if at >= per_loop else i
            f(per_loop * turn + at % per_loop, at % per_loop, turn)

    for s in range(-top, 0):
        step(0, s, False)
    turns = units // per_loop
    with eng.Fori(0, turns - 1) as i:
        for s in range(per_loop):
            step(i, s, False)
    for s in range(per_loop):
        step(turns - 1, s, True)


class Units:

    def __init__(self, layer):
        self.layer = layer
        self.per_batch = NU if layer == 0 else NT1
        self.per_loop = 2 * self.per_batch

    def rows(self, s):
        return P if self.layer == 0 else t_range(s % NT1)[1]

    def first(self, s):
        return s % self.per_batch == 0

    def edge(self, s):
        return {0: 0, NT1 - 1: 1}.get(s % NT1) if self.layer == 1 else None


def attend(nc, e, layer):
    un = Units(layer)
    n = f"a{layer}_"
    with Stage(nc) as ctx:
        sb, ps, sem = scope(nc, ctx)
        if layer == 0:
            pairs, length = 16, P
        else:
            pairs, length = 4, D
        qs = sb(n + "qs", [P, 2, pairs, length], F32R)
        ks = sb(n + "ks", [P, 2, pairs, 2, length], F32R)
        heads = 64 if layer == 0 else UH * NT1
        vraw = sb(n + "vraw", [P, 2, heads, HD])
        vpad = sb(n + "vpad", [P, 2, heads, HP])
        nmax = sb(n + "nmax", [P, 2, UH])
        probs = sb(n + "probs", [P, 2, UH, P])
        pt = sb(n + "pt", [P, 2, UH * P])
        osb = sb(n + "osb", [P, 2, 2 * P])
        rinv = sb(n + "rinv", [P, 2, UH])
        att = sb(n + "att", [P, 2, un.per_batch * P])
        stores = 1 if layer == 0 else 3
        mark = sb(n + "mark", [P, 1])
        if layer == 1:
            bandf = sb(n + "bandf", [P, 3, P])
            band = sb(n + "band", [P, 3, 2, P], BF16)
            identb = sb(n + "identb", [P, P], BF16)
            edges = sb(n + "edges", [P, 2, 2])
            raw = sb(n + "raw", [P, UH])
            low = sb(n + "low", [P, 2, UH])
            epad = sb(n + "epad", [P, 2, UH])
            den = sb(n + "den", [P, UH])
        s_bank = ps(n + "s_bank", [P, 4, 512]); t_bank = ps(n + "t_bank", [P, 2, 512])
        o_bank = ps(n + "o_bank", [P, 1, 512]); b_bank = ps(n + "b_bank", [P, 1, 512])
        zeroed = sem(n + "zeroed"); v_zeroed = sem(n + "v_zeroed"); const = sem(n + "const")
        qk_in = [sem(n + f"qk_in{k}") for k in range(2)]
        v_in = [sem(n + f"v_in{k}") for k in range(2)]
        v_ready = sem(n + "v_ready")
        scored = sem(n + "scored"); maxed = sem(n + "maxed"); expd = sem(n + "expd")
        turned = sem(n + "turned"); ev_dve = sem(n + "ev_dve"); ev_act = sem(n + "ev_act")
        valued = sem(n + "valued"); ev_o = sem(n + "ev_o"); back = sem(n + "back")
        inv = sem(n + "inv"); padmax = sem(n + "padmax"); normed = sem(n + "normed")
        out_sem = [sem(n + f"out{k}") for k in range(2)]
        block = ctx.enter_context(nc.Block())
        upb = un.per_batch

        def scores(s):
            return s_bank[:, 2 * (s % 2):2 * (s % 2) + 2, :].rearrange("p b (h x) -> p (b h) x", h=4)

        @block.sync
        def _(sp):
            begin(sp, *out_sem)
            if layer == 1:
                sp.dma_start(bandf[:], e.i["band"]).then_inc(const, 16)
                sp.dma_start(edges[:], e.i["edges"]).then_inc(const, 16)
            sp.wait_ge(zeroed, 1)

            def load_half(u, s, i):
                if s % 4:
                    return
                h, b = s // 4 % 2, 2 * i + s // NU
                if h:
                    sp.wait_ge(zeroed, 2)
                sp.wait_ge(scored, done(u - 5))
                for j in range(4):
                    q = e.q0[j // 2].rearrange("(h p r) t -> h r p t", h=2, r=32)
                    sp.dma_start(qs[32 * j:32 * j + 32, h, :, :].bitcast(F32),
                                 q[h, :, :, bass.ts(b, P)]).then_inc(qk_in[h], 16)
                    k = e.k0[j % 2].rearrange("(h p r) t -> h r p t", h=2, r=32)
                    for a in range(2):
                        r = 32 * j + 16 * a
                        sp.dma_start(ks[r:r + 16, h, :, a, :].bitcast(F32),
                                     k[h, 16 * a:16 * a + 16, :, bass.ts(b, P)]).then_inc(qk_in[h], 16)

            def load_batch(u, s, i):
                if s % NT1:
                    return
                slot, b = s // NT1, 2 * i + s // NT1
                if slot:
                    sp.wait_ge(zeroed, 2)
                sp.wait_ge(scored, done(u - NT1 - 1))
                for j in range(4):
                    q = e.q1[j // 2].rearrange("b (p r) t -> b r p t", r=32)
                    sp.dma_start(qs[32 * j:32 * j + 32, slot, :, :].bitcast(F32), q[b]).then_inc(qk_in[slot], 16)
                    k = e.k1[j % 2].rearrange("b (p r) t -> b r p t", r=32)
                    for a in range(2):
                        r = 32 * j + 16 * a
                        sp.dma_start(ks[r:r + 16, slot, :, a, :].bitcast(F32),
                                     k[b][16 * a:16 * a + 16]).then_inc(qk_in[slot], 16)

            def load_values(u, s, i):
                if s % upb:
                    return
                slot, b = s // upb, 2 * i + s // upb
                sp.wait_ge(v_ready, free(b))
                if layer == 0:
                    src = e.v0[b].rearrange("t (h d) -> t h d", d=HD)
                    sp.dma_start(vraw[:, slot], src).then_inc(v_in[slot], 16)
                else:
                    for n in range(NT1):
                        w0 = t_range(n)[2]
                        src = e.v1[b][w0:w0 + P, :].rearrange("t (h d) -> t h d", d=HD)
                        sp.dma_start(vraw[:, slot, UH * n:UH * n + UH, :], src).then_inc(v_in[slot], 16)

            def store(u, s, i):
                slot, b = s // upb, 2 * i + s // upb
                if s % upb != upb - 1:
                    return
                sp.wait_ge(normed, done(u))
                if layer == 0:
                    sp.dma_start(e.att0[b], att[:, slot, :]).then_inc(out_sem[slot], 16)
                    return
                for t0, m, tile, tiles in ((*t_range(0)[:2], 0, 1), (*t_range(1)[:2], 1, NT1 - 2),
                                           (*t_range(NT1 - 1)[:2], NT1 - 1, 1)):
                    sp.dma_start(e.att1[b][t0:t0 + m * tiles, :].rearrange("(n r) o -> r n o", n=tiles),
                                 att[0:m, slot, tile * P:(tile + tiles) * P]
                                 .rearrange("p (n o) -> p n o", n=tiles)).then_inc(out_sem[slot], 16)

            if layer == 0:
                staggered(sp, B * upb, un.per_loop, [(0, store), (upb + 1, load_half), (upb + 1, load_values)])
            else:
                staggered(sp, B * upb, un.per_loop, [(0, store), (upb + 5, load_batch), (upb + 5, load_values)])
            for k in range(2):
                sp.wait_ge(out_sem[k], 16 * (B // 2) * stores + START)

        @block.gpsimd
        def _(pool):
            pool.memset(mark[:], 0.0)
            pool.memset(vpad[:], 0.0).then_inc(v_zeroed, 1)
            pool.wait_ge(v_zeroed, 1)
            pool.memset(vpad[:, :, :, HD:HD + 1], 1.0).then_inc(v_zeroed, 1)
            pool.wait_ge(v_zeroed, 2)
            begin(pool, v_ready)
            with pool.Fori(0, B // 2) as i:
                for s in range(2):
                    b = 2 * i + s
                    pool.wait_ge(v_in[s], 16 * (i + 1) * (1 if layer == 0 else NT1))
                    pool.wait_ge(valued, upb * (b - 1) + START)
                    pool.wait_ge(v_ready, free(b, 1))
                    pool.tensor_tensor(mark[:], mark[:], mark[:], ALU.mult)
                    pool.tensor_copy(vpad[:, s, :, 0:HD], vraw[:, s]).then_inc(v_ready, 1)

        @block.vector
        def _(dve):
            for slot in range(2):
                dve.memset(ks[:, slot].bitcast(F32), 0.0).then_inc(zeroed, 1)
            begin(dve, maxed, ev_dve, ev_o, normed)
            if layer == 1:
                dve.wait_ge(const, 32)
                dve.tensor_copy(band[:], bandf[:].unsqueeze(2).to_broadcast([P, 3, 2, P]))
                dve.tensor_copy(identb[:], e.ident[:]).then_inc(const, 1)

            def maximum(u, s, i):
                m, k = un.rows(s), s % 2
                dve.wait_ge(scored, done(u))
                dve.wait_ge(expd, free(u))
                if un.edge(s) is None:
                    dve.tensor_reduce(nmax[0:m, k, :], scores(s)[0:m], X, ALU.max, negate=True).then_inc(maxed, 1)
                    return
                nth = 4 * i + 2 * (s // NT1) + un.edge(s)
                dve.tensor_reduce(raw[0:m, :], scores(s)[0:m], X, ALU.max, negate=True).then_inc(padmax, 1)
                dve.wait_ge(padmax, nth + 1)
                dve.tensor_scalar(low[0:m, un.edge(s), :], raw[0:m, :], 0.0, None, ALU.min)
                dve.tensor_scalar(nmax[0:m, k, :], raw[0:m, :], edges[0:m, un.edge(s), 1:2], None,
                                  ALU.min).then_inc(maxed, 1)

            def turn_out(u, s, i):
                m, k = un.rows(s), s % 2
                dve.wait_ge(turned, done(u))
                dve.wait_ge(valued, free(u))
                dve.tensor_copy(pt[:, k, 0:512].rearrange("p (h t) -> p h t", h=4)[:, :, 0:m],
                                t_bank[:, 0, :].rearrange("p (h t) -> p h t", h=4)[:, :, 0:m]).then_inc(ev_dve, 1)

            def value_out(u, s, i):
                m, k = un.rows(s), s % 2
                dve.wait_ge(valued, done(u))
                dve.wait_ge(back, free(u))
                dve.tensor_copy(osb[:, k, :].rearrange("p (g t) -> p g t", g=2)[:, :, 0:m],
                                o_bank[:, 0, 0:2 * P].rearrange("p (g t) -> p g t", g=2)[:, :, 0:m]).then_inc(ev_o, 1)

            def divide(u, s, i):
                m, k = un.rows(s), s % 2
                dve.wait_ge(back, done(u))
                o = b_bank[0:m, 0, 0:2 * P].rearrange("p (h d) -> p h d", d=HP)
                if un.edge(s) is None:
                    steps = u + 1 if layer == 0 else u + 4 * i + 2 * (s // NT1) + 2
                    dve.reciprocal(rinv[0:m, k, :], o[:, :, HD]).then_inc(inv, 1)
                else:
                    ed = un.edge(s)
                    steps = u + 4 * i + 2 * (s // NT1) + 2 + ed
                    dve.scalar_tensor_tensor(den[0:m, :], epad[0:m, ed, :], edges[0:m, ed, 0:1], o[:, :, HD],
                                             ALU.mult, ALU.add).then_inc(inv, 1)
                    dve.wait_ge(inv, steps - 1)
                    dve.reciprocal(rinv[0:m, k, :], den[0:m, :]).then_inc(inv, 1)
                dve.wait_ge(inv, steps)
                slot, unit = s // upb, s % upb
                if unit == 0:
                    dve.wait_ge(out_sem[slot], 16 * stores * i + START)
                if layer == 0:
                    dst = att[:, slot, unit * P:(unit + 1) * P].rearrange("p (h d m) -> p h m d", h=2, m=M)
                    g = lambda a: a.rearrange("p (h m) d -> p h m d", h=2)
                    dve.tensor_tensor(dst, g(o[:, :, 0:HD]),
                                      g(rinv[:, k, :].unsqueeze(2).to_broadcast([P, UH, HD])),
                                      ALU.mult).then_inc(normed, 1)
                else:
                    dve.tensor_tensor(att[0:m, slot, unit * P:(unit + 1) * P].rearrange("p (h d) -> p h d", d=HD), o[:, :, 0:HD],
                                      rinv[0:m, k, :].unsqueeze(2).to_broadcast([m, UH, HD]),
                                      ALU.mult).then_inc(normed, 1)

            staggered(dve, B * upb, un.per_loop, [(4, maximum), (2, turn_out), (1, value_out), (0, divide)])

        @block.scalar
        def _(act):
            begin(act, expd, ev_act)

            def exponential(u, s, i):
                m, k = un.rows(s), s % 2
                act.wait_ge(maxed, done(u))
                act.wait_ge(turned, free(u))
                if un.edge(s) is not None:
                    act.activation(epad[0:m, un.edge(s), :], low[0:m, un.edge(s), :], ACT.Exp)
                for h in range(UH):
                    a = act.activation(probs[0:m, k, h, :], scores(s)[0:m, h, :], ACT.Exp,
                                       bias=nmax[0:m, k, h:h + 1])
                a.then_inc(expd, 1)

            def turn_out(u, s, i):
                m, k = un.rows(s), s % 2
                act.wait_ge(turned, done(u))
                act.wait_ge(valued, free(u))
                act.activation(pt[:, k, 512:1024].rearrange("p (h t) -> p h t", h=4)[:, :, 0:m],
                               t_bank[:, 1, :].rearrange("p (h t) -> p h t", h=4)[:, :, 0:m],
                               ACT.Copy).then_inc(ev_act, 1)

            staggered(act, B * upb, un.per_loop, [(3, exponential), (2, turn_out)])

        @block.tensor
        def _(pe):
            begin(pe, scored, turned, valued, back)
            if layer == 1:
                pe.wait_ge(const, 33)

            def score(u, s, i):
                m, k = un.rows(s), s % 2
                if layer == 0:
                    slot = s // 4 % 2
                    if s % 4 == 0:
                        pe.wait_ge(qk_in[slot], 192 * (2 * i + s // 8 + 1))
                else:
                    slot = s // NT1
                    if un.first(s):
                        pe.wait_ge(qk_in[slot], 192 * (i + 1))
                pe.wait_ge(expd, free(u))
                for j in range(4):
                    out = s_bank[0:m, 2 * k + j // 2, (j % 2) * 256:(j % 2) * 256 + 256]
                    out = out.rearrange("p (a x) -> p a x", a=2)
                    if layer == 0:
                        a = pe.matmul(out, qs[:, slot, 4 * (s % 4) + j, :], ks[:, slot, 4 * (s % 4) + j, :, :],
                                      start=True, stop=True, skip_group_check=True)
                    else:
                        t0, _, w0 = t_range(s % NT1)
                        kind = {None: 1, 0: 0, 1: 2}[un.edge(s)]
                        pe.matmul(out, qs[:, slot, j, t0:t0 + m], ks[:, slot, j, :, w0:w0 + P],
                                  start=True, stop=False, skip_group_check=True)
                        a = pe.matmul(out, identb[:, 0:m], band[:, kind, :, :],
                                      start=False, stop=True, skip_group_check=True)
                a.then_inc(scored, 1)

            def turn(u, s, i):
                m, k = un.rows(s), s % 2
                pe.wait_ge(expd, done(u))
                pe.wait_ge(ev_dve, free(u, 1))
                pe.wait_ge(ev_act, free(u, 1))
                for h in range(UH):
                    a = pe.transpose(t_bank[:, h // 4, h % 4 * P:h % 4 * P + m], probs[0:m, k, h, :],
                                     e.ident[0:m, 0:m])
                a.then_inc(turned, 1)

            def value(u, s, i):
                m, k = un.rows(s), s % 2
                slot = s // upb
                if un.first(s):
                    pe.wait_ge(v_ready, done(2 * i + slot))
                pe.wait_ge(ev_dve, done(u))
                pe.wait_ge(ev_act, done(u))
                pe.wait_ge(ev_o, free(u, 1))
                for g in range(2):
                    for j in range(4):
                        h = 4 * g + j
                        a = pe.matmul(o_bank[32 * j:32 * j + 32, 0, g * P:g * P + m],
                                      vpad[:, slot, UH * (s % upb) + h, :], pt[:, k, h * P:h * P + m],
                                      start=True, stop=True, skip_group_check=True)
                a.then_inc(valued, 1)

            def turn_back(u, s, i):
                m, k = un.rows(s), s % 2
                pe.wait_ge(ev_o, done(u))
                pe.wait_ge(normed, free(u, 1))
                for g in range(2):
                    a = pe.transpose(b_bank[0:m, 0, g * P:(g + 1) * P], osb[:, k, g * P:g * P + m], e.ident[:])
                a.then_inc(back, 1)

            staggered(pe, B * upb, un.per_loop, [(4, score), (2, turn), (1, value), (0, turn_back)])


def attend0(nc, e):
    attend(nc, e, 0)



def gemm(nc, e, name, weight, src, resid, gate, bias, dst, mask=None):
    n = name + "_"
    ln_on = src is None
    with Stage(nc) as ctx:
        sb, ps, sem = scope(nc, ctx)
        w = weight(ctx)
        if ln_on:
            ln = Norm(nc, ctx, n + "ln")
        xin = sb(n + "xin", [P, 4, D])
        rows = sb(n + "rows", [P, 4, D])
        xt = [sb(n + "xt_hi", [P, 2, NC, P], F32R), sb(n + "xt_lo", [P, 2, NC, P], F32R)]
        biasb = sb(n + "biasb", [P, D])
        out = sb(n + "out", [P, 2, D])
        tb = ps(n + "tb", [P, 4, 512]); gb = ps(n + "gb", [P, 4, 512])
        bias_in = sem(n + "bias_in"); masked = sem(n + "masked")
        x_in = [sem(n + f"x_in{k}") for k in range(4)]
        ready = sem(n + "ready") if ln_on else None
        turned = sem(n + "turned"); xhi = sem(n + "xhi"); xlo = sem(n + "xlo"); mm = sem(n + "mm")
        based = sem(n + "based"); summed = sem(n + "res_added")
        out_sem = [sem(n + f"out{k}") for k in range(2)]
        block = ctx.enter_context(nc.Block())
        loads = 1 if ln_on else 2
        halves = lambda a: a.rearrange("p (a b) -> p a b", a=2)

        @block.sync
        def _(sp):
            begin(sp, *out_sem)
            sp.dma_start(biasb[:], bias.partition_broadcast(P)).then_inc(bias_in, 16)
            w.load(sp)

            def load(t, s, i):
                sp.wait_ge(summed, free(t, 4))
                sp.dma_start(xin[:, s, :], resid[t]).then_inc(x_in[s], 16)
                if not ln_on:
                    sp.wait_ge(turned, free(t, 4))
                    sp.dma_start(rows[:, s, :], src[t]).then_inc(x_in[s], 16)

            def store(t, s, i):
                sp.wait_ge(summed, done(t))
                sp.dma_start(dst[t], out[:, s % 2, :]).then_inc(out_sem[s % 2], 16)

            staggered(sp, B, 4, [(3, load), (0, store)])
            for k in range(2):
                sp.wait_ge(out_sem[k], 16 * (B // 2) + START)

        if ln_on:
            @block.gpsimd
            def _(pool):
                ln.pool(pool, B // 2)

        @block.vector
        def _(dve):
            dve.wait_ge(bias_in, 16)
            if mask is not None:
                dve.tensor_tensor(biasb[:], biasb[:], mask, ALU.mult).then_inc(masked, 1)
            w.split_lo(dve, gb)
            begin(dve, xlo, summed)
            if ln_on:
                begin(dve, ready)
            if mask is not None:
                dve.wait_ge(masked, 1)

            def normalise(t, s, i):
                k = s % 2
                dve.wait_ge(x_in[s], 16 * loads * (i + 1))
                if ln_on:
                    dve.wait_ge(turned, free(t))
                    ln.run(dve, t, k, xin[:, s, :], rows[:, k, :]).then_inc(ready, 1)
                    dve.wait_ge(ready, done(t))
                dve.scalar_tensor_tensor(xin[:, s, :], biasb[:], gate(t), xin[:, s, :],
                                         ALU.mult, ALU.add).then_inc(based, 1)

            def turned_lo(t, s, i):
                k = s % 2
                dve.wait_ge(xhi, done(t))
                dve.tensor_tensor(xt[1][:, k].rearrange("p (a c) t -> p a (c t)", a=2),
                                  tb[:, 2 * k:2 * k + 2, :],
                                  xt[0][:, k].rearrange("p (a c) t -> p a (c t)", a=2).bitcast(F32),
                                  ALU.subtract).then_inc(xlo, 1)

            def output(t, s, i):
                k = s % 2
                dve.wait_ge(mm, done(t))
                dve.wait_ge(based, t + 1)
                dve.wait_ge(out_sem[k], 16 * (2 * i + s // 2) + START)
                dve.scalar_tensor_tensor(halves(out[:, k, :]), gb[:, 2 * k:2 * k + 2, :], gate(t),
                                         halves(xin[:, s, :]), ALU.mult, ALU.add).then_inc(summed, 1)

            staggered(dve, B, 4, [(2, normalise), (1, turned_lo), (0, output)])

        @block.scalar
        def _(act):
            w.split_hi(act, gb)
            begin(act, xhi)

            def turned_hi(t, s, i):
                k = s % 2
                act.wait_ge(turned, done(t))
                act.wait_ge(mm, free(t))
                act.activation(xt[0][:, k].rearrange("p (a c) t -> p a (c t)", a=2),
                               tb[:, 2 * k:2 * k + 2, :], ACT.Copy).then_inc(xhi, 1)

            staggered(act, B, 4, [(0, turned_hi)])

        @block.tensor
        def _(pe):
            if w.lowrank:
                w.lowrank_product(pe, gb)
            begin(pe, turned, mm)

            def turn(t, s, i):
                if ln_on:
                    pe.wait_ge(ready, done(t))
                else:
                    pe.wait_ge(x_in[s], 16 * loads * (i + 1))
                pe.wait_ge(xlo, free(t))
                for c in range(NC):
                    m = pe.transpose(tb[:, 2 * (s % 2) + c // 4, c % 4 * P:(c % 4 + 1) * P],
                                     rows[:, s % 2 if ln_on else s, c * P:(c + 1) * P], e.ident[:])
                m.then_inc(turned, 1)

            def half(t, s, h):
                k = s % 2
                return three_passes(pe, gb[:, 2 * k + h, :], lambda x, c: xt[x][:, k, c, :],
                                    lambda y, c: (w.hi, w.lo)[y][:, c, h * 512:(h + 1) * 512], range(NC))

            def first_half(t, s, i):
                pe.wait_ge(xlo, done(t))
                pe.wait_ge(summed, free(t))
                half(t, s, 0)

            def second_half(t, s, i):
                half(t, s, 1).then_inc(mm, 1)

            w.ready(pe)
            staggered(pe, B, 4, [(0, first_half), (1, turn), (0, second_half)])


def project_o0(nc, e):
    gemm(nc, e, "wo", lambda ctx: PlainWeight(nc, ctx, "wo", e.i["WoT0"]), e.att0, e.i["x"],
         lambda t: e.gate[:, 0:1], e.i["bo0"], e.x1)


def ffn0(nc, e):
    low = (e.i["A0"], e.i["BfT0"], e.i["coeffs"], e.i["scales"])
    gemm(nc, e, "f0", lambda ctx: PlainWeight(nc, ctx, "f0", e.i["WfT0"], low), None, e.x1,
         lambda t: e.gate[:, 2:3], e.i["bf0"], e.x2)


def ffn1(nc, e):
    gemm(nc, e, "f1", lambda ctx: PlainWeight(nc, ctx, "f1", e.i["WfT1"], mask=e.row_mask[:]), None, e.x3,
         lambda t: e.token_gate[:, bass.ds(t, 1)], e.i["bf1"], e.out, mask=e.row_mask[:])



def project1(nc, e):
    with Stage(nc) as ctx:
        sb, ps, sem = scope(nc, ctx)
        ln = Norm(nc, ctx, "p1ln")
        wt = sb("p1_wt", [P, 4, P]); b = sb("p1_b", [P, 4]); bvb = sb("p1_bvb", [P, P])
        xin = sb("p1_xin", [P, 4, D]); xn = sb("p1_xn", [P, 2, D]); cin = sb("p1_cin", [P, 4, D])
        qk = [[sb(f"p1_{x}_{p}", [P, 2, D], F32R) for p in ("hi", "lo")] for x in "qk"]
        vout = sb("p1_v", [P, 2, NC, P])
        banks = [ps("p1_qb", [P, 2, 512]), ps("p1_kb", [P, 2, 512])]
        vb = ps("p1_vb", [P, 2, 512])
        w_in = sem("p1_w_in"); scaled = sem("p1_scaled")
        x_in = [sem(f"p1_x_in{k}") for k in range(4)]; c_in = [sem(f"p1_c_in{k}") for k in range(4)]
        normed = sem("p1_normed")
        mm = [sem("p1_qmm"), sem("p1_kmm")]; hi = [sem("p1_qhi"), sem("p1_khi")]
        lo = [sem("p1_qlo"), sem("p1_klo")]
        vmm = sem("p1_vmm"); vdone = sem("p1_vdone")
        out_sem = [sem(f"p1_out{k}") for k in range(2)]
        block = ctx.enter_context(nc.Block())
        halves = lambda a: a.rearrange("p (a b) -> p a b", a=2)

        @block.sync
        def _(sp):
            begin(sp, *out_sem)
            for dst, src in ((wt[:], e.i["WT1"]), (b[:], e.i["b1"]), (bvb[:], e.i["bv1"].partition_broadcast(P))):
                sp.dma_start(dst, src).then_inc(w_in, 16)

            def load(t, s, i):
                sp.wait_ge(normed, free(t, 4))
                sp.dma_start(xin[:, s, :], e.x2[t]).then_inc(x_in[s], 16)
                sp.wait_ge(vmm, free(t, 4))
                sp.dma_start(cin[:, s, :], e.i["ctx"][t]).then_inc(c_in[s], 16)

            def store(t, s, i):
                k = s % 2
                for j, dram in ((1, e.k1), (0, e.q1)):
                    sp.wait_ge(lo[j], done(t))
                    for p in range(2):
                        sp.dma_start(dram[p][t], qk[j][p][:, k, :].bitcast(F32)).then_inc(out_sem[k], 16)
                sp.wait_ge(vdone, done(t))
                sp.dma_start(e.v1[t].rearrange("(c p) o -> p c o", p=P), vout[:, k]).then_inc(out_sem[k], 16)

            staggered(sp, B, 4, [(3, load), (0, store)])
            for k in range(2):
                sp.wait_ge(out_sem[k], 80 * (B // 2) + START)

        @block.gpsimd
        def _(pool):
            ln.pool(pool, B // 2)

        @block.vector
        def _(dve):
            begin(dve, normed, lo[0], lo[1], vdone)
            dve.wait_ge(w_in, 48)
            dve.tensor_scalar(wt[:, 0, :], wt[:, 0, :], QS, None, ALU.mult)
            dve.tensor_scalar(b[:, 0:1], b[:, 0:1], QS, None, ALU.mult).then_inc(scaled, 1)
            dve.wait_ge(scaled, 1)

            def inputs(t, s, i):
                k = s % 2
                dve.wait_ge(x_in[s], 16 * i + 16)
                dve.wait_ge(mm[0], free(t))
                ln.run(dve, t, k, xin[:, s, :], xn[:, k, :]).then_inc(normed, 1)

            def outputs(t, s, i):
                k = s % 2
                for j in (1, 0):
                    dve.wait_ge(hi[j], done(t))
                    dve.scalar_tensor_tensor(halves(qk[j][1][:, k, :]), banks[j][:], b[:, j:j + 1],
                                             halves(qk[j][0][:, k, :]).bitcast(F32),
                                             ALU.add, ALU.subtract).then_inc(lo[j], 1)
                    if j == 1:
                        dve.wait_ge(vmm, done(t))
                        dve.wait_ge(out_sem[k], 80 * (2 * i + s // 2) + START)
                        dve.tensor_tensor(vout[:, k], vb[:].rearrange("p a (c o) -> p (a c) o", o=P),
                                          bvb[:].unsqueeze(1).to_broadcast([P, NC, P]), ALU.add).then_inc(vdone, 1)

            staggered(dve, B, 4, [(1, inputs), (0, outputs)])

        @block.scalar
        def _(act):
            begin(act, hi[0], hi[1])
            act.wait_ge(scaled, 1)

            def outputs(t, s, i):
                k = s % 2
                act.wait_ge(out_sem[k], 80 * (2 * i + s // 2) + START)
                for j in (1, 0):
                    act.wait_ge(mm[j], done(t))
                    act.activation(halves(qk[j][0][:, k, :]), banks[j][:], ACT.Identity,
                                   bias=b[:, j:j + 1]).then_inc(hi[j], 1)

            staggered(act, B, 4, [(0, outputs)])

        @block.tensor
        def _(pe):
            begin(pe, mm[0], mm[1], vmm)
            pe.wait_ge(scaled, 1)

            def products(t, s, i):
                pe.wait_ge(c_in[s], 16 * i + 16)
                pe.wait_ge(lo[1], free(t, 1))
                for h in range(2):
                    m = pe.matmul(banks[1][:, h, :], wt[:, 1, :], cin[:, s, h * 512:(h + 1) * 512],
                                  start=True, stop=True)
                m.then_inc(mm[1], 1)
                pe.wait_ge(vdone, free(t, 1))
                for c in range(NC):
                    m = pe.matmul(vb[:, c // 4, c % 4 * P:(c % 4 + 1) * P], cin[:, s, c * P:(c + 1) * P],
                                  wt[:, 2, :], start=True, stop=True, skip_group_check=True)
                m.then_inc(vmm, 1)
                pe.wait_ge(normed, done(t))
                pe.wait_ge(lo[0], free(t, 1))
                for h in range(2):
                    m = pe.matmul(banks[0][:, h, :], wt[:, 0, :], xn[:, s % 2, h * 512:(h + 1) * 512],
                                  start=True, stop=True)
                m.then_inc(mm[0], 1)

            staggered(pe, B, 4, [(0, products)])


def attend1(nc, e):
    attend(nc, e, 1)



def select(nc, e):
    with Stage(nc) as ctx:
        sb, ps, sem = scope(nc, ctx)
        ln = Norm(nc, ctx, "seln")
        wt = sb("se_wt", [P, P]); b = sb("se_b", [P, 4]); gbo = sb("se_gbo", [P, 1])
        cent = sb("se_cent", [P, NC, NCL]); iota = sb("se_iota", [NCL, 1])
        assign = sb("se_assign", [NCL, D], I32); onehot = sb("se_onehot", [NCL, D])
        a_in = sb("se_a", [P, 4, NC, P]); x2 = sb("se_x2", [P, 4, D])
        att_t = sb("se_att_t", [P, 2, D]); delta = sb("se_delta", [P, 2, D])
        x3 = sb("se_x3", [P, 2, D]); xn = sb("se_xn", [P, 2, D]); xt = sb("se_xt", [P, 2, NC, P])
        low = sb("se_low", [P, 2, 2]); ex = sb("se_ex", [P, 2, NCL]); total = sb("se_total", [P, 1]); share = sb("se_share", [P, 1])
        hits = sb("se_hits", [P, NCL]); seen = sb("se_seen", [P, NCL]); any_ = sb("se_any", [P, 1])
        ones = sb("se_ones", [P, 1]); sel = sb("se_sel", [NCL, P])
        ab = ps("se_ab", [P, 2, 512]); ob = ps("se_ob", [P, 2, 512]); xb = ps("se_xb", [P, 2, 512])
        lb = ps("se_lb", [P, 1, 512]); cb = ps("se_cb", [P, 1, 512])
        w_in = sem("se_w_in"); prep = sem("se_prep")
        a_in_sem = [sem(f"se_a_in{k}") for k in range(4)]; x2_in = [sem(f"se_x2_in{k}") for k in range(4)]
        a_turned = sem("se_a_turned"); a_out = sem("se_a_out"); o_mm = sem("se_o_mm"); o_out = sem("se_o_out")
        summed = sem("se_summed"); normed = sem("se_normed"); x_turned = sem("se_x_turned")
        x_out = sem("se_x_out"); logit = sem("se_logit"); lowed = sem("se_lowed"); expd = sem("se_expd")
        small = sem("se_small"); lows = sem("se_lows"); chosen = sem("se_chosen"); fin = sem("se_fin"); fin_pe = sem("se_fin_pe")
        out_sem = [sem(f"se_out{k}") for k in range(2)]
        block = ctx.enter_context(nc.Block())
        halves = lambda a: a.rearrange("p (a b) -> p a b", a=2)

        def batches(eng, stages):
            pairs = [(lead, lambda t, place, i, f=f: f(t, place % 2, place, i)) for lead, f in stages]
            staggered(eng, B, 4, pairs)

        @block.sync
        def _(sp):
            begin(sp, *out_sem)
            for dst, src in ((wt[:], e.i["WT1"][:, 3, :]), (b[:], e.i["b1"]),
                             (cent[:], e.i["centT"].rearrange("(c p) n -> p c n", p=P)),
                             (iota[:], e.i["iota"]), (assign[:], e.i["assign"].partition_broadcast(NCL))):
                sp.dma_start(dst, src).then_inc(w_in, 16)

            def load(t, s, place, i):
                sp.wait_ge(a_turned, free(t, 4))
                sp.dma_start(a_in[:, place], e.att1[t].rearrange("(c p) o -> p c o", p=P)).then_inc(a_in_sem[place], 16)
                sp.wait_ge(summed, free(t, 4))
                sp.dma_start(x2[:, place, :], e.x2[t]).then_inc(x2_in[place], 16)

            def store(t, s, place, i):
                sp.wait_ge(summed, done(t))
                sp.dma_start(e.x3[t], x3[:, s, :]).then_inc(out_sem[s], 16)

            batches(sp, [(3, load), (0, store)])
            for k in range(2):
                sp.wait_ge(out_sem[k], 16 * (B // 2) + START)

        @block.gpsimd
        def _(pool):
            ln.pool(pool, B // 2)

        @block.vector
        def _(dve):
            begin(dve, summed, normed, lowed, chosen)
            dve.memset(seen[:], 0.0)
            dve.memset(ones[:], 1.0)
            dve.wait_ge(w_in, 80)
            dve.tensor_copy(onehot[:], assign[:]).then_inc(prep, 1)
            dve.wait_ge(prep, 1)
            dve.tensor_scalar(onehot[:], onehot[:], iota[:, 0:1], None, ALU.is_equal)
            dve.tensor_tensor(gbo[:], b[:, 3:4], e.gate[:, 1:2], ALU.mult).then_inc(prep, 1)
            dve.wait_ge(prep, 2)

            def residual(t, s, place, i):
                dve.wait_ge(x2_in[place], 16 * i + 16)
                dve.wait_ge(o_out, done(t))
                dve.wait_ge(out_sem[s], 16 * (2 * i + place // 2) + START)
                dve.tensor_tensor(x3[:, s, :], delta[:, s, :], x2[:, place, :], ALU.add).then_inc(summed, 1)
                dve.wait_ge(summed, done(t))
                dve.wait_ge(x_turned, free(t))
                ln.run(dve, t, s, x3[:, s, :], xn[:, s, :]).then_inc(normed, 1)

            def lowest(t, s, place, i):
                dve.wait_ge(logit, done(t))
                dve.tensor_reduce(low[:, s, 0:1], lb[:, 0, 0:NCL], X, ALU.max, negate=True).then_inc(lows, 1)
                dve.wait_ge(lows, t + 1)
                dve.tensor_scalar(low[:, s, 1:2], low[:, s, 0:1], 10.0, None, ALU.mult).then_inc(lowed, 1)

            def choose(t, s, place, i):
                dve.wait_ge(expd, done(t))
                dve.tensor_reduce(total[:], ex[:, s, :], X, ALU.add).then_inc(small, 1)
                dve.wait_ge(small, 4 * t + 1)
                dve.reciprocal(share[:], total[:]).then_inc(small, 1)
                dve.wait_ge(small, 4 * t + 2)
                dve.tensor_scalar(hits[:], ex[:, s, :], share[:, 0:1], 0.01, ALU.mult, ALU.is_gt).then_inc(small, 1)
                dve.wait_ge(small, 4 * t + 3)
                dve.tensor_tensor(seen[:], seen[:], hits[:], ALU.max)
                dve.tensor_reduce(any_[:], hits[:], X, ALU.max).then_inc(small, 1)
                dve.wait_ge(small, 4 * t + 4)
                dve.tensor_scalar(e.token_gate[:, bass.ds(t, 1)], any_[:], e.gate[:, 3:4], None,
                                  ALU.mult).then_inc(chosen, 1)

            batches(dve, [(3, residual), (1, lowest), (0, choose)])
            dve.wait_ge(fin_pe, 1)
            dve.tensor_scalar(sel[:], cb[0:NCL, 0, 0:1].to_broadcast([NCL, P]), 1.0, None, ALU.min).then_inc(fin, 1)
            dve.wait_ge(fin_pe, 2)
            dve.tensor_copy(halves(e.row_mask[:]), ob[:]).then_inc(fin, 1)
            dve.wait_ge(fin, 2)

        @block.scalar
        def _(act):
            begin(act, a_out, o_out, x_out, expd)
            act.wait_ge(prep, 2)

            def attention_out(t, s, place, i):
                act.wait_ge(a_turned, done(t))
                act.wait_ge(o_mm, free(t))
                act.activation(halves(att_t[:, s, :]), ab[:], ACT.Copy).then_inc(a_out, 1)

            def projected(t, s, place, i):
                act.wait_ge(o_mm, done(t))
                act.wait_ge(summed, free(t))
                act.activation(halves(delta[:, s, :]), ob[:], ACT.Identity, bias=gbo[:],
                               scale=e.gate[:, 1:2]).then_inc(o_out, 1)

            def rows_out(t, s, place, i):
                act.wait_ge(x_turned, done(t))
                act.wait_ge(logit, free(t))
                act.activation(xt[:, s].rearrange("p (a c) t -> p a (c t)", a=2), xb[:], ACT.Copy).then_inc(x_out, 1)

            def exponential(t, s, place, i):
                act.wait_ge(lowed, done(t))
                act.activation(ex[:, s, :], lb[:, 0, 0:NCL], ACT.Exp, bias=low[:, s, 1:2],
                               scale=10.0).then_inc(expd, 1)

            batches(act, [(4, attention_out), (3, projected), (2, rows_out), (1, exponential)])

        @block.tensor
        def _(pe):
            begin(pe, a_turned, o_mm, x_turned, logit)
            pe.wait_ge(prep, 2)

            def turn_attention(t, s, place, i):
                pe.wait_ge(a_in_sem[place], 16 * i + 16)
                pe.wait_ge(a_out, free(t, 1))
                for c in range(NC):
                    m = pe.transpose(ab[:, c // 4, c % 4 * P:(c % 4 + 1) * P], a_in[:, place, c, :], e.ident[:])
                m.then_inc(a_turned, 1)

            def project(t, s, place, i):
                pe.wait_ge(a_out, done(t))
                pe.wait_ge(o_out, free(t, 1))
                for h in range(2):
                    m = pe.matmul(ob[:, h, :], wt[:], att_t[:, s, h * 512:(h + 1) * 512], start=True, stop=True)
                m.then_inc(o_mm, 1)

            def turn_rows(t, s, place, i):
                pe.wait_ge(normed, done(t))
                pe.wait_ge(x_out, free(t, 1))
                for c in range(NC):
                    m = pe.transpose(xb[:, c // 4, c % 4 * P:(c % 4 + 1) * P], xn[:, s, c * P:(c + 1) * P],
                                     e.ident[:])
                m.then_inc(x_turned, 1)

            def logits(t, s, place, i):
                pe.wait_ge(x_out, done(t))
                pe.wait_ge(expd, free(t, 1))
                for c in range(NC):
                    m = pe.matmul(lb[:, 0, 0:NCL], xt[:, s, c, :], cent[:, c, :], start=(c == 0), stop=(c == NC - 1))
                m.then_inc(logit, 1)

            batches(pe, [(4, turn_attention), (3, project), (2, turn_rows), (1, logits)])
            pe.wait_ge(chosen, done(B - 1))
            pe.matmul(cb[0:NCL, 0, 0:1], seen[:], ones[:], start=True, stop=True).then_inc(fin_pe, 1)
            pe.wait_ge(fin, 1)
            for h in range(2):
                m = pe.matmul(ob[:, h, :], sel[:], onehot[:, h * 512:(h + 1) * 512], start=True, stop=True)
            m.then_inc(fin_pe, 1)



def program(nc, ins, out, stages=99):
    e = Env()
    e.i = ins
    dram = lambda name, shape, dt=F32: nc.dram_tensor(name, shape, dt).ap()
    e.q0 = [dram(f"q0_{n}", [D, TOK]) for n in ("hi", "lo")]
    e.k0 = [dram(f"k0_{n}", [D, TOK]) for n in ("hi", "lo")]
    e.v0 = dram("v0", [B, P, D])
    e.att0 = dram("att0", [B, P, D])
    e.x1 = dram("x1", [B, P, D]); e.x2 = dram("x2", [B, P, D]); e.x3 = dram("x3", [B, P, D])
    e.q1 = [dram(f"q1_{n}", [B, P, D]) for n in ("hi", "lo")]
    e.k1 = [dram(f"k1_{n}", [B, P, D]) for n in ("hi", "lo")]
    e.v1 = dram("v1", [B, D, P]); e.att1 = dram("att1", [B, D, P])
    with ExitStack() as ctx:
        sb, ps, sem = scope(nc, ctx)
        e.ident = sb("ident_sb", [P, P]); e.fold = sb("fold", [P, NC, P])
        e.gate = sb("gate", [P, 4])
        e.token_gate = sb("token_gate", [P, B]); e.row_mask = sb("row_mask", [P, D])
        e.out = out
        e.bqf = sb("bqf", [P, NC]); e.bkf = sb("bkf", [P, NC]); e.bvf = sb("bvf", [P, D])
        for stage in STAGES[:stages]:
            stage(nc, e)


STAGES = [setup, project_q, project_kv, attend0, project_o0, ffn0, project1, attend1, select, ffn1]


def layout(x, ctx_4096, g_xattn, g_ffn, L0_xattn_Wq, L0_xattn_bq, L0_xattn_Wk, L0_xattn_bk, L0_xattn_Wv, L0_xattn_bv,
           L0_xattn_interference, L0_xattn_amp, L0_xattn_Wo, L0_xattn_bo, L0_ffn_W, L0_ffn_bias, L0_ffn_A, L0_ffn_Bf,
           L0_ffn_coeffs, L0_ffn_scales, L1_xattn_Wq, L1_xattn_bq, L1_xattn_Wk, L1_xattn_bk, L1_xattn_Wv,
           L1_xattn_bv, L1_xattn_Wo, L1_xattn_bo, L1_ffn_weight, L1_ffn_bias, L1_ffn_centroids,
           L1_ffn_assignments):
    part, free_ = np.arange(P)[:, None], np.arange(P)[None, :]
    h, d, i = part // 64, part // 4 % 16, part % 4
    h2, j, d2 = free_ // 64, free_ // 16 % 4, free_ % 16
    same = (h == h2) & (d == d2)
    band, edges = np.full((P, 3, P), 0.0, np.float32), np.zeros((P, 2, 2), np.float32)
    for n, tile in enumerate((0, 1, NT1 - 1)):
        t0, m, w0 = t_range(tile)
        off = w0 + free_ - (t0 + part)
        band[:, n, :] = np.where((off >= -PADL) & (off < WIN - PADL), 0.0, -1e30)
    for n, tile in enumerate((0, NT1 - 1)):
        t = t_range(tile)[0] + np.arange(P)
        edges[:, n, 0] = np.maximum(0, PADL - t) + np.maximum(0, t + WIN - PADL - D)
        edges[:, n, 1] = np.where(edges[:, n, 0] > 0, 0.0, 3e38)
    col = lambda b: np.ascontiguousarray(b.reshape(-1, P).T)
    coef = np.broadcast_to(L0_xattn_interference.reshape(NC, 2, 1, M, M), (NC, 2, HD, M, M))
    er = lambda w: np.ascontiguousarray(np.broadcast_to(w[:, None], (16, 16)).reshape(2, P).T)
    c = np.ascontiguousarray
    f = np.float32
    return {
        "ident": np.eye(P, dtype=f),
        "rep_mask": same.astype(f),
        "perm": (same & (i == j)).astype(f),
        "band": band, "edges": edges,
        "iota": np.arange(NCL, dtype=f)[:, None],
        "coef": c(coef.reshape(NC, P, M).transpose(1, 0, 2)),
        "amp": L0_xattn_amp, "g_xattn": g_xattn, "g_ffn": g_ffn,
        "x": x, "ctx": ctx_4096, "ctxT": c(ctx_4096.reshape(TOK, D).T),
        "Wq0": L0_xattn_Wq, "Wk0": L0_xattn_Wk, "Wv0": L0_xattn_Wv,
        "bq0": col(L0_xattn_bq), "bk0": col(L0_xattn_bk), "bv0": col(L0_xattn_bv),
        "WoT0": c(L0_xattn_Wo.T), "bo0": L0_xattn_bo,
        "WfT0": c(L0_ffn_W.T), "bf0": L0_ffn_bias,
        "A0": c(L0_ffn_A.reshape(256, D)), "BfT0": c(L0_ffn_Bf.transpose(0, 2, 1).reshape(256, D)),
        "coeffs": er(L0_ffn_coeffs), "scales": er(L0_ffn_scales),
        "WT1": c(np.stack([w.T for w in (L1_xattn_Wq, L1_xattn_Wk, L1_xattn_Wv, L1_xattn_Wo)], 1)),
        "b1": c(np.stack([L1_xattn_bq, L1_xattn_bk, L1_xattn_bv, L1_xattn_bo], 1)), "bv1": L1_xattn_bv,
        "WfT1": c(L1_ffn_weight.T), "bf1": L1_ffn_bias,
        "centT": c(L1_ffn_centroids.T), "assign": L1_ffn_assignments,
    }


def kernel(**inputs):
    import concourse.bacc as bacc
    from concourse.bass_utils import run_bass_kernel_spmd

    nc = bacc.Bacc("TRN2", target_bir_lowering=False, num_devices=1)
    arrays = {f"in_{name}": np.ascontiguousarray(a) for name, a in layout(**inputs).items()}
    ins = {name[3:]: nc.dram_tensor(name, a.shape, mybir.dt.from_np(a.dtype), kind="ExternalInput").ap()
           for name, a in arrays.items()}
    out = nc.dram_tensor("out", (B, P, D), F32, kind="ExternalOutput").ap()
    program(nc, ins, out)
    r = run_bass_kernel_spmd(nc, [arrays], core_ids=[0])
    return r.results[0]["out"]
```

```python
from contextlib import ExitStack

import numpy as np

import concourse.bass as bass
from concourse import mybir

F32 = mybir.dt.float32
F32R = mybir.dt.float32r
BF16 = mybir.dt.bfloat16
I32 = mybir.dt.int32
ALU = mybir.AluOpType
ACT = mybir.ActivationFunctionType
X = mybir.AxisListType.X

P = 128
B = 16
D = 1024
NC = D // P
TOK = B * P
M = 4
HD = 16
HP = 32
UH = 8
NU = D // (UH * HD)
WIN, PADL = 16, 8
TSTEP = P - WIN + 1
NT1 = 9
NCL = 64
QS = 0.25
RAW = 4
START = 16


def done(t):
    return t + START + 1


def free(t, depth=2):
    return t + START + 1 - depth


def t_range(i):
    if i == 0:
        return 0, PADL + TSTEP, 0
    t0 = PADL + TSTEP * i
    return t0, min(TSTEP, D - t0), min(t0 - PADL, D - P)


class Env:
    pass


class Stage(ExitStack):

    def __init__(self, nc):
        super().__init__()
        self.nc, self.sems = nc, []
        self.callback(self.clear)

    def clear(self):
        self.nc.clear_and_free_semaphores(self.sems)
        self.nc.all_engine_barrier()


def scope(nc, ctx):
    def sb(name, shape, dt=F32):
        return ctx.enter_context(nc.sbuf_tensor(name, shape, dt))

    def ps(name, shape, dt=F32):
        return ctx.enter_context(nc.psum_tensor(name, shape, dt))

    def sem(name):
        ctx.sems.append(nc.alloc_semaphore(name=name))
        return ctx.sems[-1]

    return sb, ps, sem


def begin(eng, *sems):
    for s in sems:
        eng.sem_inc(s, START)


def one_ahead(eng, turns, first, second, started=False):
    if not started:
        first(0, 0)
    with eng.Fori(0, turns // 2 - 1) as i:
        for s in range(2):
            first(2 * i + s + 1, 1 - s)
            second(2 * i + s, s)
    first(turns - 1, 1)
    second(turns - 2, 0)
    second(turns - 1, 1)



def setup(nc, e):
    with Stage(nc) as ctx:
        sb, ps, sem = scope(nc, ctx)
        rep_mask = sb("rep_mask", [P, P])
        perm = sb("perm", [P, P])
        coef = sb("coef", [P, NC, M])
        amp = sb("amp", [P, 1])
        coefs = sb("coefs", [P, NC, M])
        tmp = sb("tmp", [P, NC, P])
        bqk = sb("bqk", [P, 2, NC]); bv = sb("bv", [P, NC])
        bvr = sb("bvr", [P, NC, P])
        graw = sb("graw", [P, 4])
        pb = ps("pb", [P, 2, 512])
        pv = ps("pv", [P, 2, 512])
        ld = sem("su_ld"); vec = sem("su_vec"); pe_done = sem("su_pe"); gate = sem("su_gate"); folded = sem("su_folded")
        block = ctx.enter_context(nc.Block())
        rep = lambda a: a.partition_broadcast(P)

        @block.sync
        def _(sp):
            for dst, src in ((e.ident[:], e.i["ident"]), (rep_mask[:], e.i["rep_mask"]), (perm[:], e.i["perm"]),
                             (coef[:], e.i["coef"]), (amp[:], rep(e.i["amp"])),
                             (bqk[:, 0, :], e.i["bq0"]), (bqk[:, 1, :], e.i["bk0"]), (bv[:], e.i["bv0"]),
                             (graw[:, 0:2], rep(e.i["g_xattn"])), (graw[:, 2:4], rep(e.i["g_ffn"]))):
                sp.dma_start(dst, src).then_inc(ld, 16)

        @block.scalar
        def _(act):
            act.wait_ge(ld, 160)
            act.activation(e.gate[:], graw[:], ACT.Tanh).then_inc(gate, 1)

        @block.vector
        def _(dve):
            dve.wait_ge(ld, 160)
            dve.tensor_copy(bvr[:], bv[:].unsqueeze(2).to_broadcast([P, NC, P]))
            dve.tensor_scalar(coefs[:], coef[:], amp[:, 0:1], 0.1, ALU.mult, ALU.mult).then_inc(vec, 1)
            dve.wait_ge(vec, 1)
            g4 = lambda a: a.rearrange("p (h j d) -> p h j d", h=2, j=M)
            for c in range(NC):
                co = coefs[:, c, :].unsqueeze(1).unsqueeze(3).to_broadcast([P, 2, M, HD])
                dve.tensor_tensor(g4(tmp[:, c, :]), g4(rep_mask[:]), co, ALU.mult).then_inc(vec, 1)
            for c in range(NC):
                dve.wait_ge(vec, 2 + c)
                dve.tensor_tensor(e.fold[:, c, :], tmp[:, c, :], perm[:], ALU.add).then_inc(folded, 1)
            dve.wait_ge(pe_done, 1)
            both = pb[:, 0, 0:2 * NC].rearrange("p (c x) -> p x c", x=2)
            dve.tensor_scalar(e.bqf[:], both[:, 0, :], QS, None, ALU.mult)
            dve.tensor_copy(e.bkf[:], both[:, 1, :])
            dve.tensor_copy(e.bvf[:].rearrange("p (a b) -> p a b", a=2), pv[:]).then_inc(vec, 1)
            dve.wait_ge(vec, NC + 2)
            dve.wait_ge(gate, 1)

        @block.tensor
        def _(pe):
            for c in range(NC):
                pe.wait_ge(folded, c + 1)
                pe.matmul(pb[:, 0, 2 * c:2 * c + 2], e.fold[:, c, :], bqk[:, :, c], start=True, stop=True,
                          skip_group_check=True)
                m = pe.matmul(pv[:, c // 4, c % 4 * P:(c % 4 + 1) * P], bvr[:, c, :], e.fold[:, c, :],
                              start=True, stop=True, skip_group_check=True)
            m.then_inc(pe_done, 1)



class FoldedWeight:

    def __init__(self, nc, ctx, e, name, src, scale=1.0, share=None, raw=None):
        sb, ps, sem = scope(nc, ctx)
        self.e, self.src, self.scale = e, src, scale
        self.hi = sb(f"{name}_hi", [P, NC, D], F32R)
        self.lo = sb(f"{name}_lo", [P, NC, D], F32R)
        if share:
            self.raw, self.loaded, self.folded = share.raw, share.loaded, share.folded
            self.hi_done, self.lo_done, self.base = share.hi_done, share.lo_done, NC
            return
        self.base = 0
        self.raw = sb(f"{name}_raw", [P, RAW, D]) if raw is None else raw
        self.loaded = [sem(f"{name}_loaded{k}") for k in range(RAW)]
        self.folded = sem(f"{name}_folded")
        self.hi_done = sem(f"{name}_hi_done")
        self.lo_done = sem(f"{name}_lo_done")

    def load(self, sp):
        w = self.src.rearrange("(o p) c -> o p c", p=P)
        with sp.Fori(0, NC // RAW) as i:
            for k in range(RAW):
                sp.wait_ge(self.folded, free(self.base + RAW * i + k, RAW))
                sp.dma_start(self.raw[:, k, :], w[RAW * i + k]).then_inc(self.loaded[k], 16)

    def fold(self, pe, banks):
        if not self.base:
            begin(pe, self.folded)
        with pe.Fori(0, NC // RAW) as i:
            for k in range(RAW):
                pe.wait_ge(self.loaded[k], 16 * (self.base // RAW + i + 1))
                pe.wait_ge(self.lo_done, free(self.base + RAW * i + k))
                for c in range(NC):
                    m = pe.matmul(banks[:, 2 * (k % 2) + c // 4, c % 4 * P:(c % 4 + 1) * P],
                                  self.raw[:, k, c * P:(c + 1) * P],
                                  self.e.fold[:, RAW * i + k, :], start=True, stop=True, skip_group_check=True)
                m.then_inc(self.folded, 1)

    def _views(self, i, k, h, banks):
        v = banks[:, 2 * (k % 2) + h, :].rearrange("p (c o) -> p c o", c=4)
        at = (slice(None), slice(4 * h, 4 * h + 4), bass.ts(RAW * i + k, P))
        return v, self.hi[at], self.lo[at]

    def split_hi(self, act, banks):
        if not self.base:
            begin(act, self.hi_done)
        with act.Fori(0, NC // RAW) as i:
            for k in range(RAW):
                act.wait_ge(self.folded, done(self.base + RAW * i + k))
                for h in range(2):
                    v, hi, _ = self._views(i, k, h, banks)
                    a = act.activation(hi, v, ACT.Copy, scale=self.scale)
                a.then_inc(self.hi_done, 1)

    def split_lo(self, dve, banks):
        if not self.base:
            begin(dve, self.lo_done)
        with dve.Fori(0, NC // RAW) as i:
            for k in range(RAW):
                dve.wait_ge(self.hi_done, done(self.base + RAW * i + k))
                for h in range(2):
                    v, hi, lo = self._views(i, k, h, banks)
                    a = dve.scalar_tensor_tensor(lo, v, self.scale, hi.bitcast(F32), ALU.mult, ALU.subtract)
                a.then_inc(self.lo_done, 1)

    def ready(self, pe):
        pe.wait_ge(self.lo_done, done(self.base + NC - 1))


class LowRankWeight:

    def __init__(self, nc, ctx, name, src, lowrank, raw, a, bt):
        sb, ps, sem = scope(nc, ctx)
        self.src, self.lowrank, self.raw, self.a, self.bt = src, lowrank, raw, a, bt
        self.hi = sb(f"{name}_hi", [P, NC, D], F32R)
        self.lo = sb(f"{name}_lo", [P, NC, D], F32R)
        self.loaded = [sem(f"{name}_loaded{k}") for k in range(RAW)]
        self.hi_done = sem(f"{name}_hi_done")
        self.lo_done = sem(f"{name}_lo_done")
        self.ce = sb(f"{name}_ce", [P, 3, 2])
        self.lr_loaded = sem(f"{name}_lr_loaded")
        self.lr = sem(f"{name}_lr")
        self.summed = sem(f"{name}_summed")

    def load_lowrank(self, sp):
        a, bt, co, sc = self.lowrank
        for dst, src in ((self.ce[:, 0, :], co), (self.ce[:, 1, :], sc),
                         (self.bt, bt.rearrange("(k p) n -> p k n", p=P)),
                         (self.a, a.rearrange("(k p) n -> p k n", p=P))):
            sp.dma_start(dst, src).then_inc(self.lr_loaded, 16)

    def load(self, sp):
        w = self.src.rearrange("(o p) c -> o p c", p=P)
        with sp.Fori(0, NC // RAW) as i:
            for k in range(RAW):
                sp.wait_ge(self.lo_done, free(RAW * i + k, RAW))
                sp.dma_start(self.raw[:, k, :], w[RAW * i + k]).then_inc(self.loaded[k], 16)

    def lowrank_product(self, pe, banks):
        begin(pe, self.lr)
        pe.wait_ge(self.summed, 3)
        for c in range(NC):
            if c > 1:
                pe.wait_ge(self.summed, 3 + c - 1)
            for h in range(2):
                for r in range(2):
                    m = pe.matmul(banks[:, 2 * (c % 2) + h, :], self.a[:, r, c * P:(c + 1) * P],
                                  self.bt[:, r, h * 512:(h + 1) * 512], start=(r == 0), stop=(r == 1))
            m.then_inc(self.lr, 1)

    def split_hi(self, act):
        begin(act, self.hi_done)
        with act.Fori(0, NC // RAW) as i:
            for k in range(RAW):
                act.wait_ge(self.summed, 3 + RAW * i + k + 1)
                act.activation(self.hi[:, RAW * i + k, :], self.raw[:, k, :], ACT.Copy).then_inc(self.hi_done, 1)

    def scale_lowrank(self, dve):
        dve.wait_ge(self.lr_loaded, 64)
        dve.tensor_tensor(self.ce[:, 2, :], self.ce[:, 0, :], self.ce[:, 1, :], ALU.mult).then_inc(self.summed, 1)
        dve.wait_ge(self.summed, 1)
        for r in range(2):
            dve.tensor_scalar(self.bt[:, r, :], self.bt[:, r, :], self.ce[:, 2, r:r + 1], None,
                              ALU.mult).then_inc(self.summed, 1)

    def split_lo(self, dve, banks):
        begin(dve, self.lo_done)
        with dve.Fori(0, NC // RAW) as i:
            for k in range(RAW):
                raw = self.raw[:, k, :]
                dve.wait_ge(self.loaded[k], 16 * i + 16)
                dve.wait_ge(self.lr, done(RAW * i + k))
                dve.tensor_tensor(raw.rearrange("p (a b) -> p a b", a=2),
                                  banks[:, 2 * (k % 2):2 * (k % 2) + 2, :],
                                  raw.rearrange("p (a b) -> p a b", a=2), ALU.add).then_inc(self.summed, 1)
                dve.wait_ge(self.hi_done, done(RAW * i + k))
                dve.tensor_tensor(self.lo[:, RAW * i + k, :], raw, self.hi[:, RAW * i + k, :].bitcast(F32),
                                  ALU.subtract).then_inc(self.lo_done, 1)

    def ready(self, pe):
        pe.wait_ge(self.lo_done, done(NC - 1))


class EarlyWeight:

    def __init__(self, nc, ctx, name, src):
        sb, ps, sem = scope(nc, ctx)
        self.rows = src.rearrange("(o p) c -> o p c", p=P)
        self.hi = sb(f"{name}_hi", [P, NC, D], F32R)
        self.lo = sb(f"{name}_lo", [P, NC, D], F32R)
        self.raw = sb(f"{name}_raw", [P, 1, D])
        self.mark = sb(f"{name}_mark", [P, 1])
        self.loaded = sem(f"{name}_loaded"); self.hi_done = sem(f"{name}_hi_done")
        self.lo_done = sem(f"{name}_lo_done")

    def start(self, pool):
        begin(pool, self.hi_done, self.lo_done)
        pool.memset(self.mark[:], 0.0).then_inc(self.hi_done, 1)

    def load(self, pool, row):
        pool.wait_ge(self.lo_done, row + START)
        pool.dma_start(self.raw[:], self.rows[row].unsqueeze(1)).then_inc(self.loaded, 16)

    def split_hi(self, pool, row):
        pool.wait_ge(self.loaded, 16 * row + 16)
        pool.wait_ge(self.hi_done, row + START + 1)
        pool.tensor_tensor(self.mark[:], self.mark[:], self.mark[:], ALU.mult)
        pool.tensor_copy(self.hi[:, bass.ds(row, 1), :], self.raw[:]).then_inc(self.hi_done, 1)

    def split_lo(self, pool, row):
        pool.wait_ge(self.hi_done, row + START + 2)
        pool.tensor_tensor(self.lo[:, bass.ds(row, 1), :], self.raw[:],
                           self.hi[:, bass.ds(row, 1), :].bitcast(F32), ALU.subtract).then_inc(self.lo_done, 1)

    def ready(self, pe):
        pe.wait_ge(self.lo_done, done(NC - 1))


def three_passes(pe, out, a, b, chunks):
    terms = [(0, 0), (0, 1), (1, 0)]
    n = len(chunks) * len(terms)
    for j, c in enumerate(chunks):
        for i, (x, y) in enumerate(terms):
            m = pe.matmul(out, a(x, c), b(y, c), start=(i + j == 0), stop=(len(terms) * j + i == n - 1))
    return m



class Norm:

    def __init__(self, nc, ctx, name):
        sb, ps, sem = scope(nc, ctx)
        self.stats = sb(f"{name}_stats", [P, 2, 2, 6])
        self.mv = sb(f"{name}_mv", [P, 2, 2])
        self.veps = sb(f"{name}_veps", [P, 2])
        self.rstd = sb(f"{name}_rstd", [P, 2])
        self.power = sb(f"{name}_power", [P, 1])
        self.mark = sb(f"{name}_mark", [P, 1])
        self.step = sem(f"{name}_step")
        self.root = sem(f"{name}_root")

    def start(self, pool):
        pool.memset(self.power[:], -0.5).then_inc(self.root, 1)
        pool.wait_ge(self.root, 1)

    def pool(self, pool, turns, of=2):
        self.start(pool)
        with pool.Fori(0, turns) as i:
            for k in range(of):
                self.pool_tile(pool, of * i + k, k % 2)

    def pool_tile(self, pool, t, k):
        pool.wait_ge(self.step, 3 * t + 3)
        pool.tensor_tensor(self.rstd[:, k:k + 1], self.veps[:, k:k + 1], self.power[:],
                           ALU.pow).then_inc(self.root, 1)

    def run(self, dve, t, k, src, dst):
        for h in range(2):
            a = dve.bn_stats(self.stats[:, k, h, :], src[:, h * 512:(h + 1) * 512])
        a.then_inc(self.step, 1)
        dve.wait_ge(self.step, 3 * t + 1)
        dve.memset(self.mark[:], 0.0)
        dve.bn_aggr(self.mv[:, k, :], self.stats[:, k, :, :]).then_inc(self.step, 1)
        dve.wait_ge(self.step, 3 * t + 2)
        dve.tensor_scalar(self.veps[:, k:k + 1], self.mv[:, k, 1:2], 1e-5, None, ALU.add).then_inc(self.step, 1)
        dve.wait_ge(self.root, t + 2)
        return dve.tensor_scalar(dst, src, self.mv[:, k, 0:1], self.rstd[:, k:k + 1], ALU.subtract, ALU.mult)



def project_q(nc, e):
    G = B // 2
    with Stage(nc) as ctx:
        sb, ps, sem = scope(nc, ctx)
        w = FoldedWeight(nc, ctx, e, "wq", e.i["Wq0"], QS)
        ln = Norm(nc, ctx, "qln")
        xin = sb("q_xin", [P, 4, D]); xn = sb("q_xn", [P, 2, D])
        xt = [sb("q_xt_hi", [P, 2, NC, 2 * P], F32R), sb("q_xt_lo", [P, 2, NC, 2 * P], F32R)]
        out = [sb("q_out_hi", [P, 4, 2 * P], F32R), sb("q_out_lo", [P, 4, 2 * P], F32R)]
        tb = ps("q_tb", [P, 4, 512]); qb = ps("q_qb", [P, 4, 512])
        x_in = [sem(f"q_x_in{k}") for k in range(4)]
        normed = sem("q_normed"); turned = sem("q_turned"); xhi = sem("q_xhi"); xlo = sem("q_xlo")
        mm = sem("q_mm"); qhi = sem("q_qhi"); qlo = sem("q_qlo")
        q_out = [sem(f"q_q_out{s}") for s in range(4)]
        block = ctx.enter_context(nc.Block())

        @block.sync
        def _(sp):
            begin(sp, *q_out)

            def load(g, s, i):
                for k in range(2):
                    sp.wait_ge(normed, free(2 * g + k, 4))
                    sp.dma_start(xin[:, 2 * s + k, :], e.i["x"][2 * g + k]).then_inc(x_in[2 * s + k], 16)

            def store(g, s, i):
                for o in range(NC):
                    sp.wait_ge(qlo, done(NC * g + o))
                    for part, dram in zip(out, e.q0):
                        sp.dma_start(dram[o * P:(o + 1) * P, bass.ts(g, 2 * P)],
                                     part[:, o % 4, :].bitcast(F32)).then_inc(q_out[o % 4], 16)

            load(0, 0, 0)
            w.load(sp)
            load(1, 1, 0)
            staggered(sp, G, 2, [(2, load), (0, store)], started=(load,))
            for k in range(4):
                sp.wait_ge(q_out[k], 32 * (NC // 4) * G + START)

        @block.gpsimd
        def _(pool):
            ln.pool(pool, G)

        @block.vector
        def _(dve):
            begin(dve, normed, xlo, qlo)

            def normalise(g, s, i):
                for k in range(2):
                    dve.wait_ge(x_in[2 * s + k], 16 * i + 16)
                    dve.wait_ge(turned, free(2 * g + k))
                    ln.run(dve, 2 * g + k, k, xin[:, 2 * s + k, :], xn[:, k, :]).then_inc(normed, 1)

            def turned_lo(g, s, i):
                for k in range(2):
                    dve.wait_ge(xhi, done(2 * g + k))
                    for h in range(2):
                        at = (slice(None), s, slice(4 * h, 4 * h + 4), slice(k * P, (k + 1) * P))
                        a = dve.tensor_tensor(xt[1][at], tb[:, 2 * k + h, :].rearrange("p (c t) -> p c t", c=4),
                                              xt[0][at].bitcast(F32), ALU.subtract)
                    a.then_inc(xlo, 1)

            def outputs(g, first):
                for o in range(first, first + NC // 2):
                    dve.wait_ge(qhi, done(NC * g + o))
                    dve.scalar_tensor_tensor(out[1][:, o % 4, :], qb[:, o % 4, 0:2 * P], e.bqf[:, o:o + 1],
                                             out[0][:, o % 4, :].bitcast(F32), ALU.add, ALU.subtract).then_inc(qlo, 1)

            staggered(dve, G, 2, [(1, normalise), (0, lambda g, s, i: outputs(g, 0)), (1, turned_lo),
                                  (0, lambda g, s, i: outputs(g, NC // 2))], between=lambda: w.split_lo(dve, qb))

        @block.scalar
        def _(act):
            begin(act, xhi, qhi)

            def turned_hi(g, s, i):
                for k in range(2):
                    act.wait_ge(turned, done(2 * g + k))
                    for h in range(2):
                        a = act.activation(xt[0][:, s, 4 * h:4 * h + 4, k * P:(k + 1) * P],
                                           tb[:, 2 * k + h, :].rearrange("p (c t) -> p c t", c=4), ACT.Copy)
                    a.then_inc(xhi, 1)

            def outputs(g, first):
                for o in range(first, first + NC // 2):
                    act.wait_ge(mm, done(NC * g + o))
                    act.wait_ge(q_out[o % 4], 32 * ((NC // 4) * g + o // 4) + START)
                    act.activation(out[0][:, o % 4, :], qb[:, o % 4, 0:2 * P], ACT.Identity,
                                   bias=e.bqf[:, o:o + 1]).then_inc(qhi, 1)

            staggered(act, G, 2, [(0, lambda g, s, i: outputs(g, 0)), (1, turned_hi),
                                  (0, lambda g, s, i: outputs(g, NC // 2))], between=lambda: w.split_hi(act, qb))

        @block.tensor
        def _(pe):
            begin(pe, turned, mm)

            def weights():
                w.fold(pe, qb)
                w.ready(pe)

            def turn(g, s, i):
                for k in range(2):
                    pe.wait_ge(normed, done(2 * g + k))
                    pe.wait_ge(xlo, free(2 * g + k))
                    for c in range(NC):
                        m = pe.transpose(tb[:, 2 * k + c // 4, c % 4 * P:(c % 4 + 1) * P],
                                         xn[:, k, c * P:(c + 1) * P], e.ident[:])
                    m.then_inc(turned, 1)

            def product(g, s, first):
                pe.wait_ge(xlo, done(2 * g + 1))
                for o in range(first, first + NC // 2):
                    pe.wait_ge(qlo, free(NC * g + o, 4))
                    three_passes(pe, qb[:, o % 4, 0:2 * P],
                                 lambda x, c: (w.hi, w.lo)[x][:, c, o * P:(o + 1) * P],
                                 lambda y, c: xt[y][:, s, c, :], range(NC)).then_inc(mm, 1)

            staggered(pe, G, 2, [(0, lambda g, s, i: product(g, s, 0)), (1, turn),
                                 (0, lambda g, s, i: product(g, s, NC // 2))], between=weights)


def project_kv(nc, e):
    G = B // 2
    with Stage(nc) as ctx:
        sb, ps, sem = scope(nc, ctx)
        raw = sb("kv_raw", [P, RAW, D])
        vout = raw[:, 0:2, :]
        cin = sb("kv_cin", [P, NC, 2 * P])
        ct = [sb("kv_ct_hi", [P, 2, NC, 2 * P], F32R), sb("kv_ct_lo", [P, 2, NC, 2 * P], F32R)]
        wk = FoldedWeight(nc, ctx, e, "wk", e.i["Wk0"], raw=raw)
        wv = FoldedWeight(nc, ctx, e, "wv", e.i["Wv0"], share=wk)
        out = [sb("kv_k_hi", [P, 2, 2 * P], F32R), sb("kv_k_lo", [P, 2, 2 * P], F32R)]
        kb = ps("kv_kb", [P, 4, 512]); vb = ps("kv_vb", [P, 4, 512])
        c_in = sem("kv_c_in"); chi = sem("kv_chi"); clo = sem("kv_clo"); mm = sem("kv_mm")
        khi = sem("kv_khi"); klo = sem("kv_klo"); vmm = sem("kv_vmm"); vdone = sem("kv_vdone")
        k_out = [sem(f"kv_k_out{s}") for s in range(2)]; v_out = [sem(f"kv_v_out{s}") for s in range(2)]
        block = ctx.enter_context(nc.Block())
        ctx_t = e.i["ctxT"].rearrange("(c p) t -> p c t", p=P)

        @block.sync
        def _(sp):
            begin(sp, *k_out, *v_out)
            def load(g, s, i):
                sp.wait_ge(clo, free(g, 1))
                sp.dma_start(cin[:], ctx_t[:, :, bass.ts(g, 2 * P)]).then_inc(c_in, 16)

            def store_k(g, first):
                for o in range(first, first + NC // 2):
                    sp.wait_ge(klo, done(NC * g + o))
                    for part, dram in zip(out, e.k0):
                        sp.dma_start(dram[o * P:(o + 1) * P, bass.ts(g, 2 * P)],
                                     part[:, o % 2, :].bitcast(F32)).then_inc(k_out[o % 2], 16)

            def store_v(g, s, i):
                for k in range(2):
                    sp.wait_ge(vdone, 2 * (2 * g + k) + 2 + START)
                    sp.dma_start(e.v0[2 * g + k], vout[:, k, :]).then_inc(v_out[k], 16)

            load(0, 0, 0)
            wk.load(sp)
            wv.load(sp)
            load(1, 1, 0)
            staggered(sp, G, 2, [(0, lambda g, s, i: store_k(g, 0)), (2, load),
                                 (0, lambda g, s, i: store_k(g, NC // 2)), (0, store_v)], started=(load,))
            for k in range(2):
                sp.wait_ge(k_out[k], 32 * (NC // 2) * G + START)
                sp.wait_ge(v_out[k], 16 * G + START)

        @block.vector
        def _(dve):
            begin(dve, clo, klo, vdone)

            def inputs(g, s):
                dve.wait_ge(chi, done(g))
                dve.tensor_tensor(ct[1][:, s], cin[:], ct[0][:, s].bitcast(F32), ALU.subtract).then_inc(clo, 1)

            def outputs(g, s):
                for o in range(NC):
                    dve.wait_ge(khi, done(NC * g + o))
                    dve.scalar_tensor_tensor(out[1][:, o % 2, :], kb[:, o % 4, 0:2 * P], e.bkf[:, o:o + 1],
                                             out[0][:, o % 2, :].bitcast(F32), ALU.add, ALU.subtract).then_inc(klo, 1)
                for k in range(2):
                    dve.wait_ge(v_out[k], 16 * g + START)
                    for h in range(2):
                        dve.wait_ge(vmm, done(4 * g + 2 * k + h))
                        dve.tensor_tensor(vout[:, k, h * 512:(h + 1) * 512], vb[:, 2 * k + h, :],
                                          e.bvf[:, h * 512:(h + 1) * 512], ALU.add).then_inc(vdone, 1)

            inputs(0, 0)
            wk.split_lo(dve, kb)
            wv.split_lo(dve, kb)
            one_ahead(dve, G, inputs, outputs, started=True)

        @block.scalar
        def _(act):
            begin(act, chi, khi)

            def inputs(g, s):
                act.wait_ge(c_in, 16 * g + 16)
                act.wait_ge(vmm, 4 * g - 4 + START)
                act.activation(ct[0][:, s], cin[:], ACT.Copy).then_inc(chi, 1)

            def outputs(g, s):
                for o in range(NC):
                    act.wait_ge(mm, done(NC * g + o))
                    act.wait_ge(k_out[o % 2], 32 * ((NC // 2) * g + o // 2) + START)
                    act.activation(out[0][:, o % 2, :], kb[:, o % 4, 0:2 * P], ACT.Identity,
                                   bias=e.bkf[:, o:o + 1]).then_inc(khi, 1)

            inputs(0, 0)
            wk.split_hi(act, kb)
            wv.split_hi(act, kb)
            one_ahead(act, G, inputs, outputs, started=True)

        @block.tensor
        def _(pe):
            begin(pe, mm, vmm)
            wk.fold(pe, kb)
            wv.fold(pe, kb)
            wv.ready(pe)

            def product(g, s):
                pe.wait_ge(clo, done(g))
                for o in range(NC):
                    pe.wait_ge(klo, free(NC * g + o, 4))
                    three_passes(pe, kb[:, o % 4, 0:2 * P],
                                 lambda x, c: (wk.hi, wk.lo)[x][:, c, o * P:(o + 1) * P],
                                 lambda y, c: ct[y][:, s, c, :], range(NC)).then_inc(mm, 1)
                for k in range(2):
                    for h in range(2):
                        pe.wait_ge(vdone, free(4 * g + 2 * k + h, 4))
                        three_passes(pe, vb[:, 2 * k + h, :],
                                     lambda x, c: ct[x][:, s, c, k * P:(k + 1) * P],
                                     lambda y, c: (wv.hi, wv.lo)[y][:, c, h * 512:(h + 1) * 512],
                                     range(NC)).then_inc(vmm, 1)

            with pe.Fori(0, G // 2) as i:
                for s in range(2):
                    product(2 * i + s, s)



def staggered(eng, units, per_loop, stages, between=None, at=0, started=()):
    top = max(lead for lead, _ in stages)
    assert top <= per_loop

    def step(i, s, last):
        for lead, f in stages:
            place = s + lead
            if place < 0 or (last and place >= per_loop) or (s < 0 and f in started):
                continue
            turn = i + 1 if place >= per_loop else i
            f(per_loop * turn + place % per_loop, place % per_loop, turn)

    for s in range(-top, 0):
        if between and s == at:
            between()
        step(0, s, False)
    if between and at == 0:
        between()
    turns = units // per_loop
    with eng.Fori(0, turns - 1) as i:
        for s in range(per_loop):
            step(i, s, False)
    for s in range(per_loop):
        step(turns - 1, s, True)


class Units:

    def __init__(self, layer):
        self.layer = layer
        self.per_batch = NU if layer == 0 else NT1
        self.per_loop = 2 * self.per_batch

    def rows(self, s):
        return P if self.layer == 0 else t_range(s % NT1)[1]

    def first(self, s):
        return s % self.per_batch == 0

    def edge(self, s):
        return {0: 0, NT1 - 1: 1}.get(s % NT1) if self.layer == 1 else None


def attend(nc, e, layer, w=None):
    un = Units(layer)
    n = f"a{layer}_"
    with Stage(nc) as ctx:
        sb, ps, sem = scope(nc, ctx)
        if layer == 0:
            pairs, length = 16, P
        else:
            pairs, length = 4, D
        qs = sb(n + "qs", [P, 2, pairs, length], F32R)
        ks = sb(n + "ks", [P, 2, pairs, 2, length], F32R)
        heads = 64 if layer == 0 else UH * NT1
        vraw = sb(n + "vraw", [P, 2, heads, HD])
        vpad = sb(n + "vpad", [P, 2, heads, HP])
        nmax = sb(n + "nmax", [P, 2, UH])
        probs = sb(n + "probs", [P, 2, UH, P])
        pt = sb(n + "pt", [P, 2, UH * P])
        osb = sb(n + "osb", [P, 2, 2 * P])
        rinv = sb(n + "rinv", [P, 2, UH])
        att = sb(n + "att", [P, 2, un.per_batch * P])
        stores = 1 if layer == 0 else 3
        mark = sb(n + "mark", [P, 1])
        if layer == 1:
            bandf = sb(n + "bandf", [P, 3, P])
            band = sb(n + "band", [P, 3, 2, P], BF16)
            identb = sb(n + "identb", [P, P], BF16)
            edges = sb(n + "edges", [P, 2, 2])
            raw = sb(n + "raw", [P, UH])
            low = sb(n + "low", [P, 2, UH])
            epad = sb(n + "epad", [P, 2, UH])
            den = sb(n + "den", [P, UH])
        s_bank = ps(n + "s_bank", [P, 4, 512]); t_bank = ps(n + "t_bank", [P, 2, 512])
        o_bank = ps(n + "o_bank", [P, 1, 512]); b_bank = ps(n + "b_bank", [P, 1, 512])
        zeroed = [sem(n + "zeroed0"), sem(n + "zeroed1")]; v_zeroed = sem(n + "v_zeroed"); const = sem(n + "const")
        qk_in = [sem(n + f"qk_in{k}") for k in range(2)]
        v_in = [sem(n + f"v_in{k}") for k in range(2)]
        v_ready = sem(n + "v_ready")
        scored = sem(n + "scored"); maxed = sem(n + "maxed"); expd = sem(n + "expd")
        turned = sem(n + "turned"); ev_dve = sem(n + "ev_dve"); ev_act = sem(n + "ev_act")
        valued = sem(n + "valued"); ev_o = sem(n + "ev_o"); back = sem(n + "back")
        inv = sem(n + "inv"); padmax = sem(n + "padmax"); normed = sem(n + "normed")
        out_sem = [sem(n + f"out{k}") for k in range(2)]
        block = ctx.enter_context(nc.Block())
        upb = un.per_batch

        def scores(s):
            return s_bank[:, 2 * (s % 2):2 * (s % 2) + 2, :].rearrange("p b (h x) -> p (b h) x", h=4)

        @block.sync
        def _(sp):
            begin(sp, *out_sem)
            if layer == 1:
                sp.dma_start(bandf[:], e.i["band"]).then_inc(const, 16)
                sp.dma_start(edges[:], e.i["edges"]).then_inc(const, 16)

            def load_half(u, s, i):
                if s % 4:
                    return
                h, b = s // 4 % 2, 2 * i + s // NU
                sp.wait_ge(scored, done(u - 5))
                for j in range(4):
                    q = e.q0[j // 2].rearrange("(h p r) t -> h r p t", h=2, r=32)
                    sp.dma_start(qs[32 * j:32 * j + 32, h, :, :].bitcast(F32),
                                 q[h, :, :, bass.ts(b, P)]).then_inc(qk_in[h], 16)
                sp.wait_ge(zeroed[h], 2 - h)
                for j in range(4):
                    k = e.k0[j % 2].rearrange("(h p r) t -> h r p t", h=2, r=32)
                    for a in range(2):
                        r = 32 * j + 16 * a
                        sp.dma_start(ks[r:r + 16, h, :, a, :].bitcast(F32),
                                     k[h, 16 * a:16 * a + 16, :, bass.ts(b, P)]).then_inc(qk_in[h], 16)

            def load_batch(u, s, i):
                if s % NT1:
                    return
                slot, b = s // NT1, 2 * i + s // NT1
                sp.wait_ge(scored, done(u - NT1 - 1))
                for j in range(4):
                    q = e.q1[j // 2].rearrange("b (p r) t -> b r p t", r=32)
                    sp.dma_start(qs[32 * j:32 * j + 32, slot, :, :].bitcast(F32), q[b]).then_inc(qk_in[slot], 16)
                sp.wait_ge(zeroed[slot], 2 - slot)
                for j in range(4):
                    k = e.k1[j % 2].rearrange("b (p r) t -> b r p t", r=32)
                    for a in range(2):
                        r = 32 * j + 16 * a
                        sp.dma_start(ks[r:r + 16, slot, :, a, :].bitcast(F32),
                                     k[b][16 * a:16 * a + 16]).then_inc(qk_in[slot], 16)

            def load_values(u, s, i):
                if s % upb:
                    return
                slot, b = s // upb, 2 * i + s // upb
                sp.wait_ge(v_ready, free(b))
                if layer == 0:
                    src = e.v0[b].rearrange("t (h d) -> t h d", d=HD)
                    sp.dma_start(vraw[:, slot], src).then_inc(v_in[slot], 16)
                else:
                    for n in range(NT1):
                        w0 = t_range(n)[2]
                        src = e.v1[b][w0:w0 + P, :].rearrange("t (h d) -> t h d", d=HD)
                        sp.dma_start(vraw[:, slot, UH * n:UH * n + UH, :], src).then_inc(v_in[slot], 16)

            def store(u, s, i):
                slot, b = s // upb, 2 * i + s // upb
                if s % upb != upb - 1:
                    return
                sp.wait_ge(normed, done(u))
                if layer == 0:
                    sp.dma_start(e.att0[b], att[:, slot, :]).then_inc(out_sem[slot], 16)
                    return
                for t0, m, tile, tiles in ((*t_range(0)[:2], 0, 1), (*t_range(1)[:2], 1, NT1 - 2),
                                           (*t_range(NT1 - 1)[:2], NT1 - 1, 1)):
                    sp.dma_start(e.att1[b][t0:t0 + m * tiles, :].rearrange("(n r) o -> r n o", n=tiles),
                                 att[0:m, slot, tile * P:(tile + tiles) * P]
                                 .rearrange("p (n o) -> p n o", n=tiles)).then_inc(out_sem[slot], 16)

            if layer == 0:
                staggered(sp, B * upb, un.per_loop, [(0, store), (upb + 1, load_half), (upb + 1, load_values)])
            else:
                staggered(sp, B * upb, un.per_loop, [(0, store), (upb + 5, load_batch), (upb + 5, load_values)])
            for k in range(2):
                sp.wait_ge(out_sem[k], 16 * (B // 2) * stores + START)

        @block.gpsimd
        def _(pool):
            pool.memset(mark[:], 0.0)
            pool.memset(vpad[:], 0.0).then_inc(v_zeroed, 1)
            pool.wait_ge(v_zeroed, 1)
            pool.memset(vpad[:, :, :, HD:HD + 1], 1.0).then_inc(v_zeroed, 1)
            pool.memset(ks[:, 1].bitcast(F32), 0.0).then_inc(zeroed[1], 1)
            pool.wait_ge(v_zeroed, 2)
            begin(pool, v_ready)
            if w:
                w.start(pool)
            with pool.Fori(0, B // 2) as i:
                if w:
                    w.load(pool, i)
                for s in range(2):
                    b = 2 * i + s
                    pool.wait_ge(v_in[s], 16 * (i + 1) * (1 if layer == 0 else NT1))
                    pool.wait_ge(valued, upb * (b - 1) + START)
                    pool.wait_ge(v_ready, free(b, 1))
                    pool.tensor_tensor(mark[:], mark[:], mark[:], ALU.mult)
                    pool.tensor_copy(vpad[:, s, :, 0:HD], vraw[:, s]).then_inc(v_ready, 1)
                    if w:
                        (w.split_lo if s else w.split_hi)(pool, i)

        @block.vector
        def _(dve):
            dve.memset(ks[:, 0, 0:pairs // 2].bitcast(F32), 0.0).then_inc(zeroed[0], 1)
            begin(dve, maxed, ev_dve, ev_o, normed)
            if layer == 1:
                dve.wait_ge(const, 32)
                dve.tensor_copy(band[:], bandf[:].unsqueeze(2).to_broadcast([P, 3, 2, P]))
                dve.tensor_copy(identb[:], e.ident[:]).then_inc(const, 1)

            def maximum(u, s, i):
                m, k = un.rows(s), s % 2
                dve.wait_ge(scored, done(u))
                dve.wait_ge(expd, free(u))
                if un.edge(s) is None:
                    dve.tensor_reduce(nmax[0:m, k, :], scores(s)[0:m], X, ALU.max, negate=True).then_inc(maxed, 1)
                    return
                nth = 4 * i + 2 * (s // NT1) + un.edge(s)
                dve.tensor_reduce(raw[0:m, :], scores(s)[0:m], X, ALU.max, negate=True).then_inc(padmax, 1)
                dve.wait_ge(padmax, nth + 1)
                dve.tensor_scalar(low[0:m, un.edge(s), :], raw[0:m, :], 0.0, None, ALU.min)
                dve.tensor_scalar(nmax[0:m, k, :], raw[0:m, :], edges[0:m, un.edge(s), 1:2], None,
                                  ALU.min).then_inc(maxed, 1)

            def turn_out(u, s, i):
                m, k = un.rows(s), s % 2
                dve.wait_ge(turned, done(u))
                dve.wait_ge(valued, free(u))
                dve.tensor_copy(pt[:, k, 0:512].rearrange("p (h t) -> p h t", h=4)[:, :, 0:m],
                                t_bank[:, 0, :].rearrange("p (h t) -> p h t", h=4)[:, :, 0:m]).then_inc(ev_dve, 1)

            def value_out(u, s, i):
                m, k = un.rows(s), s % 2
                dve.wait_ge(valued, done(u))
                dve.wait_ge(back, free(u))
                dve.tensor_copy(osb[:, k, :].rearrange("p (g t) -> p g t", g=2)[:, :, 0:m],
                                o_bank[:, 0, 0:2 * P].rearrange("p (g t) -> p g t", g=2)[:, :, 0:m]).then_inc(ev_o, 1)

            def divide(u, s, i):
                m, k = un.rows(s), s % 2
                dve.wait_ge(back, done(u))
                o = b_bank[0:m, 0, 0:2 * P].rearrange("p (h d) -> p h d", d=HP)
                if un.edge(s) is None:
                    steps = u + 1 if layer == 0 else u + 4 * i + 2 * (s // NT1) + 2
                    dve.reciprocal(rinv[0:m, k, :], o[:, :, HD]).then_inc(inv, 1)
                else:
                    ed = un.edge(s)
                    steps = u + 4 * i + 2 * (s // NT1) + 2 + ed
                    dve.scalar_tensor_tensor(den[0:m, :], epad[0:m, ed, :], edges[0:m, ed, 0:1], o[:, :, HD],
                                             ALU.mult, ALU.add).then_inc(inv, 1)
                    dve.wait_ge(inv, steps - 1)
                    dve.reciprocal(rinv[0:m, k, :], den[0:m, :]).then_inc(inv, 1)
                dve.wait_ge(inv, steps)
                slot, unit = s // upb, s % upb
                if unit == 0:
                    dve.wait_ge(out_sem[slot], 16 * stores * i + START)
                if layer == 0:
                    dst = att[:, slot, unit * P:(unit + 1) * P].rearrange("p (h d m) -> p h m d", h=2, m=M)
                    g = lambda a: a.rearrange("p (h m) d -> p h m d", h=2)
                    dve.tensor_tensor(dst, g(o[:, :, 0:HD]),
                                      g(rinv[:, k, :].unsqueeze(2).to_broadcast([P, UH, HD])),
                                      ALU.mult).then_inc(normed, 1)
                else:
                    dve.tensor_tensor(att[0:m, slot, unit * P:(unit + 1) * P].rearrange("p (h d) -> p h d", d=HD), o[:, :, 0:HD],
                                      rinv[0:m, k, :].unsqueeze(2).to_broadcast([m, UH, HD]),
                                      ALU.mult).then_inc(normed, 1)

            staggered(dve, B * upb, un.per_loop, [(4, maximum), (2, turn_out), (1, value_out), (0, divide)])

        @block.scalar
        def _(act):
            begin(act, expd, ev_act)
            rest = ks[:, 0, pairs // 2:].rearrange("p s a l -> p (s a l)")
            rest = rest.rearrange("p (r x) -> p r x", x=P)
            act.activation(rest, e.ident[:].unsqueeze(1).to_broadcast(list(rest.shape)), ACT.Copy,
                           scale=0.0).then_inc(zeroed[0], 1)

            def exponential(u, s, i):
                m, k = un.rows(s), s % 2
                act.wait_ge(maxed, done(u))
                act.wait_ge(turned, free(u))
                if un.edge(s) is not None:
                    act.activation(epad[0:m, un.edge(s), :], low[0:m, un.edge(s), :], ACT.Exp)
                for h in range(UH):
                    a = act.activation(probs[0:m, k, h, :], scores(s)[0:m, h, :], ACT.Exp,
                                       bias=nmax[0:m, k, h:h + 1])
                a.then_inc(expd, 1)

            def turn_out(u, s, i):
                m, k = un.rows(s), s % 2
                act.wait_ge(turned, done(u))
                act.wait_ge(valued, free(u))
                act.activation(pt[:, k, 512:1024].rearrange("p (h t) -> p h t", h=4)[:, :, 0:m],
                               t_bank[:, 1, :].rearrange("p (h t) -> p h t", h=4)[:, :, 0:m],
                               ACT.Copy).then_inc(ev_act, 1)

            staggered(act, B * upb, un.per_loop, [(3, exponential), (2, turn_out)])

        @block.tensor
        def _(pe):
            begin(pe, scored, turned, valued, back)
            if layer == 1:
                pe.wait_ge(const, 33)

            def score(u, s, i):
                m, k = un.rows(s), s % 2
                if layer == 0:
                    slot = s // 4 % 2
                    if s % 4 == 0:
                        pe.wait_ge(qk_in[slot], 192 * (2 * i + s // 8 + 1))
                else:
                    slot = s // NT1
                    if un.first(s):
                        pe.wait_ge(qk_in[slot], 192 * (i + 1))
                pe.wait_ge(expd, free(u))
                for j in range(4):
                    out = s_bank[0:m, 2 * k + j // 2, (j % 2) * 256:(j % 2) * 256 + 256]
                    out = out.rearrange("p (a x) -> p a x", a=2)
                    if layer == 0:
                        a = pe.matmul(out, qs[:, slot, 4 * (s % 4) + j, :], ks[:, slot, 4 * (s % 4) + j, :, :],
                                      start=True, stop=True, skip_group_check=True)
                    else:
                        t0, _, w0 = t_range(s % NT1)
                        kind = {None: 1, 0: 0, 1: 2}[un.edge(s)]
                        pe.matmul(out, qs[:, slot, j, t0:t0 + m], ks[:, slot, j, :, w0:w0 + P],
                                  start=True, stop=False, skip_group_check=True)
                        a = pe.matmul(out, identb[:, 0:m], band[:, kind, :, :],
                                      start=False, stop=True, skip_group_check=True)
                a.then_inc(scored, 1)

            def turn(u, s, i):
                m, k = un.rows(s), s % 2
                pe.wait_ge(expd, done(u))
                pe.wait_ge(ev_dve, free(u, 1))
                pe.wait_ge(ev_act, free(u, 1))
                for h in range(UH):
                    a = pe.transpose(t_bank[:, h // 4, h % 4 * P:h % 4 * P + m], probs[0:m, k, h, :],
                                     e.ident[0:m, 0:m])
                a.then_inc(turned, 1)

            def value(u, s, i):
                m, k = un.rows(s), s % 2
                slot = s // upb
                if un.first(s):
                    pe.wait_ge(v_ready, done(2 * i + slot))
                pe.wait_ge(ev_dve, done(u))
                pe.wait_ge(ev_act, done(u))
                pe.wait_ge(ev_o, free(u, 1))
                for g in range(2):
                    for j in range(4):
                        h = 4 * g + j
                        a = pe.matmul(o_bank[32 * j:32 * j + 32, 0, g * P:g * P + m],
                                      vpad[:, slot, UH * (s % upb) + h, :], pt[:, k, h * P:h * P + m],
                                      start=True, stop=True, skip_group_check=True)
                a.then_inc(valued, 1)

            def turn_back(u, s, i):
                m, k = un.rows(s), s % 2
                pe.wait_ge(ev_o, done(u))
                pe.wait_ge(normed, free(u, 1))
                for g in range(2):
                    a = pe.transpose(b_bank[0:m, 0, g * P:(g + 1) * P], osb[:, k, g * P:g * P + m], e.ident[:])
                a.then_inc(back, 1)

            staggered(pe, B * upb, un.per_loop, [(4, score), (2, turn), (1, value), (0, turn_back)])



def gemm(nc, e, name, w, src, resid, gate, bias, dst, mask=None):
    n = name + "_"
    ln_on = src is None
    with Stage(nc) as ctx:
        sb, ps, sem = scope(nc, ctx)
        if ln_on:
            ln = Norm(nc, ctx, n + "ln")
        xin = sb(n + "xin", [P, 4, D])
        rows = sb(n + "rows", [P, 4, D])
        xt = [sb(n + "xt_hi", [P, 2, NC, P], F32R), sb(n + "xt_lo", [P, 2, NC, P], F32R)]
        biasb = sb(n + "biasb", [P, D])
        out = sb(n + "out", [P, 2, D])
        tb = ps(n + "tb", [P, 4, 512]); gb = ps(n + "gb", [P, 4, 512])
        bias_in = sem(n + "bias_in"); masked = sem(n + "masked")
        x_in = [sem(n + f"x_in{k}") for k in range(4)]
        ready = sem(n + "ready") if ln_on else None
        turned = sem(n + "turned"); xhi = sem(n + "xhi"); xlo = sem(n + "xlo"); mm = sem(n + "mm")
        based = sem(n + "based"); gated = sem(n + "gated"); summed = sem(n + "res_added")
        out_sem = [sem(n + f"out{k}") for k in range(2)]
        block = ctx.enter_context(nc.Block())
        loads = 1 if ln_on else 2
        halves = lambda a: a.rearrange("p (a b) -> p a b", a=2)

        @block.sync
        def _(sp):
            begin(sp, *out_sem)
            def load(t, s, i):
                sp.wait_ge(summed, free(t, 4))
                sp.dma_start(xin[:, s, :], resid[t]).then_inc(x_in[s], 16)
                if not ln_on:
                    sp.wait_ge(turned, free(t, 4))
                    sp.dma_start(rows[:, s, :], src[t]).then_inc(x_in[s], 16)

            def store(t, s, i):
                sp.wait_ge(summed, done(t))
                sp.dma_start(dst[t], out[:, s % 2, :]).then_inc(out_sem[s % 2], 16)

            load(0, 0, 0)
            sp.dma_start(biasb[:], bias.partition_broadcast(P)).then_inc(bias_in, 16)
            load(1, 1, 0)
            load(2, 2, 0)
            staggered(sp, B, 4, [(3, load), (0, store)], started=(load,))
            for k in range(2):
                sp.wait_ge(out_sem[k], 16 * (B // 2) + START)

        if ln_on:
            @block.gpsimd
            def _(pool):
                ln.pool(pool, B // 2)

        @block.vector
        def _(dve):
            begin(dve, xlo, summed)
            if ln_on:
                begin(dve, ready)
            dve.wait_ge(bias_in, 16)
            if mask is not None:
                dve.tensor_tensor(biasb[:], biasb[:], mask, ALU.mult).then_inc(masked, 1)
            if mask is not None:
                dve.wait_ge(masked, 1)

            def normalise(t, s, i):
                k = s % 2
                dve.wait_ge(x_in[s], 16 * loads * (i + 1))
                if ln_on:
                    dve.wait_ge(turned, free(t))
                    ln.run(dve, t, k, xin[:, s, :], rows[:, k, :]).then_inc(ready, 1)
                    dve.wait_ge(ready, done(t))
                dve.scalar_tensor_tensor(xin[:, s, :], biasb[:], gate(t), xin[:, s, :],
                                         ALU.mult, ALU.add).then_inc(based, 1)

            def turned_lo(t, s, i):
                k = s % 2
                dve.wait_ge(xhi, done(t))
                dve.tensor_tensor(xt[1][:, k].rearrange("p (a c) t -> p a (c t)", a=2),
                                  tb[:, 2 * k:2 * k + 2, :],
                                  xt[0][:, k].rearrange("p (a c) t -> p a (c t)", a=2).bitcast(F32),
                                  ALU.subtract).then_inc(xlo, 1)

            def output(t, s, i):
                k = s % 2
                dve.wait_ge(mm, done(t))
                dve.wait_ge(based, t + 1)
                dve.wait_ge(out_sem[k], 16 * (2 * i + s // 2) + START)
                if mask is None:
                    dve.scalar_tensor_tensor(halves(out[:, k, :]), gb[:, 2 * k:2 * k + 2, :], gate(t),
                                             halves(xin[:, s, :]), ALU.mult, ALU.add).then_inc(summed, 1)
                    return
                dve.scalar_tensor_tensor(halves(out[:, k, :]), gb[:, 2 * k:2 * k + 2, :], gate(t),
                                         halves(mask), ALU.mult, ALU.mult).then_inc(gated, 1)
                dve.wait_ge(gated, t + 1)
                dve.tensor_tensor(out[:, k, :], out[:, k, :], xin[:, s, :], ALU.add).then_inc(summed, 1)

            staggered(dve, B, 4, [(2, normalise), (1, turned_lo), (0, output)])

        @block.scalar
        def _(act):
            begin(act, xhi)

            def turned_hi(t, s, i):
                k = s % 2
                act.wait_ge(turned, done(t))
                act.wait_ge(mm, free(t))
                act.activation(xt[0][:, k].rearrange("p (a c) t -> p a (c t)", a=2),
                               tb[:, 2 * k:2 * k + 2, :], ACT.Copy).then_inc(xhi, 1)

            staggered(act, B, 4, [(0, turned_hi)])

        @block.tensor
        def _(pe):
            begin(pe, turned, mm)

            def turn(t, s, i):
                if ln_on:
                    pe.wait_ge(ready, done(t))
                else:
                    pe.wait_ge(x_in[s], 16 * loads * (i + 1))
                pe.wait_ge(xlo, free(t))
                for c in range(NC):
                    m = pe.transpose(tb[:, 2 * (s % 2) + c // 4, c % 4 * P:(c % 4 + 1) * P],
                                     rows[:, s % 2 if ln_on else s, c * P:(c + 1) * P], e.ident[:])
                m.then_inc(turned, 1)

            def half(t, s, h):
                k = s % 2
                return three_passes(pe, gb[:, 2 * k + h, :], lambda x, c: xt[x][:, k, c, :],
                                    lambda y, c: (w.hi, w.lo)[y][:, c, h * 512:(h + 1) * 512], range(NC))

            def first_half(t, s, i):
                pe.wait_ge(xlo, done(t))
                pe.wait_ge(summed, free(t))
                half(t, s, 0)

            def second_half(t, s, i):
                half(t, s, 1).then_inc(mm, 1)

            w.ready(pe)
            staggered(pe, B, 4, [(0, first_half), (1, turn), (0, second_half)])



def ffn0_project1(nc, e):
    with Stage(nc) as ctx:
        sb, ps, sem = scope(nc, ctx)
        ln1 = Norm(nc, ctx, "fln"); ln2 = Norm(nc, ctx, "pln")
        shared = sb("f0_shared", [P, 8, D])
        w = LowRankWeight(nc, ctx, "f0", e.i["WfT0"], (e.i["A0"], e.i["BfT0"], e.i["coeffs"], e.i["scales"]),
                        raw=shared[:, 0:RAW, :], a=shared[:, RAW:RAW + 2, :], bt=shared[:, RAW + 2:RAW + 4, :])
        qk = [[shared[:, 4 * j + 2 * part:4 * j + 2 * part + 2, :] for part in range(2)] for j in range(2)]
        qk = [[hi.bitcast(F32R), lo.bitcast(F32R)] for hi, lo in qk]
        xin = sb("f0_xin", [P, 4, D]); rows = sb("f0_rows", [P, 2, D])
        xt = [sb("f0_xt_hi", [P, 2, NC, P], F32R), sb("f0_xt_lo", [P, 2, NC, P], F32R)]
        biasb = sb("f0_biasb", [P, D]); x2 = sb("f0_x2", [P, 2, D])
        wt = sb("p1_wt", [P, 4, P]); b = sb("p1_b", [P, 4]); bvb = sb("p1_bvb", [P, P])
        xn = sb("p1_xn", [P, 2, D]); cin = sb("p1_cin", [P, 2, D]); vout = sb("p1_v", [P, 2, NC, P])
        banks = ps("f0_banks", [P, 8, 512])
        tb, gb, pb, vb = banks[:, 0:2, :], banks[:, 2:4, :], banks[:, 4:6, :], banks[:, 6:8, :]
        w_in = sem("p1_w_in"); scaled = sem("p1_scaled"); bias_in = sem("f0_bias_in")
        x_in = [sem(f"f0_x_in{k}") for k in range(4)]; c_in = [sem(f"p1_c_in{k}") for k in range(2)]
        ready = sem("f0_ready"); turned = sem("f0_turned"); xhi = sem("f0_xhi"); xlo = sem("f0_xlo")
        mm = sem("f0_mm"); based = sem("f0_based"); summed = sem("f0_res_added")
        normed = sem("p1_normed"); pmm = [sem("p1_qmm"), sem("p1_kmm")]; hi = [sem("p1_qhi"), sem("p1_khi")]
        lo = [sem("p1_qlo"), sem("p1_klo")]; vmm = sem("p1_vmm"); vdone = sem("p1_vdone")
        x_out = [sem(f"f0_x_out{k}") for k in range(2)]; v_out = [sem(f"p1_v_out{k}") for k in range(2)]
        qk_out = [[sem(f"p1_{c}_out{k}") for k in range(2)] for c in "qk"]
        block = ctx.enter_context(nc.Block())
        halves = lambda a: a.rearrange("p (a b) -> p a b", a=2)
        gate = e.gate[:, 2:3]

        @block.sync
        def _(sp):
            begin(sp, *x_out, *v_out, *qk_out[0], *qk_out[1])
            w.load_lowrank(sp)

            def load_x(t, s, i):
                sp.wait_ge(summed, free(2 * t + 1, 8))
                sp.dma_start(xin[:, s, :], e.x1[t]).then_inc(x_in[s], 16)

            def load_ctx(t, s, i):
                sp.wait_ge(vmm, free(t))
                sp.dma_start(cin[:, s % 2, :], e.i["ctx"][t]).then_inc(c_in[s % 2], 16)

            def store_x2(t, s, i):
                sp.wait_ge(summed, done(2 * t + 1))
                sp.dma_start(e.x2[t], x2[:, s % 2, :]).then_inc(x_out[s % 2], 16)

            def store_qk(j, dram):
                def store(t, s, i):
                    sp.wait_ge(lo[j], done(t))
                    for part in range(2):
                        sp.dma_start(dram[part][t],
                                     qk[j][part][:, s % 2, :].bitcast(F32)).then_inc(qk_out[j][s % 2], 16)
                return store

            def store_v(t, s, i):
                sp.wait_ge(vdone, done(t))
                sp.dma_start(e.v1[t].rearrange("(c p) o -> p c o", p=P), vout[:, s % 2]).then_inc(v_out[s % 2], 16)

            def weights():
                w.load(sp)
                for dst, src in ((wt[:], e.i["WT1"]), (b[:], e.i["b1"]), (bvb[:], e.i["bv1"].partition_broadcast(P))):
                    sp.dma_start(dst, src).then_inc(w_in, 16)

            sp.dma_start(biasb[:], e.i["bf0"].partition_broadcast(P)).then_inc(bias_in, 16)
            load_x(0, 0, 0)
            load_x(1, 1, 0)
            weights()
            load_x(2, 2, 0)
            load_x(3, 3, 0)
            load_ctx(0, 0, 0)
            steps = [(4, load_x), (1, load_ctx), (0, store_qk(1, e.k1)), (1, store_x2),
                     (0, store_qk(0, e.q1)), (0, store_v)]
            staggered(sp, B, 4, steps, started=(load_x, load_ctx))
            for k in range(2):
                sp.wait_ge(x_out[k], 16 * (B // 2) + START)
                sp.wait_ge(v_out[k], 16 * (B // 2) + START)
                sp.wait_ge(qk_out[0][k], 32 * (B // 2) + START)
                sp.wait_ge(qk_out[1][k], 32 * (B // 2) + START)

        @block.gpsimd
        def _(pool):
            ln1.start(pool)
            ln2.start(pool)
            staggered(pool, B, 4, [(3, lambda t, s, i: ln1.pool_tile(pool, t, s % 2)),
                                   (1, lambda t, s, i: ln2.pool_tile(pool, t, s % 2))])

        @block.vector
        def _(dve):
            begin(dve, ready, xlo, summed, normed, lo[0], lo[1], vdone)
            w.scale_lowrank(dve)
            dve.wait_ge(bias_in, 16)

            def normalise(t, s, i):
                k = s % 2
                dve.wait_ge(x_in[s], 16 * (i + 1))
                dve.wait_ge(turned, free(t))
                ln1.run(dve, t, k, xin[:, s, :], rows[:, k, :]).then_inc(ready, 1)
                dve.wait_ge(ready, done(t))
                dve.scalar_tensor_tensor(xin[:, s, :], biasb[:], gate, xin[:, s, :],
                                         ALU.mult, ALU.add).then_inc(based, 1)

            def turned_lo(t, s, i):
                dve.wait_ge(xhi, done(t))
                dve.tensor_tensor(xt[1][:, s % 2].rearrange("p (a c) t -> p a (c t)", a=2), tb,
                                  xt[0][:, s % 2].rearrange("p (a c) t -> p a (c t)", a=2).bitcast(F32),
                                  ALU.subtract).then_inc(xlo, 1)

            def output(h):
                def run(t, s, i):
                    k, part = s % 2, slice(h * 512, h * 512 + 512)
                    dve.wait_ge(mm, done(2 * t + h))
                    dve.wait_ge(based, t + 1)
                    dve.wait_ge(x_out[k], 16 * (2 * i + s // 2) + START)
                    dve.scalar_tensor_tensor(x2[:, k, part], gb[:, h, :], gate, xin[:, s, part],
                                             ALU.mult, ALU.add).then_inc(summed, 1)
                return run

            def normalise_x2(t, s, i):
                dve.wait_ge(summed, done(2 * t + 1))
                dve.wait_ge(pmm[0], free(t))
                ln2.run(dve, t, s % 2, x2[:, s % 2, :], xn[:, s % 2, :]).then_inc(normed, 1)

            def qk_lo(j):
                def run(t, s, i):
                    dve.wait_ge(hi[j], done(t))
                    dve.scalar_tensor_tensor(halves(qk[j][1][:, s % 2, :]), pb, b[:, j:j + 1],
                                             halves(qk[j][0][:, s % 2, :]).bitcast(F32),
                                             ALU.add, ALU.subtract).then_inc(lo[j], 1)
                return run

            def values(t, s, i):
                dve.wait_ge(vmm, done(t))
                dve.wait_ge(v_out[s % 2], 16 * (2 * i + s // 2) + START)
                dve.tensor_tensor(vout[:, s % 2], vb.rearrange("p a (c o) -> p (a c) o", o=P),
                                  bvb[:].unsqueeze(1).to_broadcast([P, NC, P]), ALU.add).then_inc(vdone, 1)

            def weights():
                w.split_lo(dve, banks[:, 4:8, :])
                dve.wait_ge(w_in, 48)
                dve.tensor_scalar(wt[:, 0, :], wt[:, 0, :], QS, None, ALU.mult)
                dve.tensor_scalar(b[:, 0:1], b[:, 0:1], QS, None, ALU.mult).then_inc(scaled, 1)
                dve.wait_ge(scaled, 1)

            normalise(0, 0, 0)
            normalise(1, 1, 0)
            weights()
            staggered(dve, B, 4, [(3, normalise), (0, qk_lo(1)), (2, turned_lo), (1, output(0)), (1, output(1)),
                                  (1, normalise_x2), (0, qk_lo(0)), (0, values)],
                      between=lambda: normalise(2, 2, 0), at=-1, started=(normalise,))

        @block.scalar
        def _(act):
            begin(act, xhi, hi[0], hi[1])

            def qk_hi(j):
                def run(t, s, i):
                    act.wait_ge(pmm[j], done(t))
                    act.wait_ge(qk_out[j][s % 2], 32 * (2 * i + s // 2) + START)
                    act.activation(halves(qk[j][0][:, s % 2, :]), pb, ACT.Identity,
                                   bias=b[:, j:j + 1]).then_inc(hi[j], 1)
                return run

            def turned_hi(t, s, i):
                act.wait_ge(turned, done(t))
                act.wait_ge(mm, done(2 * t - 3))
                act.activation(xt[0][:, s % 2].rearrange("p (a c) t -> p a (c t)", a=2), tb,
                               ACT.Copy).then_inc(xhi, 1)

            def weights():
                w.split_hi(act)
                act.wait_ge(scaled, 1)

            staggered(act, B, 4, [(0, qk_hi(1)), (2, turned_hi), (0, qk_hi(0))], between=weights, at=-2)

        @block.tensor
        def _(pe):
            begin(pe, turned, mm, pmm[0], pmm[1], vmm)
            w.lowrank_product(pe, banks[:, 4:8, :])

            def turn(t, s, i):
                pe.wait_ge(ready, done(t))
                pe.wait_ge(xlo, free(t, 1))
                for c in range(NC):
                    m = pe.transpose(tb[:, c // 4, c % 4 * P:(c % 4 + 1) * P],
                                     rows[:, s % 2, c * P:(c + 1) * P], e.ident[:])
                m.then_inc(turned, 1)

            def product(h):
                def run(t, s, i):
                    if h == 0:
                        pe.wait_ge(xlo, done(t))
                    pe.wait_ge(summed, free(2 * t + h))
                    three_passes(pe, gb[:, h, :], lambda x, c: xt[x][:, s % 2, c, :],
                                 lambda y, c: (w.hi, w.lo)[y][:, c, h * 512:(h + 1) * 512],
                                 range(NC)).then_inc(mm, 1)
                return run

            def project(j, other, late):
                def run(t, s, i):
                    if j:
                        pe.wait_ge(c_in[s % 2], 16 * (2 * i + s // 2 + 1))
                    else:
                        pe.wait_ge(normed, done(t))
                    pe.wait_ge(lo[other], done(t - late))
                    src = (cin if j else xn)[:, s % 2, :]
                    for h in range(2):
                        m = pe.matmul(pb[:, h, :], wt[:, j, :], src[:, h * 512:(h + 1) * 512], start=True, stop=True)
                    m.then_inc(pmm[j], 1)
                return run

            def values(t, s, i):
                pe.wait_ge(vdone, free(t, 1))
                for c in range(NC):
                    m = pe.matmul(vb[:, c // 4, c % 4 * P:(c % 4 + 1) * P], cin[:, s % 2, c * P:(c + 1) * P],
                                  wt[:, 2, :], start=True, stop=True, skip_group_check=True)
                m.then_inc(vmm, 1)

            def weights():
                w.ready(pe)
                pe.wait_ge(scaled, 1)

            staggered(pe, B, 4, [(1, product(0)), (0, project(1, 0, 1)), (2, turn), (1, product(1)),
                                 (0, project(0, 1, 0)), (0, values)], between=weights, at=-1)


def attend1(nc, e):
    attend(nc, e, 1)



def select(nc, e, w):
    with Stage(nc) as ctx:
        sb, ps, sem = scope(nc, ctx)
        ln = Norm(nc, ctx, "seln")
        wt = sb("se_wt", [P, P]); b = sb("se_b", [P, 4]); gbo = sb("se_gbo", [P, 1])
        cent = sb("se_cent", [P, NC, NCL]); iota = sb("se_iota", [NCL, 1])
        assign = sb("se_assign", [NCL, D], I32); onehot = sb("se_onehot", [NCL, D])
        a_in = sb("se_a", [P, 4, NC, P]); x2 = sb("se_x2", [P, 4, D])
        att_t = sb("se_att_t", [P, 2, D]); delta = sb("se_delta", [P, 2, D])
        x3 = sb("se_x3", [P, 2, D]); xn = sb("se_xn", [P, 2, D]); xt = sb("se_xt", [P, 2, NC, P])
        low = sb("se_low", [P, 2, 2]); ex = sb("se_ex", [P, 2, NCL]); total = sb("se_total", [P, 1]); share = sb("se_share", [P, 1])
        hits = sb("se_hits", [P, NCL]); seen = sb("se_seen", [P, NCL]); any_ = sb("se_any", [P, 1])
        ones = sb("se_ones", [P, 1]); sel = sb("se_sel", [NCL, P])
        ab = ps("se_ab", [P, 2, 512]); ob = ps("se_ob", [P, 2, 512]); xb = ps("se_xb", [P, 2, 512])
        lb = ps("se_lb", [P, 1, 512]); cb = ps("se_cb", [P, 1, 512])
        w_in = sem("se_w_in"); prep = sem("se_prep")
        a_in_sem = [sem(f"se_a_in{k}") for k in range(4)]; x2_in = [sem(f"se_x2_in{k}") for k in range(4)]
        a_turned = sem("se_a_turned"); a_out = sem("se_a_out"); o_mm = sem("se_o_mm"); o_out = sem("se_o_out")
        summed = sem("se_summed"); normed = sem("se_normed"); x_turned = sem("se_x_turned")
        x_out = sem("se_x_out"); logit = sem("se_logit"); lowed = sem("se_lowed"); expd = sem("se_expd")
        small = sem("se_small"); lows = sem("se_lows"); chosen = sem("se_chosen"); fin = sem("se_fin"); fin_pe = sem("se_fin_pe")
        out_sem = [sem(f"se_out{k}") for k in range(2)]
        block = ctx.enter_context(nc.Block())
        halves = lambda a: a.rearrange("p (a b) -> p a b", a=2)

        def batches(eng, stages):
            pairs = [(lead, lambda t, place, i, f=f: f(t, place % 2, place, i)) for lead, f in stages]
            staggered(eng, B, 4, pairs)

        @block.sync
        def _(sp):
            begin(sp, *out_sem)
            for dst, src in ((wt[:], e.i["WT1"][:, 3, :]), (b[:], e.i["b1"]),
                             (cent[:], e.i["centT"].rearrange("(c p) n -> p c n", p=P)),
                             (iota[:], e.i["iota"]), (assign[:], e.i["assign"].partition_broadcast(NCL))):
                sp.dma_start(dst, src).then_inc(w_in, 16)

            def load(t, s, place, i):
                sp.wait_ge(a_turned, free(t, 4))
                sp.dma_start(a_in[:, place], e.att1[t].rearrange("(c p) o -> p c o", p=P)).then_inc(a_in_sem[place], 16)
                sp.wait_ge(summed, free(t, 4))
                sp.dma_start(x2[:, place, :], e.x2[t]).then_inc(x2_in[place], 16)

            def store(t, s, place, i):
                sp.wait_ge(summed, done(t))
                sp.dma_start(e.x3[t], x3[:, s, :]).then_inc(out_sem[s], 16)

            batches(sp, [(3, load), (0, store)])
            for k in range(2):
                sp.wait_ge(out_sem[k], 16 * (B // 2) + START)

        @block.gpsimd
        def _(pool):
            ln.start(pool)
            w.start(pool)
            with pool.Fori(0, B // 2) as i:
                w.load(pool, i)
                for k in range(2):
                    ln.pool_tile(pool, 2 * i + k, k)
                    (w.split_lo if k else w.split_hi)(pool, i)

        @block.vector
        def _(dve):
            begin(dve, summed, normed, lowed, chosen)
            dve.memset(seen[:], 0.0)
            dve.memset(ones[:], 1.0)
            dve.wait_ge(w_in, 80)
            dve.tensor_copy(onehot[:], assign[:]).then_inc(prep, 1)
            dve.wait_ge(prep, 1)
            dve.tensor_scalar(onehot[:], onehot[:], iota[:, 0:1], None, ALU.is_equal)
            dve.tensor_tensor(gbo[:], b[:, 3:4], e.gate[:, 1:2], ALU.mult).then_inc(prep, 1)
            dve.wait_ge(prep, 2)

            def residual(t, s, place, i):
                dve.wait_ge(x2_in[place], 16 * i + 16)
                dve.wait_ge(o_out, done(t))
                dve.wait_ge(out_sem[s], 16 * (2 * i + place // 2) + START)
                dve.tensor_tensor(x3[:, s, :], delta[:, s, :], x2[:, place, :], ALU.add).then_inc(summed, 1)
                dve.wait_ge(summed, done(t))
                dve.wait_ge(x_turned, free(t))
                ln.run(dve, t, s, x3[:, s, :], xn[:, s, :]).then_inc(normed, 1)

            def lowest(t, s, place, i):
                dve.wait_ge(logit, done(t))
                dve.tensor_reduce(low[:, s, 0:1], lb[:, 0, 0:NCL], X, ALU.max, negate=True).then_inc(lows, 1)
                dve.wait_ge(lows, t + 1)
                dve.tensor_scalar(low[:, s, 1:2], low[:, s, 0:1], 10.0, None, ALU.mult).then_inc(lowed, 1)

            def choose(t, s, place, i):
                dve.wait_ge(expd, done(t))
                dve.tensor_reduce(total[:], ex[:, s, :], X, ALU.add).then_inc(small, 1)
                dve.wait_ge(small, 4 * t + 1)
                dve.reciprocal(share[:], total[:]).then_inc(small, 1)
                dve.wait_ge(small, 4 * t + 2)
                dve.tensor_scalar(hits[:], ex[:, s, :], share[:, 0:1], 0.01, ALU.mult, ALU.is_gt).then_inc(small, 1)
                dve.wait_ge(small, 4 * t + 3)
                dve.tensor_tensor(seen[:], seen[:], hits[:], ALU.max)
                dve.tensor_reduce(any_[:], hits[:], X, ALU.max).then_inc(small, 1)
                dve.wait_ge(small, 4 * t + 4)
                dve.tensor_scalar(e.token_gate[:, bass.ds(t, 1)], any_[:], e.gate[:, 3:4], None,
                                  ALU.mult).then_inc(chosen, 1)

            batches(dve, [(3, residual), (1, lowest), (0, choose)])
            dve.wait_ge(fin_pe, 1)
            dve.tensor_scalar(sel[:], cb[0:NCL, 0, 0:1].to_broadcast([NCL, P]), 1.0, None, ALU.min).then_inc(fin, 1)
            dve.wait_ge(fin_pe, 2)
            dve.tensor_copy(halves(e.row_mask[:]), ob[:]).then_inc(fin, 1)
            dve.wait_ge(fin, 2)

        @block.scalar
        def _(act):
            begin(act, a_out, o_out, x_out, expd)
            act.wait_ge(prep, 2)

            def attention_out(t, s, place, i):
                act.wait_ge(a_turned, done(t))
                act.wait_ge(o_mm, free(t))
                act.activation(halves(att_t[:, s, :]), ab[:], ACT.Copy).then_inc(a_out, 1)

            def projected(t, s, place, i):
                act.wait_ge(o_mm, done(t))
                act.wait_ge(summed, free(t))
                act.activation(halves(delta[:, s, :]), ob[:], ACT.Identity, bias=gbo[:],
                               scale=e.gate[:, 1:2]).then_inc(o_out, 1)

            def rows_out(t, s, place, i):
                act.wait_ge(x_turned, done(t))
                act.wait_ge(logit, free(t))
                act.activation(xt[:, s].rearrange("p (a c) t -> p a (c t)", a=2), xb[:], ACT.Copy).then_inc(x_out, 1)

            def exponential(t, s, place, i):
                act.wait_ge(lowed, done(t))
                act.activation(ex[:, s, :], lb[:, 0, 0:NCL], ACT.Exp, bias=low[:, s, 1:2],
                               scale=10.0).then_inc(expd, 1)

            batches(act, [(3, projected), (4, attention_out), (2, rows_out), (1, exponential)])

        @block.tensor
        def _(pe):
            begin(pe, a_turned, o_mm, x_turned, logit)
            pe.wait_ge(prep, 2)

            def turn_attention(t, s, place, i):
                pe.wait_ge(a_in_sem[place], 16 * i + 16)
                pe.wait_ge(a_out, free(t, 1))
                for c in range(NC):
                    m = pe.transpose(ab[:, c // 4, c % 4 * P:(c % 4 + 1) * P], a_in[:, place, c, :], e.ident[:])
                m.then_inc(a_turned, 1)

            def project(t, s, place, i):
                pe.wait_ge(a_out, done(t))
                pe.wait_ge(o_out, free(t, 1))
                for h in range(2):
                    m = pe.matmul(ob[:, h, :], wt[:], att_t[:, s, h * 512:(h + 1) * 512], start=True, stop=True)
                m.then_inc(o_mm, 1)

            def turn_rows(t, s, place, i):
                pe.wait_ge(normed, done(t))
                pe.wait_ge(x_out, free(t, 1))
                for c in range(NC):
                    m = pe.transpose(xb[:, c // 4, c % 4 * P:(c % 4 + 1) * P], xn[:, s, c * P:(c + 1) * P],
                                     e.ident[:])
                m.then_inc(x_turned, 1)

            def logits(t, s, place, i):
                pe.wait_ge(x_out, done(t))
                pe.wait_ge(expd, free(t, 1))
                for c in range(NC):
                    m = pe.matmul(lb[:, 0, 0:NCL], xt[:, s, c, :], cent[:, c, :], start=(c == 0), stop=(c == NC - 1))
                m.then_inc(logit, 1)

            batches(pe, [(3, project), (4, turn_attention), (2, turn_rows), (1, logits)])
            pe.wait_ge(chosen, done(B - 1))
            pe.matmul(cb[0:NCL, 0, 0:1], seen[:], ones[:], start=True, stop=True).then_inc(fin_pe, 1)
            pe.wait_ge(fin, 1)
            for h in range(2):
                m = pe.matmul(ob[:, h, :], sel[:], onehot[:, h * 512:(h + 1) * 512], start=True, stop=True)
            m.then_inc(fin_pe, 1)



def attention0(nc, e):
    with Stage(nc) as ctx:
        w = EarlyWeight(nc, ctx, "wo", e.i["WoT0"])
        attend(nc, e, 0, w)
        gemm(nc, e, "wo", w, e.att0, e.i["x"], lambda t: e.gate[:, 0:1], e.i["bo0"], e.x1)


def select_ffn1(nc, e):
    with Stage(nc) as ctx:
        w = EarlyWeight(nc, ctx, "f1", e.i["WfT1"])
        e.row_mask = scope(nc, ctx)[0]("row_mask", [P, D])
        select(nc, e, w)
        gemm(nc, e, "f1", w, None, e.x3, lambda t: e.token_gate[:, bass.ds(t, 1)], e.i["bf1"], e.out,
             mask=e.row_mask[:])



def program(nc, ins, out, stages=99):
    e = Env()
    e.i = ins
    dram = lambda name, shape, dt=F32: nc.dram_tensor(name, shape, dt).ap()
    e.q0 = [dram(f"q0_{n}", [D, TOK]) for n in ("hi", "lo")]
    e.k0 = [dram(f"k0_{n}", [D, TOK]) for n in ("hi", "lo")]
    e.v0 = dram("v0", [B, P, D])
    e.att0 = dram("att0", [B, P, D])
    e.x1 = dram("x1", [B, P, D]); e.x2 = dram("x2", [B, P, D]); e.x3 = dram("x3", [B, P, D])
    e.q1 = [dram(f"q1_{n}", [B, P, D]) for n in ("hi", "lo")]
    e.k1 = [dram(f"k1_{n}", [B, P, D]) for n in ("hi", "lo")]
    e.v1 = dram("v1", [B, D, P]); e.att1 = dram("att1", [B, D, P])
    with ExitStack() as ctx:
        sb, ps, sem = scope(nc, ctx)
        e.ident = sb("ident_sb", [P, P]); e.fold = sb("fold", [P, NC, P])
        e.gate = sb("gate", [P, 4])
        e.token_gate = sb("token_gate", [P, B])
        e.out = out
        e.bqf = sb("bqf", [P, NC]); e.bkf = sb("bkf", [P, NC]); e.bvf = sb("bvf", [P, D])
        for stage in STAGES[:stages]:
            stage(nc, e)


STAGES = [setup, project_q, project_kv, attention0, ffn0_project1, attend1, select_ffn1]


def layout(x, ctx_4096, g_xattn, g_ffn, L0_xattn_Wq, L0_xattn_bq, L0_xattn_Wk, L0_xattn_bk, L0_xattn_Wv, L0_xattn_bv,
           L0_xattn_interference, L0_xattn_amp, L0_xattn_Wo, L0_xattn_bo, L0_ffn_W, L0_ffn_bias, L0_ffn_A, L0_ffn_Bf,
           L0_ffn_coeffs, L0_ffn_scales, L1_xattn_Wq, L1_xattn_bq, L1_xattn_Wk, L1_xattn_bk, L1_xattn_Wv,
           L1_xattn_bv, L1_xattn_Wo, L1_xattn_bo, L1_ffn_weight, L1_ffn_bias, L1_ffn_centroids,
           L1_ffn_assignments):
    part, free_ = np.arange(P)[:, None], np.arange(P)[None, :]
    h, d, i = part // 64, part // 4 % 16, part % 4
    h2, j, d2 = free_ // 64, free_ // 16 % 4, free_ % 16
    same = (h == h2) & (d == d2)
    band, edges = np.full((P, 3, P), 0.0, np.float32), np.zeros((P, 2, 2), np.float32)
    for n, tile in enumerate((0, 1, NT1 - 1)):
        t0, m, w0 = t_range(tile)
        off = w0 + free_ - (t0 + part)
        band[:, n, :] = np.where((off >= -PADL) & (off < WIN - PADL), 0.0, -1e30)
    for n, tile in enumerate((0, NT1 - 1)):
        t = t_range(tile)[0] + np.arange(P)
        edges[:, n, 0] = np.maximum(0, PADL - t) + np.maximum(0, t + WIN - PADL - D)
        edges[:, n, 1] = np.where(edges[:, n, 0] > 0, 0.0, 3e38)
    col = lambda b: np.ascontiguousarray(b.reshape(-1, P).T)
    coef = np.broadcast_to(L0_xattn_interference.reshape(NC, 2, 1, M, M), (NC, 2, HD, M, M))
    er = lambda w: np.ascontiguousarray(np.broadcast_to(w[:, None], (16, 16)).reshape(2, P).T)
    c = np.ascontiguousarray
    f = np.float32
    return {
        "ident": np.eye(P, dtype=f),
        "rep_mask": same.astype(f),
        "perm": (same & (i == j)).astype(f),
        "band": band, "edges": edges,
        "iota": np.arange(NCL, dtype=f)[:, None],
        "coef": c(coef.reshape(NC, P, M).transpose(1, 0, 2)),
        "amp": L0_xattn_amp, "g_xattn": g_xattn, "g_ffn": g_ffn,
        "x": x, "ctx": ctx_4096, "ctxT": c(ctx_4096.reshape(TOK, D).T),
        "Wq0": L0_xattn_Wq, "Wk0": L0_xattn_Wk, "Wv0": L0_xattn_Wv,
        "bq0": col(L0_xattn_bq), "bk0": col(L0_xattn_bk), "bv0": col(L0_xattn_bv),
        "WoT0": c(L0_xattn_Wo.T), "bo0": L0_xattn_bo,
        "WfT0": c(L0_ffn_W.T), "bf0": L0_ffn_bias,
        "A0": c(L0_ffn_A.reshape(256, D)), "BfT0": c(L0_ffn_Bf.transpose(0, 2, 1).reshape(256, D)),
        "coeffs": er(L0_ffn_coeffs), "scales": er(L0_ffn_scales),
        "WT1": c(np.stack([w.T for w in (L1_xattn_Wq, L1_xattn_Wk, L1_xattn_Wv, L1_xattn_Wo)], 1)),
        "b1": c(np.stack([L1_xattn_bq, L1_xattn_bk, L1_xattn_bv, L1_xattn_bo], 1)), "bv1": L1_xattn_bv,
        "WfT1": c(L1_ffn_weight.T), "bf1": L1_ffn_bias,
        "centT": c(L1_ffn_centroids.T), "assign": L1_ffn_assignments,
    }


def kernel(**inputs):
    import concourse.bacc as bacc
    from concourse.bass_utils import run_bass_kernel_spmd

    nc = bacc.Bacc("TRN2", target_bir_lowering=False, num_devices=1)
    arrays = {f"in_{name}": np.ascontiguousarray(a) for name, a in layout(**inputs).items()}
    ins = {name[3:]: nc.dram_tensor(name, a.shape, mybir.dt.from_np(a.dtype), kind="ExternalInput").ap()
           for name, a in arrays.items()}
    out = nc.dram_tensor("out", (B, P, D), F32, kind="ExternalOutput").ap()
    program(nc, ins, out)
    r = run_bass_kernel_spmd(nc, [arrays], core_ids=[0])
    return r.results[0]["out"]
```
